# Optimizing a Trainium2 kernel written in Bass

```python
import numpy as np
import jax
import jax.numpy as jnp

def _softmax(x, axis=-1):
    return jax.nn.softmax(x, axis=axis)

def _gelu(x):
    return jax.nn.gelu(x, approximate=True)

def _silu(x):
    return jax.nn.silu(x)

def _sigmoid(x):
    return jax.nn.sigmoid(x)

def _layernorm(x, axis=-1, eps=1e-05):
    m = jnp.mean(x, axis=axis, keepdims=True)
    v = jnp.var(x, axis=axis, keepdims=True)
    return (x - m) / jnp.sqrt(v + eps)

def _scatter_add(tgt, idx, src, axis=0):
    return tgt.at[idx].add(src)

def _segment_sum(src, seg, n):
    return jax.ops.segment_sum(src, seg, n)
kernel_name = 'mk_audio_tower_d1_tok_audfeat1024_r4_fa134e'

def setup_inputs(seed: int=0):
    np.random.seed(seed)
    _w = jnp.asarray

    def _rec_inputs():
        import jax
        import jax.numpy as jnp
        _rk = jax.random.key(seed)
        x = 7.22013e-05 + 1.00017 * jax.random.normal(jax.random.fold_in(_rk, 1), (4, 512, 256), jnp.float32)
        return x
    x = _rec_inputs()

    def _L0_tok_setup():
        import jax, jax.numpy as jnp
        import numpy as np
        HEADS = 16
        LN_EPS = 1e-05

        def _layernorm(x, g, b):
            mu = jnp.mean(x, axis=-1, keepdims=True)
            var = jnp.var(x, axis=-1, keepdims=True)
            return (x - mu) * jax.lax.rsqrt(var + LN_EPS) * g + b
        key = jax.random.key(seed)
        ks = jax.random.split(key, 4)
        B, N, C = (4, 512, 256)
        x = jax.random.normal(ks[0], (B, N, C), dtype=jnp.float32)
        general_token = jax.random.normal(ks[1], (1, 1, C), dtype=jnp.float32)
        W_qkv = jax.random.normal(ks[2], (C, 3 * C), dtype=jnp.float32) * C ** (-0.5)
        b_qkv = jnp.zeros((3 * C,), dtype=jnp.float32)
        W_proj = jax.random.normal(ks[3], (C, C), dtype=jnp.float32) * C ** (-0.5)
        b_proj = jnp.zeros((C,), dtype=jnp.float32)
        ln_g = jnp.ones((C,), dtype=jnp.float32)
        ln_b = jnp.zeros((C,), dtype=jnp.float32)
        return {'x': x, 'general_token': general_token, 'W_qkv': W_qkv, 'b_qkv': b_qkv, 'W_proj': W_proj, 'b_proj': b_proj, 'ln_g': ln_g, 'ln_b': ln_b}
    _L0_tok_all = _L0_tok_setup()
    _L0_tok_in = {k: v for k, v in _L0_tok_all.items() if k in ('general_token', 'W_qkv', 'b_qkv', 'W_proj', 'b_proj', 'ln_g', 'ln_b')}
    del _L0_tok_all

    def _L0_attn_setup():
        import jax, jax.numpy as jnp
        import numpy as np
        T, B, E, H = (256, 2, 256, 16)
        D = E // H
        R = 2 * T - 1

        def _rel_shift(x):
            b, h, q, r = x.shape
            zp = jnp.zeros((b, h, q, 1), x.dtype)
            xp = jnp.concatenate([zp, x], axis=3)
            xp = xp.reshape(b, h, r + 1, q)[:, :, 1:, :]
            return xp.reshape(b, h, q, r)
        key = jax.random.key(seed)
        ks = jax.random.split(key, 8)
        std = (2.0 / (E + E)) ** 0.5
        return {'x': jax.random.normal(ks[0], (T, B, E), jnp.float32), 'pos': jax.random.normal(ks[1], (R, 1, E), jnp.float32), 'in_proj_weight': jax.random.normal(ks[2], (3 * E, E), jnp.float32) * std, 'in_proj_bias': jnp.zeros((3 * E,), jnp.float32), 'pos_proj_weight': jax.random.normal(ks[3], (E, E), jnp.float32) * std, 'pos_proj_bias': jnp.zeros((E,), jnp.float32), 'out_proj_weight': jax.random.normal(ks[4], (E, E), jnp.float32) * std, 'out_proj_bias': jnp.zeros((E,), jnp.float32), 'r_w_bias': jax.random.normal(ks[5], (H, D), jnp.float32) * 0.02, 'r_r_bias': jax.random.normal(ks[6], (H, D), jnp.float32) * 0.02}
    _L0_attn_all = _L0_attn_setup()
    _L0_attn_in = {k: v for k, v in _L0_attn_all.items() if k in ('pos', 'in_proj_weight', 'in_proj_bias', 'pos_proj_weight', 'pos_proj_bias', 'out_proj_weight', 'out_proj_bias', 'r_w_bias', 'r_r_bias')}
    del _L0_attn_all

    def _L0_ffn_setup():
        import jax, jax.numpy as jnp
        import numpy as np
        N_EXPERTS = 32
        TOP_K = 8
        N_GROUP = 4
        TOPK_GROUP = 2
        ROUTED_SCALING = 2.5

        def _gate(x, gate_w, gate_bias):
            T, E = (x.shape[0], gate_w.shape[0])
            logits = jnp.einsum('th,eh->te', x, gate_w)
            scores = jax.nn.sigmoid(logits)
            scores_choice = scores + gate_bias[None, :]
            grp = scores_choice.reshape(T, N_GROUP, E // N_GROUP)
            top2, _ = jax.lax.top_k(grp, 2)
            group_scores = top2.sum(-1)
            _, grp_idx = jax.lax.top_k(group_scores, TOPK_GROUP)
            group_mask = jax.nn.one_hot(grp_idx, N_GROUP, dtype=scores.dtype).sum(1)
            expert_mask = jnp.repeat(group_mask, E // N_GROUP, axis=1)
            masked = jnp.where(expert_mask > 0, scores_choice, 0.0)
            _, topk_idx = jax.lax.top_k(masked, TOP_K)
            topk_w = jnp.take_along_axis(scores, topk_idx, axis=1)
            topk_w = topk_w / (topk_w.sum(-1, keepdims=True) + 1e-20)
            topk_w = topk_w * ROUTED_SCALING
            return (topk_idx, topk_w)

        def _mlp(x, wg, wu, wd):
            return jnp.einsum('...i,hi->...h', jax.nn.silu(jnp.einsum('...h,ih->...i', x, wg)) * jnp.einsum('...h,ih->...i', x, wu), wd)
        key = jax.random.key(seed)
        ks = jax.random.split(key, 9)
        B, S, H, I = (2, 128, 256, 128)
        w = 0.02
        return {'hidden_states': jax.random.normal(ks[0], (B, S, H), jnp.float32), 'gate_w': jax.random.normal(ks[1], (N_EXPERTS, H), jnp.float32) * w, 'gate_bias': jax.random.normal(ks[2], (N_EXPERTS,), jnp.float32) * w, 'expert_gate': jax.random.normal(ks[3], (N_EXPERTS, I, H), jnp.float32) * w, 'expert_up': jax.random.normal(ks[4], (N_EXPERTS, I, H), jnp.float32) * w, 'expert_down': jax.random.normal(ks[5], (N_EXPERTS, H, I), jnp.float32) * w, 'shared_gate': jax.random.normal(ks[6], (2 * I, H), jnp.float32) * w, 'shared_up': jax.random.normal(ks[7], (2 * I, H), jnp.float32) * w, 'shared_down': jax.random.normal(ks[8], (H, 2 * I), jnp.float32) * w}
    _L0_ffn_all = _L0_ffn_setup()
    _L0_ffn_in = {k: v for k, v in _L0_ffn_all.items() if k in ('gate_w', 'gate_bias', 'expert_gate', 'expert_up', 'expert_down', 'shared_gate', 'shared_up', 'shared_down')}
    del _L0_ffn_all
    return {'x': x, 'L0_tok_general_token': _L0_tok_in['general_token'], 'L0_tok_W_qkv': _L0_tok_in['W_qkv'], 'L0_tok_b_qkv': _L0_tok_in['b_qkv'], 'L0_tok_W_proj': _L0_tok_in['W_proj'], 'L0_tok_b_proj': _L0_tok_in['b_proj'], 'L0_tok_ln_g': _L0_tok_in['ln_g'], 'L0_tok_ln_b': _L0_tok_in['ln_b'], 'L0_attn_pos': _L0_attn_in['pos'], 'L0_attn_in_proj_weight': _L0_attn_in['in_proj_weight'], 'L0_attn_in_proj_bias': _L0_attn_in['in_proj_bias'], 'L0_attn_pos_proj_weight': _L0_attn_in['pos_proj_weight'], 'L0_attn_pos_proj_bias': _L0_attn_in['pos_proj_bias'], 'L0_attn_out_proj_weight': _L0_attn_in['out_proj_weight'], 'L0_attn_out_proj_bias': _L0_attn_in['out_proj_bias'], 'L0_attn_r_w_bias': _L0_attn_in['r_w_bias'], 'L0_attn_r_r_bias': _L0_attn_in['r_r_bias'], 'L0_ffn_gate_w': _L0_ffn_in['gate_w'], 'L0_ffn_gate_bias': _L0_ffn_in['gate_bias'], 'L0_ffn_expert_gate': _L0_ffn_in['expert_gate'], 'L0_ffn_expert_up': _L0_ffn_in['expert_up'], 'L0_ffn_expert_down': _L0_ffn_in['expert_down'], 'L0_ffn_shared_gate': _L0_ffn_in['shared_gate'], 'L0_ffn_shared_up': _L0_ffn_in['shared_up'], 'L0_ffn_shared_down': _L0_ffn_in['shared_down']}

def reference(x, L0_tok_general_token, L0_tok_W_qkv, L0_tok_b_qkv, L0_tok_W_proj, L0_tok_b_proj, L0_tok_ln_g, L0_tok_ln_b, L0_attn_pos, L0_attn_in_proj_weight, L0_attn_in_proj_bias, L0_attn_pos_proj_weight, L0_attn_pos_proj_bias, L0_attn_out_proj_weight, L0_attn_out_proj_bias, L0_attn_r_w_bias, L0_attn_r_r_bias, L0_ffn_gate_w, L0_ffn_gate_bias, L0_ffn_expert_gate, L0_ffn_expert_up, L0_ffn_expert_down, L0_ffn_shared_gate, L0_ffn_shared_up, L0_ffn_shared_down):
    import jax
    import jax.numpy as jnp

    def _L0_tok_ref(x, general_token, W_qkv, b_qkv, W_proj, b_proj, ln_g, ln_b):
        import jax, jax.numpy as jnp
        import numpy as np
        HEADS = 16
        LN_EPS = 1e-05

        def _layernorm(x, g, b):
            mu = jnp.mean(x, axis=-1, keepdims=True)
            var = jnp.var(x, axis=-1, keepdims=True)
            return (x - mu) * jax.lax.rsqrt(var + LN_EPS) * g + b
        B, N, C = x.shape
        H = HEADS
        hd = C // H
        scale = hd ** (-0.5)
        gt = jnp.broadcast_to(general_token, (B, general_token.shape[1], C))
        gt = gt @ W_proj + b_proj
        gt = _layernorm(gt, ln_g, ln_b)
        kv_in = jnp.concatenate([x, gt], axis=1)
        L = kv_in.shape[1]
        qkv = (kv_in @ W_qkv + b_qkv).reshape(B, L, 3, H, hd)
        qkv = jnp.transpose(qkv, (2, 0, 3, 1, 4))
        q, k, v = (qkv[0], qkv[1], qkv[2])
        attn = jnp.einsum('bhqd,bhkd->bhqk', q, k) * scale
        attn = jax.nn.softmax(attn, axis=-1)
        out = jnp.einsum('bhqk,bhkd->bhqd', attn, v)
        out = jnp.transpose(out, (0, 2, 1, 3)).reshape(B, L, C)
        out = out @ W_proj + b_proj
        return out

    def _L0_attn_ref(x, pos, in_proj_weight, in_proj_bias, pos_proj_weight, pos_proj_bias, out_proj_weight, out_proj_bias, r_w_bias, r_r_bias):
        import jax, jax.numpy as jnp
        import numpy as np
        T, B, E, H = (256, 2, 256, 16)
        D = E // H
        R = 2 * T - 1

        def _rel_shift(x):
            b, h, q, r = x.shape
            zp = jnp.zeros((b, h, q, 1), x.dtype)
            xp = jnp.concatenate([zp, x], axis=3)
            xp = xp.reshape(b, h, r + 1, q)[:, :, 1:, :]
            return xp.reshape(b, h, q, r)
        t, b, e = x.shape
        h, d = r_w_bias.shape
        qkv = x @ in_proj_weight.T + in_proj_bias
        q, k, v = jnp.split(qkv, 3, axis=-1)
        q = q.reshape(t, b, h, d)
        k = k.reshape(t, b, h, d)
        v = v.reshape(t, b, h, d)
        p = (pos @ pos_proj_weight.T + pos_proj_bias).reshape(-1, h, d)
        scale = 1.0 / jnp.sqrt(jnp.asarray(d, x.dtype))
        ac = jnp.einsum('tbhd,sbhd->bhts', q + r_w_bias, k)
        bd = jnp.einsum('tbhd,rhd->bhtr', q + r_r_bias, p)
        bd = _rel_shift(bd)[..., :t]
        attn = jax.nn.softmax((ac + bd) * scale, axis=-1)
        ctx = jnp.einsum('bhts,sbhd->tbhd', attn, v).reshape(t, b, e)
        return ctx @ out_proj_weight.T + out_proj_bias

    def _L0_ffn_ref(hidden_states, gate_w, gate_bias, expert_gate, expert_up, expert_down, shared_gate, shared_up, shared_down):
        import jax, jax.numpy as jnp
        import numpy as np
        N_EXPERTS = 32
        TOP_K = 8
        N_GROUP = 4
        TOPK_GROUP = 2
        ROUTED_SCALING = 2.5

        def _gate(x, gate_w, gate_bias):
            T, E = (x.shape[0], gate_w.shape[0])
            logits = jnp.einsum('th,eh->te', x, gate_w)
            scores = jax.nn.sigmoid(logits)
            scores_choice = scores + gate_bias[None, :]
            grp = scores_choice.reshape(T, N_GROUP, E // N_GROUP)
            top2, _ = jax.lax.top_k(grp, 2)
            group_scores = top2.sum(-1)
            _, grp_idx = jax.lax.top_k(group_scores, TOPK_GROUP)
            group_mask = jax.nn.one_hot(grp_idx, N_GROUP, dtype=scores.dtype).sum(1)
            expert_mask = jnp.repeat(group_mask, E // N_GROUP, axis=1)
            masked = jnp.where(expert_mask > 0, scores_choice, 0.0)
            _, topk_idx = jax.lax.top_k(masked, TOP_K)
            topk_w = jnp.take_along_axis(scores, topk_idx, axis=1)
            topk_w = topk_w / (topk_w.sum(-1, keepdims=True) + 1e-20)
            topk_w = topk_w * ROUTED_SCALING
            return (topk_idx, topk_w)

        def _mlp(x, wg, wu, wd):
            return jnp.einsum('...i,hi->...h', jax.nn.silu(jnp.einsum('...h,ih->...i', x, wg)) * jnp.einsum('...h,ih->...i', x, wu), wd)
        orig_shape = hidden_states.shape
        H = orig_shape[-1]
        residuals = hidden_states
        x = hidden_states.reshape(-1, H)
        topk_idx, topk_w = _gate(x, gate_w, gate_bias)
        g = jnp.einsum('th,eih->eti', x, expert_gate)
        u = jnp.einsum('th,eih->eti', x, expert_up)
        outs = jnp.einsum('eti,ehi->eth', jax.nn.silu(g) * u, expert_down)
        outs_t = jnp.transpose(outs, (1, 0, 2))
        gathered = jnp.take_along_axis(outs_t, topk_idx[:, :, None], axis=1)
        final = (gathered * topk_w[:, :, None]).sum(1)
        shared = _mlp(residuals, shared_gate, shared_up, shared_down)
        return final.reshape(orig_shape) + shared
    h = _L0_tok_ref(x, L0_tok_general_token, L0_tok_W_qkv, L0_tok_b_qkv, L0_tok_W_proj, L0_tok_b_proj, L0_tok_ln_g, L0_tok_ln_b)
    h = h + _L0_attn_ref(_layernorm(h, axis=-1), L0_attn_pos, L0_attn_in_proj_weight, L0_attn_in_proj_bias, L0_attn_pos_proj_weight, L0_attn_pos_proj_bias, L0_attn_out_proj_weight, L0_attn_out_proj_bias, L0_attn_r_w_bias, L0_attn_r_r_bias)
    h = h + _L0_ffn_ref(_layernorm(h, axis=-1), L0_ffn_gate_w, L0_ffn_gate_bias, L0_ffn_expert_gate, L0_ffn_expert_up, L0_ffn_expert_down, L0_ffn_shared_gate, L0_ffn_shared_up, L0_ffn_shared_down)
    return h

_drawn_inputs = setup_inputs


def setup_inputs(seed=0):
    import zlib

    import numpy as np

    out = dict(_drawn_inputs(seed))
    spreads = {'L0_tok_b_qkv': (0.0, 0.1),
     'L0_tok_b_proj': (0.0, 0.1),
     'L0_tok_ln_g': (1.0, 0.6),
     'L0_tok_ln_b': (0.0, 0.8),
     'L0_attn_in_proj_bias': (0.0, 0.1),
     'L0_attn_pos_proj_bias': (0.0, 0.8),
     'L0_attn_out_proj_bias': (0.0, 0.1)}
    factors = {'L0_attn_r_w_bias': 8.0,
     'L0_attn_r_r_bias': 8.0,
     'L0_ffn_gate_w': 6.758,
     'L0_ffn_gate_bias': 8.0,
     'L0_ffn_expert_gate': 4.741,
     'L0_ffn_expert_up': 4.854,
     'L0_ffn_expert_down': 4.733,
     'L0_ffn_shared_gate': 3.181,
     'L0_ffn_shared_up': 2.926,
     'L0_ffn_shared_down': 3.146}
    for name, (base, spread) in spreads.items():
        noise = np.random.default_rng([zlib.crc32(name.encode()), seed]).standard_normal(out[name].shape)
        drawn = base * np.exp(spread * noise) if base else spread * noise
        out[name] = jnp.asarray(drawn.astype(out[name].dtype))
    for name, factor in factors.items():
        out[name] = (out[name] * factor).astype(out[name].dtype)
    return out
```

```python
from contextlib import ExitStack

import numpy as np

import concourse.bass as bass
from concourse import mybir

F32 = mybir.dt.float32
F32R = mybir.dt.float32r
ALU = mybir.AluOpType
ACT = mybir.ActivationFunctionType
AX_X = mybir.AxisListType.X

B, N, C, H = 4, 512, 256, 16
HD = C // H
L = N + 1
LP = 516
HALF = LP // 2
KC = C // 128
SCALE = float(HD) ** -0.5
EPS = 1e-5
NCH = 5
CH = 103
QSIZE = [CH] * 4 + [LP - 4 * CH]
KSIZE = [CH] * 4 + [L - 4 * CH]
PAIRS = H // 2
GROUPS = H // 4
TILES = B * NCH
T = B * L
REL = 2 * B - 1
QKVB = 3 * C + REL * H
E, GE, TOPK, EGROUPS, KGROUPS = 32, 8, 8, 4, 2
ROUTED_SCALING = 2.5
INNER = 128
BLK = 342
NBLK = T // BLK
UNITS = 4
LOWEST = -3.0e38


def f32(ap):
    return ap.bitcast(F32)


def split_matmul(nc, out, left, right, first=True, last=True):
    terms = [(l, r) for l, r in zip(left, right)]
    n = 3 * len(terms)
    i = 0
    for (lh, ll), (rh, rl) in terms:
        for a, b in ((lh, rh), (lh, rl), (ll, rh)):
            m = nc.tensor.matmul(out, a, b, start=first and i == 0, stop=last and i == n - 1)
            i += 1
    return m


def token_attention(nc, d, h0):
    with ExitStack() as ctx:
        def sb(name, shape, dt=F32):
            return ctx.enter_context(nc.sbuf_tensor("a_" + name, shape, dt))

        def sem(name):
            return ctx.enter_context(nc.semaphore("a_" + name))

        x = sb("x", [128, KC, B, LP])
        w_qk = sb("w_qk", [128, KC, 2, PAIRS * 128])
        w_v = sb("w_v", [128, KC, C])
        w_proj = sb("w_proj", [128, KC, C])
        w_ctx = sb("w_ctx", [128, GROUPS, C])
        cols = sb("cols", [128, 64])
        rows = sb("rows", [128, 2, C])
        ident = sb("ident", [128, 128])
        sum_rows = sb("sum_rows", [128, 128])
        mean_all = sb("mean_all", [128, 128])
        B_QK, CB_QK, MASK, B_P, LN_G, LN_B, GT = 0, 16, 32, 34, 36, 38, 40

        whi = sb("whi", [128, KC, 2, PAIRS * 128], F32R)
        wlo = sb("wlo", [128, KC, 2, PAIRS * 128], F32R)
        vhi = sb("vhi", [128, KC, C], F32R)
        vlo = sb("vlo", [128, KC, C], F32R)
        xhi = sb("xhi", [128, KC, LP], F32R)
        xlo = sb("xlo", [128, KC, LP], F32R)
        opnd = sb("opnd", [128, 2, PAIRS, LP], F32R)
        part = sb("part", [128, 3, LP], F32R)
        vaug = sb("vaug", [CH, NCH, H, 2 * HD])
        mx = sb("mx", [128, 4, NCH])
        negm = sb("negm", [128, 4, NCH])
        mcols = sb("mcols", [128, 2, NCH, 128])
        mhi = sb("mhi", [128, 4, NCH], F32R)
        probs = sb("probs", [CH, 8, LP])
        osb = sb("osb", [128, LP])
        rsum = sb("rsum", [128, LP])
        ctxt = sb("ctxt", [128, GROUPS, LP])
        g = sb("g", [128, 32])

        ring = [ctx.enter_context(nc.psum_tensor(f"a_ring{i}", [128, 2, 512], F32)) for i in range(3)]
        ps_o = ctx.enter_context(nc.psum_tensor("a_ps_o", [128, 2, 512], F32))

        loaded = sem("loaded")
        gt_pe = sem("gt_pe")
        gt_dve = sem("gt_dve")
        gt_act = sem("gt_act")
        w_high = sem("w_high")
        w_low = sem("w_low")
        x_high = sem("x_high")
        x_low = sem("x_low")
        filled = [sem(f"filled{i}") for i in range(3)]
        freed = [sem(f"freed{i}") for i in range(3)]
        part_ready = sem("part_ready")
        gt_x = sem("gt_x")
        zero_mx = sem("zero_mx")
        neg_done = sem("neg_done")
        high_done = sem("high_done")
        mcols_ready = sem("mcols_ready")
        o_full = sem("o_full")
        o_copied = sem("o_copied")
        ctx_ready = sem("ctx_ready")
        zeroed = sem("zeroed")

        PRO = [("P", 0), ("P", 1), ("P", 2), ("P", 3)] + [("M", i) for i in range(20)] + [("P", 0), ("P", 1)]
        order = []
        for s in range(1, 5):
            if s == 1:
                order += [("V", s, i) for i in range(NCH)]
            order += [("X", s, 0), ("X", s, 1), ("P", s, 2), ("P", s, 3)]
            for i in range(20):
                order += [("T", s, i), ("M", s, i)]
            order += [("P", s, 0), ("P", s, 1), ("S", s, 0)]
            if s == 4:
                order += [("O", s, i) for i in range(NCH)]
        tail = [t for t in order if not (
            (t[0] == "P" and (t[1] == 4 or (t[1] == 3 and t[2] < 2))) or (t[0] == "M" and t[1] == 4))]
        assert len(order) % 3 == 0
        START = len(PRO)
        BODY = len(order) // 3
        at_body = {t: START + i for i, t in enumerate(order)}
        at_tail = {t: START + i for i, t in enumerate(tail)}

        class Use:

            def __init__(self, u, b=0):
                self.slot = u % 3
                self.tile = ring[self.slot]
                self.n = u // 3 + b * BODY

        def use(t, b, last):
            return Use((at_tail if last else at_body)[t], b)

        def consumed(eng, u):
            eng.wait_ge(freed[u.slot], u.n + 1)

        def fill_wait(pe, u, first=False):
            if not first:
                pe.wait_ge(freed[u.slot], u.n)

        with nc.Block() as block:
            @block.sync
            def _(sp):
                for dst, src in ((x, d["xt"]), (w_proj, d["w_proj"]), (cols, d["cols"]), (rows, d["rows"]),
                                 (ident, d["ident"]), (sum_rows, d["sum_rows"]), (mean_all, d["mean_all"]),
                                 (w_qk, d["w_qk"]), (w_v, d["w_v"]), (w_ctx, d["w_ctx"])):
                    sp.dma_start(dst[:], src).then_inc(loaded, 16)

            LOADED = 160

            @block.gpsimd
            def _(pool):
                nc.gpsimd.memset(mcols[:], 0.0).then_inc(zeroed, 1)
                nc.gpsimd.memset(vaug[:], 1.0).then_inc(zeroed, 1)

            @block.tensor
            def _(pe):
                gp = ps_o[:, 0, :]
                pe.wait_ge(loaded, LOADED)
                for j in range(KC):
                    for k in range(KC):
                        m = nc.tensor.matmul(gp[:, j:j + 1], w_proj[:, k, 128 * j:128 * j + 128],
                                             cols[:, GT + k:GT + k + 1], start=k == 0, stop=k == KC - 1)
                m.then_inc(gt_pe, 1)
                pe.wait_ge(gt_dve, 1)
                for k in range(KC):
                    m = nc.tensor.matmul(gp[:, 2:3], mean_all[:], g[:, k:k + 1], start=k == 0, stop=k == KC - 1)
                m.then_inc(gt_pe, 1)
                pe.wait_ge(gt_dve, 3)
                for k in range(KC):
                    m = nc.tensor.matmul(gp[:, 3:4], mean_all[:], g[:, 4 + k:5 + k], start=k == 0, stop=k == KC - 1)
                m.then_inc(gt_pe, 1)

                def project(u, pair, qk, first=False):
                    fill_wait(pe, u, first)
                    c0 = pair * 128
                    for half in range(2):
                        hs = slice(half * HALF, half * HALF + HALF)
                        m = split_matmul(nc, u.tile[:, half, 0:HALF],
                                         [(whi[:, k, qk, c0:c0 + 128], wlo[:, k, qk, c0:c0 + 128]) for k in range(KC)],
                                         [(xhi[:, k, hs], xlo[:, k, hs]) for k in range(KC)])
                    m.then_inc(filled[u.slot], 1)

                def values(u, c):
                    fill_wait(pe, u)
                    ks = slice(c * CH, c * CH + KSIZE[c])
                    split_matmul(nc, u.tile[0:KSIZE[c], 0, 0:C],
                                 [(xhi[:, k, ks], xlo[:, k, ks]) for k in range(KC)],
                                 [(vhi[:, k, :], vlo[:, k, :]) for k in range(KC)]).then_inc(filled[u.slot], 1)

                def head(grp, j):
                    return 64 * (j % 2), 2 * grp + j // 2

                def row_scores(u, grp, i, first=False):
                    fill_wait(pe, u, first)
                    r, pair = head(grp, i % 4)
                    c = i // 4
                    for half in range(2):
                        m = nc.tensor.matmul(u.tile[0:QSIZE[c], half, 0:HALF],
                                             opnd[r:r + 64, 0, pair, c * CH:c * CH + QSIZE[c]],
                                             opnd[r:r + 64, 1, pair, half * HALF:half * HALF + HALF],
                                             start=True, stop=True)
                    m.then_inc(filled[u.slot], 1)

                def turn_max(u, pl):
                    fill_wait(pe, u)
                    for c in range(NCH):
                        lo, hi = c * CH, c * CH + QSIZE[c]
                        for half in range(2):
                            a, z = max(lo, half * HALF), min(hi, half * HALF + HALF)
                            if a < z:
                                m = nc.tensor.matmul(u.tile[:, half, a - half * HALF:z - half * HALF],
                                                     mcols[0:QSIZE[c], pl, c, :], ident[0:QSIZE[c], a - lo:z - lo],
                                                     start=True, stop=True)
                    m.then_inc(filled[u.slot], 1)

                def key_scores(u, grp, i):
                    fill_wait(pe, u)
                    r, pair = head(grp, i % 4)
                    c = i // 4
                    for half in range(2):
                        m = nc.tensor.matmul(u.tile[0:KSIZE[c], half, 0:HALF],
                                             opnd[r:r + 64, 1, pair, c * CH:c * CH + KSIZE[c]],
                                             opnd[r:r + 64, 0, pair, half * HALF:half * HALF + HALF],
                                             start=True, stop=True)
                    m.then_inc(filled[u.slot], 1)

                def weigh_values(grp, c, b, s, last):
                    for half in range(2):
                        for j in range(4):
                            if half == 0:
                                consumed(pe, use(("T", s, 4 * c + j), b, last))
                            m = nc.tensor.matmul(ps_o[32 * j:32 * j + 32, half, 0:HALF],
                                                 vaug[0:KSIZE[c], c, 4 * grp + j, :],
                                                 probs[0:KSIZE[c], (4 * c + j) % 8, half * HALF:half * HALF + HALF],
                                                 start=c == 0, stop=c == NCH - 1)
                    return m

                pe.wait_ge(w_high, 2)
                pe.wait_ge(w_low, 2)
                pe.wait_ge(x_high, 1)
                pe.wait_ge(x_low, 1)
                for u in range(4):
                    project(Use(u), u // 2, u % 2, first=u < 3)
                for u in range(4):
                    consumed(pe, Use(u))
                for i in range(20):
                    row_scores(Use(4 + i), 0, i)
                for i in range(2):
                    project(Use(24 + i), 2, i)

                def batch(b, last):
                    for s in range(1, 5):
                        grp = s - 1
                        ahead = not (last and s == 4)
                        if s == 1:
                            for i in range(NCH):
                                values(use(("V", s, i), b, last), i)
                        pe.wait_ge(mcols_ready, b * 4 + s)
                        for i in range(2):
                            turn_max(use(("X", s, i), b, last), i)
                        if ahead:
                            for i in (2, 3):
                                project(use(("P", s, i), b, last), 2 * (s % 4) + 1, i % 2)
                        for i in range(2):
                            consumed(pe, use(("X", s, i), b, last))
                        if s == 1:
                            for i in range(NCH):
                                consumed(pe, use(("V", s, i), b, last))
                        for i in range(20):
                            key_scores(use(("T", s, i), b, last), grp, i)
                            if i % 4 == 3 and i >= 7:
                                if i == 7:
                                    pe.wait_ge(o_copied, b * 4 + s)
                                weigh_values(grp, i // 4 - 1, b, s, last)
                            if ahead:
                                if i == 0:
                                    for k in (2, 3):
                                        consumed(pe, use(("P", s, k), b, last))
                                row_scores(use(("M", s, i), b, last), s % 4, i)
                        weigh_values(grp, NCH - 1, b, s, last).then_inc(o_full, 1)
                        if ahead and not (last and s == 3):
                            if s == 3:
                                pe.wait_ge(x_high, b + 2)
                                pe.wait_ge(x_low, b + 2)
                            for i in range(2):
                                project(use(("P", s, i), b, last), 2 * ((s + 1) % 4), i)
                        u = use(("S", s, 0), b, last)
                        fill_wait(pe, u)
                        pe.wait_ge(o_copied, b * 4 + s + 1)
                        for half in range(2):
                            m = nc.tensor.matmul(u.tile[:, half, 0:HALF], sum_rows[:],
                                                 osb[:, half * HALF:half * HALF + HALF], start=True, stop=True)
                        m.then_inc(filled[u.slot], 1)
                    pe.wait_ge(ctx_ready, b * 4 + 5)
                    for c in range(NCH):
                        u = use(("O", 4, c), b, last)
                        fill_wait(pe, u)
                        for grp in range(GROUPS):
                            m = nc.tensor.matmul(u.tile[0:CH, 0, 0:C], ctxt[:, grp, c * CH:c * CH + CH],
                                                 w_ctx[:, grp, :], start=grp == 0, stop=grp == GROUPS - 1)
                        m.then_inc(filled[u.slot], 1)

                with pe.Fori(0, B - 1) as b:
                    batch(b, False)
                batch(B - 1, True)

            @block.scalar
            def _(act):
                act.sem_inc(o_copied, 1)
                act.wait_ge(loaded, LOADED)
                nc.scalar.activation(whi[:], w_qk[:], ACT.Copy).then_inc(w_high, 1)
                nc.scalar.activation(vhi[:], w_v[:], ACT.Copy).then_inc(w_high, 1)
                act.wait_ge(gt_dve, 4)
                nc.scalar.activation(g[:, 8:9], g[:, 7:8], ACT.Sqrt).then_inc(gt_act, 1)

                def split_x(b):
                    nc.scalar.activation(xhi[:], x[:, :, bass.ds(b, 1), :].rearrange("p k b n -> p k (b n)"),
                                         ACT.Copy).then_inc(x_high, 1)

                def high_part(u, pair, qk):
                    act.wait_ge(filled[u.slot], u.n + 1)
                    cb = CB_QK + qk * PAIRS + pair
                    nc.scalar.activation(part[:, u.slot, :].rearrange("p (h n) -> p h n", h=2), u.tile[:, :, 0:HALF],
                                         ACT.Identity, bias=cols[:, cb:cb + 1],
                                         scale=cols[:, MASK + qk:MASK + qk + 1]).then_inc(part_ready, 1)

                act.wait_ge(gt_dve, 10)
                split_x(0)
                for i in range(4):
                    high_part(Use(i), i // 2, i % 2)
                for i in range(2):
                    high_part(Use(24 + i), 2, i)

                def batch(b, last):
                    for s in range(1, 5):
                        if not (last and s == 4):
                            for i in (2, 3):
                                high_part(use(("P", s, i), b, last), 2 * (s % 4) + 1, i % 2)
                        if s == 3 and not last:
                            split_x(b + 1)
                        for i in range(20):
                            u = use(("T", s, i), b, last)
                            act.wait_ge(filled[u.slot], u.n + 1)
                            sz = KSIZE[i // 4]
                            nc.scalar.activation(probs[0:sz, i % 8, :].rearrange("p (h n) -> p h n", h=2),
                                                 u.tile[0:sz, :, 0:HALF], ACT.Exp,
                                                 scale=SCALE).then_inc(freed[u.slot], 1)
                        act.wait_ge(o_full, b * 4 + s)
                        act.wait_ge(ctx_ready, b * 4 + s)
                        nc.scalar.activation(osb[:].rearrange("p (h n) -> p h n", h=2), ps_o[:, :, 0:HALF],
                                             ACT.Copy).then_inc(o_copied, 1)
                        if not last or s < 3:
                            for i in range(2):
                                high_part(use(("P", s, i), b, last), 2 * ((s + 1) % 4), i)

                with act.Fori(0, B - 1) as b:
                    batch(b, False)
                batch(B - 1, True)

            @block.vector
            def _(dve):
                gp = ps_o[:, 0, :]

                def c_(i, n=1):
                    return cols[:, i:i + n]

                dve.sem_inc(ctx_ready, 1)
                dve.wait_ge(gt_pe, 1)
                nc.vector.tensor_tensor(g[:, 0:2], gp[:, 0:2], c_(B_P, 2), ALU.add).then_inc(gt_dve, 1)
                dve.wait_ge(gt_pe, 2)
                dve.wait_ge(gt_dve, 1)
                nc.vector.tensor_scalar(g[:, 2:4], g[:, 0:2], gp[:, 2:3], None, ALU.subtract).then_inc(gt_dve, 1)
                dve.wait_ge(gt_dve, 2)
                nc.vector.tensor_tensor(g[:, 4:6], g[:, 2:4], g[:, 2:4], ALU.mult).then_inc(gt_dve, 1)
                dve.wait_ge(gt_pe, 3)
                nc.vector.tensor_scalar(g[:, 7:8], gp[:, 3:4], EPS, None, ALU.add).then_inc(gt_dve, 1)
                dve.wait_ge(gt_act, 1)
                nc.vector.reciprocal(g[:, 9:10], g[:, 8:9]).then_inc(gt_dve, 1)
                dve.wait_ge(gt_dve, 5)
                nc.vector.scalar_tensor_tensor(g[:, 10:11], g[:, 9:10], g[:, 9:10], g[:, 7:8], ALU.mult,
                                               ALU.mult).then_inc(gt_dve, 1)
                dve.wait_ge(gt_dve, 6)
                nc.vector.tensor_scalar(g[:, 11:12], g[:, 10:11], -0.5, 1.5, ALU.mult, ALU.add).then_inc(gt_dve, 1)
                dve.wait_ge(gt_dve, 7)
                nc.vector.tensor_scalar(g[:, 12:14], g[:, 2:4], g[:, 9:10], g[:, 11:12], ALU.mult,
                                        ALU.mult).then_inc(gt_dve, 1)
                dve.wait_ge(gt_dve, 8)
                nc.vector.tensor_tensor(g[:, 14:16], g[:, 12:14], c_(LN_G, 2), ALU.mult).then_inc(gt_dve, 1)
                dve.wait_ge(gt_dve, 9)
                nc.vector.tensor_tensor(g[:, 16:18], g[:, 14:16], c_(LN_B, 2), ALU.add).then_inc(gt_x, 1)
                dve.wait_ge(gt_x, 1)
                for k in range(KC):
                    m = nc.vector.tensor_scalar(x[:, k, :, N], ident[:, 0:B], 0.0, g[:, 16 + k:17 + k],
                                                ALU.mult, ALU.add)
                m.then_inc(gt_dve, 1)
                dve.wait_ge(w_high, 2)
                nc.vector.tensor_tensor(wlo[:], w_qk[:], f32(whi[:]), ALU.subtract).then_inc(w_low, 1)
                nc.vector.tensor_tensor(vlo[:], w_v[:], f32(vhi[:]), ALU.subtract).then_inc(w_low, 1)

                def split_x(b):
                    dve.wait_ge(x_high, b + 1)
                    nc.vector.tensor_tensor(xlo[:], x[:, :, bass.ds(b, 1), :].rearrange("p k b n -> p k (b n)"),
                                            f32(xhi[:]), ALU.subtract).then_inc(x_low, 1)

                def operand(u, pair, qk, n):
                    dve.wait_ge(part_ready, n + 1)
                    cb = B_QK + qk * PAIRS + pair
                    nc.vector.scalar_tensor_tensor(
                        opnd[:, qk, pair, :].rearrange("p (h n) -> p h n", h=2), u.tile[:, :, 0:HALF],
                        cols[:, cb:cb + 1], f32(part[:, u.slot, :]).rearrange("p (h n) -> p h n", h=2),
                        ALU.add, ALU.subtract).then_inc(freed[u.slot], 1)

                def maxima(u, i):
                    sz = QSIZE[i // 4]
                    dve.wait_ge(filled[u.slot], u.n + 1)
                    nc.vector.tensor_reduce(mx[0:sz, i % 4, i // 4:i // 4 + 1], u.tile[0:sz, :, 0:HALF],
                                            mybir.AxisListType.XY, ALU.max).then_inc(freed[u.slot], 1)
                    if i == 19:
                        consumed(dve, u)

                def negate(n):
                    nc.vector.tensor_scalar(negm[:], mx[:], -1.0, None, ALU.mult).then_inc(neg_done, 1)
                    dve.wait_ge(neg_done, n + 1)
                    nc.vector.tensor_copy(mhi[:], negm[:]).then_inc(high_done, 1)
                    dve.wait_ge(high_done, n + 1)
                    cols_of = mcols[:].rearrange("p l c (e r) -> p l e c r", e=2)
                    neg4 = negm[:].rearrange("p (l e) c -> p l e c", l=2)
                    hi4 = f32(mhi[:]).rearrange("p (l e) c -> p l e c", l=2)
                    nc.vector.tensor_copy(cols_of[:, :, :, :, 48], hi4)
                    nc.vector.tensor_tensor(cols_of[:, :, :, :, 49], neg4, hi4, ALU.subtract).then_inc(mcols_ready, 1)

                nc.vector.memset(mx[:], 0.0).then_inc(zero_mx, 1)
                split_x(0)
                for i in range(4):
                    operand(Use(i), i // 2, i % 2, i)
                dve.wait_ge(zero_mx, 1)
                for i in range(20):
                    maxima(Use(4 + i), i)
                dve.wait_ge(zeroed, 2)
                negate(0)
                for i in range(2):
                    operand(Use(24 + i), 2, i, 4 + i)

                def batch(b, last):
                    for s in range(1, 5):
                        ahead = not (last and s == 4)
                        if s == 1:
                            for c in range(NCH):
                                u = use(("V", s, c), b, last)
                                dve.wait_ge(filled[u.slot], u.n + 1)
                                nc.vector.tensor_tensor(
                                    vaug[0:KSIZE[c], c, :, 0:HD],
                                    u.tile[0:KSIZE[c], 0, 0:C].rearrange("p (h d) -> p h d", h=H),
                                    rows[0:KSIZE[c], 0, :].rearrange("p (h d) -> p h d", h=H),
                                    ALU.add).then_inc(freed[u.slot], 1)
                        for i in range(2):
                            u = use(("X", s, i), b, last)
                            dve.wait_ge(filled[u.slot], u.n + 1)
                            q = opnd[:, 0, 2 * (s - 1) + i, :].rearrange("p (h n) -> p h n", h=2)
                            nc.vector.tensor_tensor(q, f32(q), u.tile[:, :, 0:HALF], ALU.add).then_inc(freed[u.slot], 1)
                        if ahead:
                            for i in (2, 3):
                                operand(use(("P", s, i), b, last), 2 * (s % 4) + 1, i % 2, b * 16 + 4 * s + i)
                        if s == 3 and not last:
                            split_x(b + 1)
                        if ahead:
                            for i in range(20):
                                maxima(use(("M", s, i), b, last), i)
                            negate(b * 4 + s)
                        if ahead and not (last and s == 3):
                            for i in range(2):
                                operand(use(("P", s, i), b, last), 2 * ((s + 1) % 4), i, b * 16 + 4 * s + 4 + i)
                        u = use(("S", s, 0), b, last)
                        dve.wait_ge(filled[u.slot], u.n + 1)
                        nc.vector.reciprocal(rsum[:].rearrange("p (h n) -> p h n", h=2),
                                             u.tile[:, :, 0:HALF]).then_inc(freed[u.slot], 1)
                        consumed(dve, u)
                        nc.vector.tensor_tensor(ctxt[:, s - 1, :], osb[:], rsum[:], ALU.mult).then_inc(ctx_ready, 1)
                    for c in range(NCH):
                        u = use(("O", 4, c), b, last)
                        dve.wait_ge(filled[u.slot], u.n + 1)
                        nc.vector.tensor_tensor(h0[:, bass.ds(b * NCH + c, 1), :].rearrange("p t f -> p (t f)"),
                                                u.tile[0:CH, 0, 0:C], rows[0:CH, 1, :],
                                                ALU.add).then_inc(freed[u.slot], 1)

                with dve.Fori(0, B - 1) as b:
                    batch(b, False)
                batch(B - 1, True)


def relative_attention(nc, d, h0, route, y, xh, xl):
    with ExitStack() as ctx:
        def sb(name, shape, dt=F32):
            return ctx.enter_context(nc.sbuf_tensor("b_" + name, shape, dt))

        def sem(name):
            return ctx.enter_context(nc.semaphore("b_" + name))

        W2 = REL * H
        w_in = sb("w_in", [128, KC, QKVB])
        w_q = sb("w_q", [128, KC, C])
        w_pos = sb("w_pos", [128, KC, C])
        w_out = sb("w_out", [128, KC, C])
        w_gate = sb("w_gate", [128, KC, E])
        pos = sb("pos", [128, KC, REL])
        own = sb("own", [128, KC, W2])
        small = sb("small", [128, 16])
        B_POS, B_Q, R_R = 0, 2, 4
        in_rows = sb("in_rows", [128, QKVB])
        rw_row = sb("rw_row", [128, C])
        out_row = sb("out_row", [128, C])
        gate_row = sb("gate_row", [128, E])
        ident = sb("ident", [128, 128])

        posT = sb("posT", [128, KC, REL])
        pblk = sb("pblk", [128, KC, W2])
        qrr = sb("qrr", [128, KC])
        qrr_all = sb("qrr_all", [128, KC, 128])
        inhi = sb("inhi", [128, KC, QKVB], F32R)
        inlo = sb("inlo", [128, KC, QKVB], F32R)
        ghi = sb("ghi", [128, KC, E], F32R)
        glo = sb("glo", [128, KC, E], F32R)

        stats = sb("stats", [CH, TILES, 6])
        stat = sb("stat", [CH, 6, TILES])
        MEAN, VAR, RSTD, TMP, TMP2 = range(5)
        xn = sb("xn", [CH, 2, C])
        hT = sb("hT", [128, 2, KC, CH], F32R)
        hTl = sb("hTl", [128, 2, KC, CH], F32R)
        qkvb = sb("qkvb", [CH, 4272])
        prod = sb("prod", [CH, B, B, C])
        sc = sb("sc", [CH, B, B * H])
        m2 = sb("m2", [CH, B, 2 * H])
        m1 = sb("m1", [CH, B, H])
        ctx_t = sb("ctx_t", [CH, B, C])
        cT = sb("cT", [128, 2, KC, CH])
        hs = sb("hs", [CH, 2, C])
        lg = sb("lg", [CH, TILES, E])
        choice = sb("choice", [CH, TILES, E])
        masked = sb("masked", [CH, TILES, E])
        left = sb("left", [CH, TILES, E])
        top = sb("top", [CH, TILES, EGROUPS, 8])
        gs = sb("gs", [CH, TILES, EGROUPS])
        beat = sb("beat", [CH, TILES, EGROUPS])
        rank = sb("rank", [CH, TILES, EGROUPS])
        gsum = sb("gsum", [CH, TILES, 2])
        w64 = sb("w64", [CH, TILES, 2 * E])
        whi_r = sb("whi_r", [CH, TILES, E], F32R)

        tp = [ctx.enter_context(nc.psum_tensor(f"b_tp{i}", [128, 512], F32)) for i in range(2)]
        pq = [ctx.enter_context(nc.psum_tensor(f"b_pq{i}", [128, 2, 512], F32)) for i in range(2)]
        po = [ctx.enter_context(nc.psum_tensor(f"b_po{i}", [128, 512], F32)) for i in range(2)]

        loaded = sem("loaded")
        setup_pe = sem("setup_pe")
        setup = sem("setup")
        setup_act = sem("setup_act")
        rel_ready = sem("rel_ready")
        stats_done = sem("stats_done")
        chain = sem("chain")
        xn_ready = sem("xn_ready")
        turned = sem("turned")
        hi_ready = sem("hi_ready")
        lo_ready = sem("lo_ready")
        qkv_full = sem("qkv_full")
        qkv_read = sem("qkv_read")
        qk_done = sem("qk_done")
        shifted = sem("shifted")
        expd = sem("expd")
        p_ready = sem("p_ready")
        pv_done = sem("pv_done")
        ctx_ready = sem("ctx_ready")
        c_turned = sem("c_turned")
        c_copied = sem("c_copied")
        out_full = sem("out_full")
        h_half = sem("h_half")
        h_done = sem("h_done")
        prod_used = sem("prod_used")
        sq = sem("sq")
        sq2 = sem("sq2")
        h_copied = sem("h_copied")
        x2_ready = sem("x2_ready")
        t2 = sem("t2")
        x2hi = sem("x2hi")
        y_copied = sem("y_copied")
        x2lo = sem("x2lo")
        x2_stored = sem("x2_stored")
        lg_full = sem("lg_full")
        lg_read = sem("lg_read")
        routed = sem("routed")
        w_turned = sem("w_turned")
        w_stored = sem("w_stored")

        COLS = [(0, 512), (512, QKVB)]

        with nc.Block() as block:
            @block.sync
            def _(sp):
                for dst, name in ((w_pos, "w_pos"), (pos, "pos"), (own, "own"), (small, "small"), (w_q, "w_q"),
                                  (ident, "ident"), (out_row, "out_row"), (gate_row, "gate_row"), (rw_row, "rw_row"),
                                  (w_out, "w_out"), (w_gate, "w_gate")):
                    sp.dma_start(dst[:], d[name]).then_inc(loaded, 16)
                sp.dma_start(w_in[:, :, 0:3 * C], d["w_in"]).then_inc(loaded, 16)
                sp.dma_start(in_rows[:, 0:3 * C], d["in_rows"]).then_inc(loaded, 16)

            LOADED = 13 * 16

            @block.tensor
            def _(pe):
                pe.wait_ge(loaded, LOADED)
                for j in range(KC):
                    for k in range(KC):
                        m = nc.tensor.matmul(po[0][:, 8 * j:8 * j + REL], w_pos[:, k, 128 * j:128 * j + 128],
                                             pos[:, k, :], start=k == 0, stop=k == KC - 1)
                m.then_inc(setup_pe, 1)
                pe.wait_ge(rel_ready, 1)
                for j in range(KC):
                    for k in range(KC):
                        nc.tensor.matmul(po[1][:, W2 * j:W2 * j + W2], w_q[:, k, 128 * j:128 * j + 128],
                                         pblk[:, k, :], start=k == 0, stop=k == KC - 1)
                for k in range(KC):
                    m = nc.tensor.matmul(po[1][:, W2 * 2:W2 * 3], qrr_all[:, k, :], pblk[:, k, :],
                                         start=k == 0, stop=k == KC - 1)
                m.then_inc(setup_pe, 1)
                pe.wait_ge(setup_act, 1)
                pe.wait_ge(rel_ready, 3)

                def turn(b, n):
                    pe.wait_ge(xn_ready, n + 1)
                    pe.wait_ge(lo_ready, n - 1 + 2)
                    for k in range(KC):
                        m = nc.tensor.transpose(tp[b % 2][:, k * 128:k * 128 + CH], xn[:, b % 2, 128 * k:128 * k + 128],
                                                ident[0:CH, 0:CH])
                    m.then_inc(turned, 1)

                def project(b, n):
                    pe.wait_ge(hi_ready, n + 1)
                    pe.wait_ge(lo_ready, n + 1 + 2)
                    pe.wait_ge(qkv_read, n - 1 + 2)
                    for i, (a, z) in enumerate(COLS):
                        m = split_matmul(nc, pq[b % 2][0:CH, i, 0:z - a],
                                         [(hT[:, b % 2, k, 0:CH], hTl[:, b % 2, k, 0:CH]) for k in range(KC)],
                                         [(inhi[:, k, a:z], inlo[:, k, a:z]) for k in range(KC)])
                    m.then_inc(qkv_full, 1)

                with pe.Fori(0, NCH) as c:
                    turn(0, c * B)
                    for b in range(B):
                        if b + 1 < B:
                            turn(b + 1, c * B + b + 1)
                        project(b, c * B + b)
                    pe.wait_ge(ctx_ready, c + 1)
                    for b in range(B):
                        n = c * B + b
                        pe.wait_ge(c_copied, n - 1 + 2)
                        for k in range(KC):
                            m = nc.tensor.transpose(tp[b % 2][:, 256 + k * 128:256 + k * 128 + CH],
                                                    ctx_t[:, b, 128 * k:128 * k + 128], ident[0:CH, 0:CH])
                        m.then_inc(c_turned, 1)
                        pe.wait_ge(c_copied, n + 1 + 2)
                        pe.wait_ge(h_half, n - 1 + 2)
                        for k in range(KC):
                            m = nc.tensor.matmul(po[b % 2][0:CH, 0:C], cT[:, b % 2, k, :], w_out[:, k, :],
                                                 start=k == 0, stop=k == KC - 1)
                        m.then_inc(out_full, 1)

                with pe.Fori(0, NCH) as c:
                    for b in range(B):
                        n = c * B + b
                        pe.wait_ge(h_copied, n + 1)
                        pe.wait_ge(x2_ready, n + 1)
                        pe.wait_ge(x2lo, n - 1 + 2)
                        pe.wait_ge(y_copied, n - 1 + 2)
                        for k in range(KC):
                            nc.tensor.transpose(tp[b % 2][:, k * 128:k * 128 + CH], xn[:, b % 2, 128 * k:128 * k + 128],
                                                ident[0:CH, 0:CH])
                            m = nc.tensor.transpose(pq[b % 2][:, 0, k * 128:k * 128 + CH],
                                                    hs[:, b % 2, 128 * k:128 * k + 128], ident[0:CH, 0:CH])
                        m.then_inc(t2, 1)
                        pe.wait_ge(x2lo, n + 1 + 2)
                        pe.wait_ge(lg_read, n - 1 + 2)
                        split_matmul(nc, po[b % 2][0:CH, 0:E],
                                     [(hT[:, b % 2, k, 0:CH], hTl[:, b % 2, k, 0:CH]) for k in range(KC)],
                                     [(ghi[:, k, :], glo[:, k, :]) for k in range(KC)]).then_inc(lg_full, 1)
                pe.wait_ge(routed, 1)
                for t in range(TILES):
                    if t % 4 == 0 and t >= 8:
                        pe.wait_ge(w_stored, t // 4 - 1)
                    m = nc.tensor.transpose(pq[t // 4 % 2][0:2 * E, 0, t % 4 * CH:t % 4 * CH + CH], w64[:, t, :],
                                            ident[0:CH, 0:CH])
                    if t % 4 == 3:
                        m.then_inc(w_turned, 1)

            @block.gpsimd
            def _(pool):
                with pool.Fori(0, NCH) as c:
                    pool.wait_ge(qkv_read, c * B + B + 2)
                    for t in (2, 3):
                        for s in range(B):
                            m = nc.gpsimd.tensor_tensor(prod[:, t, s, :], qkvb[:, t * QKVB:t * QKVB + C],
                                                        qkvb[:, s * QKVB + C:s * QKVB + 2 * C], ALU.mult)
                    m.then_inc(qk_done, 1)
                pool.wait_ge(h_done, TILES)
                with pool.Fori(0, NCH) as c:
                    for b in range(B):
                        n = c * B + b
                        pool.wait_ge(t2, n - 1 + 2)
                        nc.gpsimd.tensor_copy(hs[:, b % 2, :], h0[:, bass.ds(b * NCH + c, 1), :].rearrange(
                            "p t f -> p (t f)")).then_inc(h_copied, 1)
                        pool.wait_ge(x2lo, n + 1 + 2)
                        pos_ = b * NCH + c
                        nc.gpsimd.tensor_copy(xh[:, :, bass.ds(pos_, 1), :].rearrange("p k t n -> p k (t n)"),
                                              f32(hT[:, b % 2]))
                        nc.gpsimd.tensor_copy(xl[:, :, bass.ds(pos_, 1), :].rearrange("p k t n -> p k (t n)"),
                                              f32(hTl[:, b % 2])).then_inc(x2_stored, 1)

            @block.scalar
            def _(act):
                act.wait_ge(rel_ready, 2)
                nc.scalar.activation(inhi[:], w_in[:], ACT.Copy)
                nc.scalar.activation(ghi[:], w_gate[:], ACT.Copy).then_inc(setup_act, 1)
                act.wait_ge(stats_done, 1)
                nc.scalar.activation(stat[:, TMP, :], stat[:, VAR, :], ACT.Sqrt).then_inc(sq, 1)
                with act.Fori(0, NCH) as c:
                    for b in range(B):
                        n = c * B + b
                        act.wait_ge(turned, n + 1)
                        act.wait_ge(qkv_full, n - 1 + 2)
                        nc.scalar.activation(hT[:, b % 2, :, :],
                                             tp[b % 2][:, 0:256].rearrange("p (k n) -> p k n", k=KC)[:, :, 0:CH],
                                             ACT.Copy).then_inc(hi_ready, 1)
                    act.wait_ge(shifted, c + 1)
                    nc.scalar.activation(sc[:], sc[:], ACT.Exp, scale=SCALE).then_inc(expd, 1)
                    for b in range(B):
                        n = c * B + b
                        act.wait_ge(c_turned, n + 1)
                        act.wait_ge(out_full, n - 1 + 2)
                        nc.scalar.activation(cT[:, b % 2, :, :],
                                             tp[b % 2][:, 256:512].rearrange("p (k n) -> p k n", k=KC)[:, :, 0:CH],
                                             ACT.Copy).then_inc(c_copied, 1)
                act.wait_ge(stats_done, 2)
                nc.scalar.activation(stat[:, TMP, :], stat[:, VAR, :], ACT.Sqrt).then_inc(sq, 1)
                with act.Fori(0, NCH) as c:
                    for b in range(B):
                        n = c * B + b
                        act.wait_ge(t2, n + 1 + 2)
                        act.wait_ge(lg_full, n - 1 + 2)
                        act.wait_ge(x2_stored, n - 1 + 2)
                        turned_x, turned_h = (t_.rearrange("p (k n) -> p k n", k=KC)[:, :, 0:CH]
                                              for t_ in (tp[b % 2][:, 0:256], pq[b % 2][:, 0, 0:256]))
                        nc.scalar.activation(hT[:, b % 2, :, :], turned_x, ACT.Copy).then_inc(x2hi, 1)
                        nc.scalar.activation(y[:, :, bass.ds(b * NCH + c, 1), :].rearrange("p k t n -> p k (t n)"),
                                             turned_h, ACT.Copy).then_inc(y_copied, 1)
                        act.wait_ge(lg_full, n + 1 + 2)
                        nc.scalar.activation(lg[:, bass.ds(b * NCH + c, 1), :].rearrange("p t f -> p (t f)"),
                                             po[b % 2][0:CH, 0:E], ACT.Sigmoid).then_inc(lg_read, 1)
                for k in range(TILES // 4):
                    act.wait_ge(w_turned, k + 1)
                    nc.scalar.activation(route[:, k * BLKP:(k + 1) * BLKP], pq[k % 2][0:2 * E, 0, 0:BLKP],
                                         ACT.Copy).then_inc(w_stored, 1)
                act.wait_ge(w_stored, TILES // 4)

            @block.vector
            def _(dve):
                V = nc.vector
                done = [0]

                def link(ins):
                    done[0] += 1
                    ins.then_inc(setup, 1)
                    dve.wait_ge(setup, done[0])

                for s_ in (lo_ready, qkv_read, h_half, x2lo, c_copied, y_copied, lg_read, qkv_full, out_full,
                           lg_full, x2_stored, t2):
                    dve.sem_inc(s_, 2)

                dve.wait_ge(loaded, LOADED)
                dve.wait_ge(setup_pe, 1)
                for k in range(KC):
                    link(V.tensor_scalar(posT[:, k, :], po[0][:, 8 * k:8 * k + REL], small[:, B_POS + k:B_POS + k + 1],
                                         None, ALU.add))
                    link(V.tensor_tensor(pblk[:, k, :].rearrange("p (r h) -> p r h", h=H),
                                         own[:, k, :].rearrange("p (r h) -> p r h", h=H),
                                         posT[:, k, :].unsqueeze(2).to_broadcast([128, REL, H]), ALU.mult))
                link(V.tensor_tensor(qrr[:], small[:, B_Q:B_Q + 2], small[:, R_R:R_R + 2], ALU.add))
                for k in range(KC):
                    m = V.tensor_scalar(qrr_all[:, k, :], ident[:], 0.0, qrr[:, k:k + 1], ALU.mult, ALU.add)
                m.then_inc(rel_ready, 1)
                link(V.tensor_tensor(in_rows[:, 0:C], in_rows[:, 0:C], rw_row[:], ALU.add))
                dve.wait_ge(setup_pe, 2)
                for k in range(KC):
                    link(V.tensor_copy(w_in[:, k, 3 * C:QKVB], po[1][:, W2 * k:W2 * k + W2]))
                V.tensor_copy(in_rows[:, 3 * C:QKVB], po[1][:, 2 * W2:3 * W2]).then_inc(rel_ready, 1)
                dve.wait_ge(rel_ready, 2)
                dve.wait_ge(setup_act, 1)
                V.tensor_tensor(inlo[:], w_in[:], f32(inhi[:]), ALU.subtract)
                V.tensor_tensor(glo[:], w_gate[:], f32(ghi[:]), ALU.subtract).then_inc(rel_ready, 1)

                def statistics(k):
                    for t in range(TILES):
                        m = V.bn_stats(stats[:, t, :], h0[:, t, :])
                    link(m)
                    me, ve, mo, vo = (stats[:, :, i] for i in (1, 2, 4, 5))
                    link(V.tensor_tensor(stat[:, MEAN, :], me, mo, ALU.add))
                    link(V.tensor_scalar(stat[:, MEAN, :], stat[:, MEAN, :], 0.5, None, ALU.mult))
                    link(V.tensor_tensor(stat[:, TMP, :], me, mo, ALU.subtract))
                    link(V.tensor_tensor(stat[:, TMP, :], stat[:, TMP, :], stat[:, TMP, :], ALU.mult))
                    link(V.tensor_scalar(stat[:, TMP, :], stat[:, TMP, :], 0.25, EPS, ALU.mult, ALU.add))
                    link(V.tensor_tensor(stat[:, TMP2, :], ve, vo, ALU.add))
                    V.scalar_tensor_tensor(stat[:, VAR, :], stat[:, TMP2, :], 1.0 / C, stat[:, TMP, :], ALU.mult,
                                           ALU.add).then_inc(stats_done, 1)
                    dve.wait_ge(sq, k)
                    link(V.reciprocal(stat[:, RSTD, :], stat[:, TMP, :]))
                    link(V.tensor_tensor(stat[:, TMP2, :], stat[:, RSTD, :], stat[:, RSTD, :], ALU.mult))
                    link(V.tensor_tensor(stat[:, TMP2, :], stat[:, TMP2, :], stat[:, VAR, :], ALU.mult))
                    link(V.tensor_scalar(stat[:, TMP2, :], stat[:, TMP2, :], -0.5, 1.5, ALU.mult, ALU.add))
                    link(V.tensor_tensor(stat[:, RSTD, :], stat[:, RSTD, :], stat[:, TMP2, :], ALU.mult))

                def normalise(b, c):
                    t = b * NCH + c
                    V.tensor_scalar(xn[:, b % 2, :], h0[:, bass.ds(t, 1), :].rearrange("p t f -> p (t f)"),
                                    stat[:, MEAN, bass.ds(t, 1)], stat[:, RSTD, bass.ds(t, 1)],
                                    ALU.subtract, ALU.mult).then_inc(xn_ready, 1)

                statistics(1)
                qk = qkvb[:, 0:B * QKVB].rearrange("p (t f) -> p t f", t=B)
                STEP = QKVB - H
                rel = qkvb[:, 3 * C + 3 * H:3 * C + 3 * H + B * STEP].rearrange("p (t f) -> p t f", f=STEP)[:, :, 0:B * H]
                STEPS = 14
                with dve.Fori(0, NCH) as c:
                    steps = [0]

                    def step(ins):
                        steps[0] += 1
                        ins.then_inc(chain, 1)
                        dve.wait_ge(chain, c * STEPS + steps[0])

                    def low(b):
                        n = c * B + b
                        dve.wait_ge(hi_ready, n + 1)
                        V.tensor_tensor(hTl[:, b % 2, :, :],
                                        tp[b % 2][:, 0:256].rearrange("p (k n) -> p k n", k=KC)[:, :, 0:CH],
                                        f32(hT[:, b % 2, :, :]), ALU.subtract).then_inc(lo_ready, 1)

                    def bias(b):
                        n = c * B + b
                        dve.wait_ge(qkv_full, n + 1 + 2)
                        V.tensor_tensor(qk[:, b, 0:512], pq[b % 2][0:CH, 0, :], in_rows[0:CH, 0:512], ALU.add)
                        V.tensor_tensor(qk[:, b, 512:QKVB], pq[b % 2][0:CH, 1, 0:QKVB - 512],
                                        in_rows[0:CH, 512:QKVB], ALU.add).then_inc(qkv_read, 1)

                    normalise(0, c)
                    normalise(1, c)
                    low(0)
                    low(1)
                    for b in range(B):
                        bias(b)
                        if b + 2 < B:
                            normalise(b + 2, c)
                            low(b + 2)
                    dve.wait_ge(qkv_read, c * B + B + 2)
                    for t in (0, 1):
                        m = V.tensor_tensor(prod[:, t, :, :], qk[:, t, 0:C].unsqueeze(1).to_broadcast([CH, B, C]),
                                            qk[:, :, C:2 * C], ALU.mult)
                    step(m)
                    dve.wait_ge(qk_done, c + 1)
                    step(V.tensor_reduce(sc[:].rearrange("p t x -> p (t x)"),
                                         prod[:].rearrange("p t s (h e) -> p (t s h) e", e=HD), AX_X, ALU.add))
                    step(V.tensor_tensor(sc[:], sc[:], rel, ALU.add))
                    step(V.tensor_tensor(m2[:], sc[:, :, 0:2 * H], sc[:, :, 2 * H:4 * H], ALU.max))
                    step(V.tensor_tensor(m1[:], m2[:, :, 0:H], m2[:, :, H:2 * H], ALU.max))
                    V.tensor_tensor(sc[:].rearrange("p t (s h) -> p t s h", h=H),
                                    sc[:].rearrange("p t (s h) -> p t s h", h=H),
                                    m1[:].unsqueeze(2).to_broadcast([CH, B, B, H]), ALU.subtract).then_inc(shifted, 1)
                    dve.wait_ge(expd, c + 1)
                    step(V.tensor_tensor(m2[:], sc[:, :, 0:2 * H], sc[:, :, 2 * H:4 * H], ALU.add))
                    step(V.tensor_tensor(m1[:], m2[:, :, 0:H], m2[:, :, H:2 * H], ALU.add))
                    step(V.reciprocal(m1[:], m1[:]))
                    step(V.tensor_tensor(sc[:].rearrange("p t (s h) -> p t s h", h=H),
                                         sc[:].rearrange("p t (s h) -> p t s h", h=H),
                                         m1[:].unsqueeze(2).to_broadcast([CH, B, B, H]), ALU.mult))
                    for t in range(B):
                        for s in range(B):
                            m = V.tensor_tensor(prod[:, t, s, :].rearrange("p (h e) -> p h e", e=HD),
                                                sc[:, t, s * H:(s + 1) * H].unsqueeze(2).to_broadcast([CH, H, HD]),
                                                qk[:, s, 2 * C:3 * C].rearrange("p (h e) -> p h e", e=HD), ALU.mult)
                    step(m)
                    step(V.tensor_tensor(prod[:, :, 0:2, :], prod[:, :, 0:2, :], prod[:, :, 2:4, :], ALU.add))
                    V.tensor_tensor(ctx_t[:], prod[:, :, 0, :], prod[:, :, 1, :], ALU.add).then_inc(ctx_ready, 1)
                    for b in range(B):
                        n = c * B + b
                        t = b * NCH + c
                        hb = h0[:, bass.ds(t, 1), :].rearrange("p t f -> p (t f)")
                        dve.wait_ge(out_full, n + 1 + 2)
                        V.tensor_tensor(hs[:, b % 2, :], po[b % 2][0:CH, 0:C], out_row[0:CH, :],
                                        ALU.add).then_inc(h_half, 1)
                        dve.wait_ge(h_half, n + 1 + 2)
                        V.tensor_tensor(hb, hb, hs[:, b % 2, :], ALU.add).then_inc(h_done, 1)
                    while steps[0] < STEPS:
                        step(V.tensor_copy(m2[:, 0, 0:1], m1[:, 0, 0:1]))
                    assert steps[0] == STEPS

                dve.wait_ge(h_done, TILES)
                statistics(2)
                with dve.Fori(0, NCH) as c:
                    for b in range(B):
                        n = c * B + b
                        t = b * NCH + c
                        dve.wait_ge(t2, n - 1 + 2)
                        V.tensor_scalar(xn[:, b % 2, :], h0[:, bass.ds(t, 1), :].rearrange("p t f -> p (t f)"),
                                        stat[:, MEAN, bass.ds(t, 1)], stat[:, RSTD, bass.ds(t, 1)],
                                        ALU.subtract, ALU.mult).then_inc(x2_ready, 1)
                        dve.wait_ge(x2hi, n + 1)
                        V.tensor_tensor(hTl[:, b % 2, :, :],
                                        tp[b % 2][:, 0:256].rearrange("p (k n) -> p k n", k=KC)[:, :, 0:CH],
                                        f32(hT[:, b % 2, :, :]), ALU.subtract).then_inc(x2lo, 1)

                dve.wait_ge(lg_read, TILES + 2)
                link(V.tensor_tensor(choice[:], lg[:], gate_row[0:CH, :].unsqueeze(1).to_broadcast([CH, TILES, E]),
                                     ALU.add))
                for t in range(TILES):
                    for g_ in range(EGROUPS):
                        m = V.max(top[:, t, g_, :], choice[:, t, g_ * GE:(g_ + 1) * GE])
                link(m)
                link(V.tensor_tensor(gs[:], top[:, :, :, 0], top[:, :, :, 1], ALU.add))
                link(V.memset(rank[:], 0.0))
                for i in range(1, EGROUPS):
                    link(V.tensor_tensor(beat[:, :, 0:EGROUPS - i], gs[:, :, 0:EGROUPS - i], gs[:, :, i:EGROUPS],
                                         ALU.is_ge))
                    link(V.tensor_tensor(rank[:, :, i:EGROUPS], rank[:, :, i:EGROUPS], beat[:, :, 0:EGROUPS - i],
                                         ALU.add))
                    link(V.tensor_scalar(beat[:, :, 0:EGROUPS - i], beat[:, :, 0:EGROUPS - i], -1.0, 1.0,
                                         ALU.mult, ALU.add))
                    link(V.tensor_tensor(rank[:, :, 0:EGROUPS - i], rank[:, :, 0:EGROUPS - i],
                                         beat[:, :, 0:EGROUPS - i], ALU.add))
                link(V.tensor_scalar(beat[:], rank[:], KGROUPS - 0.5, None, ALU.is_lt))
                link(V.tensor_tensor(masked[:].rearrange("p t (g e) -> p (t g) e", e=GE),
                                     choice[:].rearrange("p t (g e) -> p (t g) e", e=GE),
                                     beat[:].rearrange("p t g -> p (t g)").unsqueeze(2).to_broadcast(
                                         [CH, TILES * EGROUPS, GE]), ALU.mult))
                for t in range(TILES):
                    m = V.max(top[:, t, 0, :], masked[:, t, :])
                link(m)
                for t in range(TILES):
                    m = V.match_replace(left[:, t, :], top[:, t, 0, :], masked[:, t, :], LOWEST)
                link(m)
                link(V.tensor_tensor(left[:], left[:], masked[:], ALU.not_equal))
                link(V.tensor_tensor(left[:], left[:], lg[:], ALU.mult))
                link(V.tensor_reduce(gsum[:, :, 0:1], left[:], AX_X, ALU.add))
                link(V.tensor_scalar(gsum[:, :, 0:1], gsum[:, :, 0:1], 1e-20, None, ALU.add))
                link(V.reciprocal(gsum[:, :, 1:2], gsum[:, :, 0:1]))
                link(V.tensor_tensor(left[:], left[:], gsum[:, :, 1:2].to_broadcast([CH, TILES, E]), ALU.mult))
                link(V.tensor_scalar(left[:], left[:], ROUTED_SCALING, None, ALU.mult))
                link(V.tensor_copy(whi_r[:], left[:]))
                link(V.tensor_copy(w64[:, :, 0:E], f32(whi_r[:])))
                V.tensor_tensor(w64[:, :, E:2 * E], left[:], f32(whi_r[:]), ALU.subtract).then_inc(routed, 1)


BLKP = 4 * CH
TP = B * NCH * CH
NB = TP // BLKP
WU = 3 * KC * INNER


def experts(nc, d, route, y, xh, xl, out):
    with ExitStack() as ctx:
        def sb(name, shape, dt=F32):
            return ctx.enter_context(nc.sbuf_tensor("e_" + name, shape, dt))

        def sem(name):
            return ctx.enter_context(nc.semaphore("e_" + name))

        stage = sb("stage", [128, 2, UNITS * WU])
        wh = sb("wh", [128, 2, UNITS * WU], F32R)
        wl = sb("wl", [128, 2, UNITS * WU], F32R)
        sel_in = sb("sel_in", [2 * E, E, 128])
        sel = sb("sel", [2 * E, E, 128], F32R)
        sg = sb("sg", [128, 2, BLKP])
        su = sb("su", [128, 2, BLKP])
        hv = sb("hv", [128, 2, BLKP])
        hh = sb("hh", [128, 2, BLKP], F32R)
        hl = sb("hl", [128, 2, BLKP], F32R)
        ps = [[ctx.enter_context(nc.psum_tensor(f"e_{n}{i}", [128, 512], F32)) for n in ("g", "u", "w")]
              for i in range(2)]
        ps_y = [ctx.enter_context(nc.psum_tensor(f"e_y{i}", [128, 512], F32)) for i in range(KC)]

        sel_loaded = sem("sel_loaded")
        sel_ready = sem("sel_ready")
        w_loaded = [sem("w_loaded0"), sem("w_loaded1")]
        w_high = sem("w_high")
        w_low = sem("w_low")
        up_full = sem("up_full")
        silu_done = sem("silu_done")
        mul_done = sem("mul_done")
        h_ready = sem("h_ready")
        high_done = sem("high_done")
        low_done = sem("low_done")
        down_done = sem("down_done")
        y_added = sem("y_added")
        stored = sem("stored")

        groups = [(2, None)] + [(UNITS, e) for e in range(0, E, UNITS)]
        base = [NB * sum(n for n, _ in groups[:i]) for i in range(len(groups) + 1)]
        G = len(groups)

        with nc.Block() as block:
            def yv(nb):
                return y[:].rearrange("p k t n -> p k (t n)")[:, :, bass.ds(nb * BLKP, BLKP)]

            @block.sync
            def _(sp):
                sp.dma_start(sel_in[:], d["sel"]).then_inc(sel_loaded, 16)
                for i, (n, _) in enumerate(groups):
                    if i >= 2:
                        sp.wait_ge(w_high, i - 1)
                        sp.wait_ge(w_low, i - 1)
                    sp.dma_start(stage[:, i % 2, 0:n * WU], d["w_exp"][i, :, 0:n * WU]).then_inc(w_loaded[i % 2], 16)
                with sp.Fori(0, NB) as nb:
                    sp.wait_ge(y_added, (G - 1) * NB + nb + 2)
                    sp.dma_start(out.rearrange("(k p) n -> p k n", k=KC)[:, :, bass.ds(nb * BLKP, BLKP)],
                                 yv(nb)).then_inc(stored, 16)
                sp.wait_ge(stored, NB * 16)

            def xv(x, k, nb):
                return x[:, k].rearrange("p t n -> p (t n)")[:, bass.ds(nb * BLKP, BLKP)]

            def weights(slot, u, kind, k):
                a = u * WU + kind * KC * INNER + k * INNER
                return wh[:, slot, a:a + INNER], wl[:, slot, a:a + INNER]

            @block.gpsimd
            def _(pool):
                for i, (n, _) in enumerate(groups):
                    pool.wait_ge(w_high, i + 1)
                    s = i % 2
                    nc.gpsimd.tensor_tensor(wl[:, s, 0:n * WU], stage[:, s, 0:n * WU], f32(wh[:, s, 0:n * WU]),
                                            ALU.subtract).then_inc(w_low, 1)

            @block.tensor
            def _(pe):
                def up(i, u, nb, n):
                    _, e0 = groups[i]
                    slot = u % 2
                    pe.wait_ge(h_ready, n - 1 + 2)
                    xs = [(xv(xh, k, nb), xv(xl, k, nb)) for k in range(KC)]
                    for kind in range(2):
                        m = split_matmul(nc, ps[slot][kind][:, 0:BLKP],
                                         [weights(i % 2, u, kind, k) for k in range(KC)], xs)
                    if e0 is not None:
                        m = nc.tensor.matmul(ps[slot][2][:, 0:BLKP], sel[:, e0 + u, :],
                                             route[:, bass.ds(nb * BLKP, BLKP)], start=True, stop=True)
                    m.then_inc(up_full, 1)

                def down(i, u, nb, n):
                    slot = u % 2
                    if u == 0:
                        pe.wait_ge(y_added, i * NB + nb + 1)
                    pe.wait_ge(low_done, n + 2)
                    last = u == groups[i][0] - 1
                    for k in range(KC):
                        m = split_matmul(nc, ps_y[k][:, 0:BLKP], [weights(i % 2, u, 2, k)],
                                         [(hh[:, slot, :], hl[:, slot, :])], first=u == 0, last=last)
                    m.then_inc(down_done, 1)

                pe.sem_inc(down_done, 2)
                pe.wait_ge(sel_ready, 1)
                pe.wait_ge(w_low, 1)
                for u in range(2):
                    up(0, u, 0, u)
                for i, (U, _) in enumerate(groups):
                    def block_of(nb, nxt):
                        for u in range(U):
                            n = nb * U + base[i] + u
                            if u + 2 < U:
                                up(i, u + 2, nb, n + 2)
                            elif nxt is None:
                                up(i, u + 2 - U, nb + 1, n + 2)
                            elif nxt < G:
                                if u == U - 2:
                                    pe.wait_ge(w_low, nxt + 1)
                                up(nxt, u + 2 - U, 0, n + 2)
                            down(i, u, nb, n)
                    with pe.Fori(0, NB - 1) as nb:
                        block_of(nb, None)
                    block_of(NB - 1, i + 1)

            @block.scalar
            def _(act):
                act.wait_ge(sel_loaded, 16)
                nc.scalar.activation(sel[:], sel_in[:], ACT.Copy).then_inc(sel_ready, 1)

                def split_weights(i):
                    n = groups[i][0]
                    act.wait_ge(w_loaded[i % 2], 16 * (i // 2 + 1))
                    if i >= 2:
                        act.wait_ge(down_done, base[i - 1] + 2)
                    nc.scalar.activation(wh[:, i % 2, 0:n * WU], stage[:, i % 2, 0:n * WU], ACT.Copy).then_inc(w_high, 1)

                def silu(slot, n):
                    act.wait_ge(up_full, n + 1)
                    nc.scalar.activation(sg[:, slot, :], ps[slot][0][:, 0:BLKP], ACT.Silu).then_inc(silu_done, 1)

                split_weights(0)
                split_weights(1)
                silu(0, 0)
                for i, (U, _) in enumerate(groups):
                    def block_of(nb, final):
                        for u in range(U):
                            n = nb * U + base[i] + u
                            if not (final and u == U - 1):
                                silu((u + 1) % 2, n + 1)
                            act.wait_ge(h_ready, n + 1 + 2)
                            act.wait_ge(down_done, n - 1 + 2)
                            nc.scalar.activation(hh[:, u % 2, :], hv[:, u % 2, :], ACT.Copy).then_inc(high_done, 1)
                    block_of(0, False)
                    if i >= 1 and i + 1 < G:
                        split_weights(i + 1)
                    with act.Fori(1, NB - 1) as nb:
                        block_of(nb, False)
                    block_of(NB - 1, i == G - 1)

            @block.vector
            def _(dve):
                V = nc.vector
                dve.sem_inc(h_ready, 2)
                dve.sem_inc(low_done, 1)
                dve.sem_inc(y_added, 1)

                def multiply(shared, slot, n, first=False):
                    dve.wait_ge(silu_done, n + 1)
                    if not first:
                        dve.wait_ge(low_done, n)
                    if shared:
                        V.tensor_tensor(hv[:, slot, :], sg[:, slot, :], ps[slot][1][:, 0:BLKP],
                                        ALU.mult).then_inc(h_ready, 1)
                        return
                    V.tensor_tensor(su[:, slot, :], sg[:, slot, :], ps[slot][1][:, 0:BLKP],
                                    ALU.mult).then_inc(mul_done, 1)
                    dve.wait_ge(mul_done, n + 1 - base[1])
                    V.tensor_tensor(hv[:, slot, :], su[:, slot, :], ps[slot][2][:, 0:BLKP],
                                    ALU.mult).then_inc(h_ready, 1)

                def add_y(i, nb, count):
                    dve.wait_ge(down_done, count + 2)
                    for k in range(KC):
                        part = y[:, k].rearrange("p t n -> p (t n)")[:, bass.ds(nb * BLKP, BLKP)]
                        m = V.tensor_tensor(part, part, ps_y[k][:, 0:BLKP], ALU.add)
                    m.then_inc(y_added, 1)

                multiply(True, 0, 0, first=True)
                for i, (U, e0) in enumerate(groups):
                    def block_of(nb, end):
                        for u in range(U):
                            n = nb * U + base[i] + u
                            if u < U - 1 or not end:
                                multiply(e0 is None, (u + 1) % 2, n + 1)
                            elif i + 1 < G:
                                multiply(False, (u + 1) % 2, n + 1)
                            dve.wait_ge(high_done, n + 1)
                            V.tensor_tensor(hl[:, u % 2, :], hv[:, u % 2, :], f32(hh[:, u % 2, :]),
                                            ALU.subtract).then_inc(low_done, 1)
                        add_y(i, nb, nb * U + base[i] + U)
                    with dve.Fori(0, NB - 1) as nb:
                        block_of(nb, False)
                    block_of(NB - 1, True)


def build(nc, d, out):
    with ExitStack() as ctx:
        def sb(name, shape, dt=F32):
            return ctx.enter_context(nc.sbuf_tensor(name, shape, dt))
        h0 = sb("h0", [CH, TILES, C])
        token_attention(nc, d, h0)
        route = sb("route", [2 * E, TP], F32R)
        y = sb("y", [128, KC, TILES, CH])
        xh = sb("xh", [128, KC, TILES, CH], F32R)
        xl = sb("xl", [128, KC, TILES, CH], F32R)
        relative_attention(nc, d, h0, route, y, xh, xl)
        experts(nc, d, route, y, xh, xl, out)


def kernel(**inputs):
    import numpy as _np
    import concourse.bacc as _bacc
    from concourse import mybir as _mybir
    from concourse.bass_utils import run_bass_kernel_spmd as _run

    v = {k: _np.asarray(a) for k, a in inputs.items()}
    f = _np.float32
    dt = v["x"].dtype

    def fold(a):
        return a.reshape(KC, 128, -1).transpose(1, 0, 2)

    def col(a):
        return a.reshape(KC, 128).T

    def row(a):
        return _np.broadcast_to(a, (128, a.shape[0]))

    a = {}
    xt = v["x"].transpose(2, 0, 1)
    xt = _np.concatenate([xt, xt[:, :, 0:LP - N]], axis=2)
    a["xt"] = xt.reshape(KC, 128, B, LP).transpose(1, 0, 2, 3)
    wqkv, bqkv = v["L0_tok_W_qkv"], v["L0_tok_b_qkv"]
    wqk = _np.zeros((C, 2, PAIRS, 2, 4, HD), dt)
    bqk = _np.zeros((2, PAIRS, 2, 4, HD), dt)
    for s in range(3):
        wqk[:, :, :, :, s] = wqkv[:, 0:2 * C].reshape(C, 2, PAIRS, 2, HD)
        bqk[:, :, :, s] = bqkv[0:2 * C].reshape(2, PAIRS, 2, HD)
    low = (2, 1)
    mbqk = _np.zeros_like(bqk)
    mask = _np.zeros((2, 4, HD, 2), dt)
    for i in range(2):
        mbqk[i, :, :, low[i]] = bqk[i, :, :, low[i]]
        mask[:, low[i], :, i] = 1
    bqk[1, :, :, 3] = 1
    a["w_qk"] = fold(wqk.reshape(C, -1)).reshape(128, KC, 2, PAIRS * 128)
    a["w_v"] = fold(wqkv[:, 2 * C:])
    a["w_proj"] = fold(v["L0_tok_W_proj"])
    wc = _np.zeros((GROUPS, 4, 2, HD, C), dt)
    wc[:, :, 0] = v["L0_tok_W_proj"].reshape(GROUPS, 4, HD, C)
    a["w_ctx"] = wc.reshape(GROUPS, 128, C).transpose(1, 0, 2)
    cols = _np.zeros((128, 64), dt)
    cols[:, 0:16] = bqk.reshape(16, 128).T
    cols[:, 16:32] = mbqk.reshape(16, 128).T
    cols[:, 32:34] = mask.reshape(128, 2)
    cols[:, 34:36] = col(v["L0_tok_b_proj"])
    cols[:, 36:38] = col(v["L0_tok_ln_g"])
    cols[:, 38:40] = col(v["L0_tok_ln_b"])
    cols[:, 40:42] = col(v["L0_tok_general_token"].reshape(C))
    a["cols"] = cols
    a["rows"] = _np.stack([row(bqkv[2 * C:]), row(v["L0_tok_b_proj"])], axis=1)
    a["ident"] = _np.eye(128, dtype=f)
    sums = _np.zeros((4, 2 * HD, 4, 2 * HD), f)
    for j in range(4):
        sums[j, HD, j, :] = 1
    a["sum_rows"] = sums.reshape(128, 128)
    a["mean_all"] = _np.full((128, 128), 1.0 / C, f)

    w_in = v["L0_attn_in_proj_weight"]
    b_in = v["L0_attn_in_proj_bias"]
    a["w_in"] = fold(w_in.T)
    a["w_q"] = fold(w_in[0:C])
    a["w_pos"] = fold(v["L0_attn_pos_proj_weight"].T)
    a["w_out"] = fold(v["L0_attn_out_proj_weight"].T)
    a["w_gate"] = fold(v["L0_ffn_gate_w"].T)
    a["pos"] = fold(v["L0_attn_pos"][0:REL, 0].T)
    own = _np.zeros((H, HD, REL, H), f)
    for h in range(H):
        own[h, :, :, h] = 1
    a["own"] = fold(own.reshape(C, REL * H))
    small = _np.zeros((128, 16), dt)
    small[:, 0:2] = col(v["L0_attn_pos_proj_bias"])
    small[:, 2:4] = col(b_in[0:C])
    small[:, 4:6] = col(v["L0_attn_r_r_bias"].reshape(C))
    a["small"] = small
    a["in_rows"] = row(b_in)
    a["rw_row"] = row(v["L0_attn_r_w_bias"].reshape(C))
    a["out_row"] = row(v["L0_attn_out_proj_bias"])
    a["gate_row"] = row(v["L0_ffn_gate_bias"])

    def unit(wg, wu, wd):
        return _np.concatenate([fold(wg.T).reshape(128, -1), fold(wu.T).reshape(128, -1), wd.T], axis=1)

    units = [unit(v["L0_ffn_shared_gate"][i:i + INNER], v["L0_ffn_shared_up"][i:i + INNER],
                  v["L0_ffn_shared_down"][:, i:i + INNER]) for i in (0, INNER)]
    units += [_np.zeros_like(units[0])] * (UNITS - 2)
    units += [unit(v["L0_ffn_expert_gate"][e], v["L0_ffn_expert_up"][e], v["L0_ffn_expert_down"][e])
              for e in range(E)]
    a["w_exp"] = _np.stack(units).reshape(-1, UNITS, 128, WU).transpose(0, 2, 1, 3).reshape(-1, 128, UNITS * WU)
    sel = _np.zeros((2, E, E, 128), f)
    for e in range(E):
        sel[:, e, e] = 1
    a["sel"] = sel.reshape(2 * E, E, 128)

    nc = _bacc.Bacc("TRN2", target_bir_lowering=False, num_devices=1)
    arrays, d = {}, {}
    for name, arr in a.items():
        arr = _np.ascontiguousarray(arr)
        arrays[f"in_{name}"] = arr
        d[name] = nc.dram_tensor(f"in_{name}", arr.shape, _mybir.dt.from_np(arr.dtype), kind="ExternalInput").ap()
    out = nc.dram_tensor("out", (C, TP), F32, kind="ExternalOutput").ap()
    build(nc, d, out)
    r = _run(nc, [arrays], core_ids=[0])
    res = r.results[0]["out"].reshape(C, B, NCH * CH)[:, :, 0:L]
    return _np.ascontiguousarray(res.transpose(1, 2, 0))
```

```python
from contextlib import ExitStack

import numpy as np

import concourse.bass as bass
from concourse import mybir

F32 = mybir.dt.float32
F32R = mybir.dt.float32r
ALU = mybir.AluOpType
ACT = mybir.ActivationFunctionType
AX_X = mybir.AxisListType.X

B, N, C, H = 4, 512, 256, 16
HD = C // H
L = N + 1
LP = 516
HALF = LP // 2
KC = C // 128
SCALE = float(HD) ** -0.5
EPS = 1e-5
NCH = 5
CH = 103
QSIZE = [CH] * 4 + [LP - 4 * CH]
KSIZE = [CH] * 4 + [L - 4 * CH]
PAIRS = H // 2
GROUPS = H // 4
TILES = B * NCH
T = B * L
REL = 2 * B - 1
QKVB = 3 * C + REL * H
E, GE, TOPK, EGROUPS, KGROUPS = 32, 8, 8, 4, 2
ROUTED_SCALING = 2.5
INNER = 128
UNITS = 4
TURNS = [(0, 2), (2, 3), (3, 4), (4, 5)]
LOWEST = -3.0e38
RING = 6


def f32(ap):
    return ap.bitcast(F32)


def split_matmul(nc, out, left, right, first=True, last=True):
    terms = [(l, r) for l, r in zip(left, right)]
    n = 3 * len(terms)
    i = 0
    for (lh, ll), (rh, rl) in terms:
        for a, b in ((lh, rh), (lh, rl), (ll, rh)):
            m = nc.tensor.matmul(out, a, b, start=first and i == 0, stop=last and i == n - 1)
            i += 1
    return m


def token_attention(nc, d, h0):
    with ExitStack() as ctx:
        def sb(name, shape, dt=F32):
            return ctx.enter_context(nc.sbuf_tensor("a_" + name, shape, dt))

        def sem(name):
            return ctx.enter_context(nc.semaphore("a_" + name))

        x = sb("x", [128, KC, B, LP])
        w_qk = sb("w_qk", [128, KC, 2, PAIRS * 128])
        w_v = sb("w_v", [128, KC, C])
        w_proj = sb("w_proj", [128, KC, C])
        cols = sb("cols", [128, 64])
        rows = sb("rows", [128, 2, C])
        ident = sb("ident", [128, 128])
        mean_all = sb("mean_all", [128, 128])
        B_QK, CB_QK, MASK, B_P, LN_G, LN_B, GT = 0, 16, 32, 34, 36, 38, 40

        whi = sb("whi", [128, KC, 2, PAIRS * 128], F32R)
        wlo = sb("wlo", [128, KC, 2, PAIRS * 128], F32R)
        vhi = sb("vhi", [128, KC, C], F32R)
        vlo = sb("vlo", [128, KC, C], F32R)
        xhi = sb("xhi", [128, KC, LP], F32R)
        xlo = sb("xlo", [128, KC, LP], F32R)
        q_op = sb("q_op", [128, PAIRS, LP], F32R)
        k_op = sb("k_op", [128, 2, PAIRS, LP], F32R)
        part = sb("part", [128, 6, HALF], F32R)
        vaug = sb("vaug", [CH, NCH, H, 2 * HD])
        mx = sb("mx", [128, 4, NCH, 2])
        mx1 = sb("mx1", [128, 4, NCH])
        negm = sb("negm", [128, 4, NCH])
        mcols = sb("mcols", [128, 2, NCH, 128])
        probs = sb("probs", [CH, 8, LP])
        osb = sb("osb", [128, LP])
        rsum = sb("rsum", [CH, NCH, 4])
        ctok = sb("ctok", [CH, NCH, C])
        ctxt = sb("ctxt", [128, NCH, KC, CH])
        g = sb("g", [128, 32])

        ring = [ctx.enter_context(nc.psum_tensor(f"a_ring{i}", [128, 512], F32)) for i in range(RING)]
        ps_o = ctx.enter_context(nc.psum_tensor("a_ps_o", [128, 2, 512], F32))

        loaded = sem("loaded")
        gt_pe = sem("gt_pe")
        gt_dve = sem("gt_dve")
        gt_act = sem("gt_act")
        w_high = sem("w_high")
        w_low = sem("w_low")
        x_high = sem("x_high")
        x_low = sem("x_low")
        filled = [sem(f"filled{i}") for i in range(RING)]
        freed = [sem(f"freed{i}") for i in range(RING)]
        part_ready = sem("part_ready")
        gt_x = sem("gt_x")
        zero_mx = sem("zero_mx")
        max_done = sem("max_done")
        k_zeroed = sem("k_zeroed")
        neg_done = sem("neg_done")
        high_done = sem("high_done")
        mcols_ready = sem("mcols_ready")
        o_full = sem("o_full")
        o_copied = sem("o_copied")
        ctx_ready = sem("ctx_ready")
        recip_done = sem("recip_done")
        zeroed = sem("zeroed")

        def halves(kind, s, n):
            return [(kind, s, i, h) for i in n for h in range(2)]

        PRO = halves("P", 0, range(4)) + halves("M", 0, range(20)) + halves("N", 0, range(2))
        order = []
        for s in range(1, 5):
            if s == 1:
                order += [("V", s, i, 0) for i in range(NCH)]
            order += halves("P", s, (2, 3)) + halves("X", s, range(2))
            for i in range(20):
                order += halves("T", s, (i,)) + halves("M", s, (i,))
            order += halves("P", s, (0, 1)) + halves("S", s, (0,))
            if s == 4:
                order += [("C", s, i, 0) for i in range(len(TURNS))] + [("O", s, i, 0) for i in range(NCH)]
        tail = [t for t in order if not (
            (t[0] == "P" and (t[1] == 4 or (t[1] == 3 and t[2] < 2))) or (t[0] == "M" and t[1] == 4))]
        assert len(order) % RING == 0
        START = len(PRO)
        BODY = len(order) // RING
        at_pro = {t: i for i, t in enumerate(PRO)}
        at_body = {t: START + i for i, t in enumerate(order)}
        at_tail = {t: START + i for i, t in enumerate(tail)}

        class Use:

            def __init__(self, u, b=0):
                self.slot = u % RING
                self.tile = ring[self.slot]
                self.n = u // RING + b * BODY

        def use(kind, s, i, half, b, last):
            return Use((at_tail if last else at_body)[kind, s, i, half], b)

        def pro(kind, i, half):
            return Use(at_pro[kind, 0, i, half])

        def consumed(eng, u):
            eng.wait_ge(freed[u.slot], u.n + 1)

        def fill_wait(pe, u):
            if not (isinstance(u.n, int) and u.n == 0):
                pe.wait_ge(freed[u.slot], u.n)

        def span(half):
            return slice(half * HALF, half * HALF + HALF)

        with nc.Block() as block:
            @block.sync
            def _(sp):
                for dst, src in ((x, d["xt"]), (w_proj, d["w_proj"]), (cols, d["cols"]), (rows, d["rows"]),
                                 (ident, d["ident"]), (mean_all, d["mean_all"]),
                                 (w_qk, d["w_qk"]), (w_v, d["w_v"])):
                    sp.dma_start(dst[:], src).then_inc(loaded, 16)

            LOADED = 128

            @block.gpsimd
            def _(pool):
                nc.gpsimd.memset(f32(k_op[64:128, 0]), 0.0).then_inc(k_zeroed, 1)
                pool.wait_ge(k_zeroed, 1)
                nc.gpsimd.memset(f32(k_op[0:64, 1]), 0.0).then_inc(k_zeroed, 1)
                pool.wait_ge(k_zeroed, 2)
                nc.gpsimd.memset(mcols[:], 0.0).then_inc(zeroed, 1)
                nc.gpsimd.memset(vaug[:], 1.0).then_inc(zeroed, 1)

            @block.tensor
            def _(pe):
                gp = ps_o[:, 0, :]
                pe.wait_ge(loaded, LOADED)
                for j in range(KC):
                    for k in range(KC):
                        m = nc.tensor.matmul(gp[:, j:j + 1], w_proj[:, k, 128 * j:128 * j + 128],
                                             cols[:, GT + k:GT + k + 1], start=k == 0, stop=k == KC - 1)
                m.then_inc(gt_pe, 1)
                pe.wait_ge(gt_dve, 1)
                for k in range(KC):
                    m = nc.tensor.matmul(gp[:, 2:3], mean_all[:], g[:, k:k + 1], start=k == 0, stop=k == KC - 1)
                m.then_inc(gt_pe, 1)
                pe.wait_ge(gt_dve, 3)
                for k in range(KC):
                    m = nc.tensor.matmul(gp[:, 3:4], mean_all[:], g[:, 4 + k:5 + k], start=k == 0, stop=k == KC - 1)
                m.then_inc(gt_pe, 1)

                def project(u, pair, qk, half):
                    fill_wait(pe, u)
                    c0 = pair * 128
                    split_matmul(nc, u.tile[:, 0:HALF],
                                 [(whi[:, k, qk, c0:c0 + 128], wlo[:, k, qk, c0:c0 + 128]) for k in range(KC)],
                                 [(xhi[:, k, span(half)], xlo[:, k, span(half)])
                                  for k in range(KC)]).then_inc(filled[u.slot], 1)

                def values(u, c):
                    fill_wait(pe, u)
                    ks = slice(c * CH, c * CH + KSIZE[c])
                    split_matmul(nc, u.tile[0:KSIZE[c], 0:C],
                                 [(xhi[:, k, ks], xlo[:, k, ks]) for k in range(KC)],
                                 [(vhi[:, k, :], vlo[:, k, :]) for k in range(KC)]).then_inc(filled[u.slot], 1)

                def head(grp, j):
                    return j % 2, 2 * grp + j // 2

                def row_scores(u, grp, i, half):
                    fill_wait(pe, u)
                    e, pair = head(grp, i % 4)
                    c = i // 4
                    nc.tensor.matmul(u.tile[0:QSIZE[c], 0:HALF], q_op[:, pair, c * CH:c * CH + QSIZE[c]],
                                     k_op[:, e, pair, span(half)], start=True, stop=True).then_inc(filled[u.slot], 1)

                def turn_max(u, pl, half):
                    fill_wait(pe, u)
                    for c in range(NCH):
                        lo, hi = c * CH, c * CH + QSIZE[c]
                        a, z = max(lo, half * HALF), min(hi, half * HALF + HALF)
                        if a < z:
                            m = nc.tensor.matmul(u.tile[:, a - half * HALF:z - half * HALF],
                                                 mcols[0:QSIZE[c], pl, c, :], ident[0:QSIZE[c], a - lo:z - lo],
                                                 start=True, stop=True)
                    m.then_inc(filled[u.slot], 1)

                def key_scores(u, grp, i, half):
                    fill_wait(pe, u)
                    e, pair = head(grp, i % 4)
                    c = i // 4
                    nc.tensor.matmul(u.tile[0:KSIZE[c], 0:HALF], k_op[:, e, pair, c * CH:c * CH + KSIZE[c]],
                                     q_op[:, pair, span(half)], start=True, stop=True).then_inc(filled[u.slot], 1)

                def weigh_values(grp, c, b, s, last):
                    for half in range(2):
                        for j in range(4):
                            consumed(pe, use("T", s, 4 * c + j, half, b, last))
                            m = nc.tensor.matmul(ps_o[32 * j:32 * j + 32, half, 0:HALF],
                                                 vaug[0:KSIZE[c], c, 4 * grp + j, :],
                                                 probs[0:KSIZE[c], (4 * c + j) % 8, span(half)],
                                                 start=c == 0, stop=c == NCH - 1)
                    return m

                pe.wait_ge(w_high, 2)
                pe.wait_ge(w_low, 2)
                pe.wait_ge(x_high, 1)
                pe.wait_ge(x_low, 1)
                for i in range(4):
                    for half in range(2):
                        project(pro("P", i, half), i // 2, i % 2, half)
                for i in range(4):
                    for half in range(2):
                        consumed(pe, pro("P", i, half))
                pe.wait_ge(k_zeroed, 2)
                for i in range(20):
                    for half in range(2):
                        row_scores(pro("M", i, half), 0, i, half)
                for i in range(2):
                    for half in range(2):
                        project(pro("N", i, half), 2, i, half)

                def batch(b, last):
                    for s in range(1, 5):
                        grp = s - 1
                        ahead = not (last and s == 4)
                        if s == 1:
                            for i in range(NCH):
                                values(use("V", s, i, 0, b, last), i)
                        if ahead:
                            for i in (2, 3):
                                for half in range(2):
                                    project(use("P", s, i, half, b, last), 2 * (s % 4) + 1, i % 2, half)
                        pe.wait_ge(mcols_ready, b * 4 + s)
                        for i in range(2):
                            for half in range(2):
                                turn_max(use("X", s, i, half, b, last), i, half)
                        for i in range(2):
                            for half in range(2):
                                consumed(pe, use("X", s, i, half, b, last))
                        if s == 1:
                            for i in range(NCH):
                                consumed(pe, use("V", s, i, 0, b, last))
                        for i in range(20):
                            for half in range(2):
                                key_scores(use("T", s, i, half, b, last), grp, i, half)
                            if i % 4 == 3 and i >= 7:
                                if i == 7:
                                    pe.wait_ge(o_copied, b * 4 + s)
                                weigh_values(grp, i // 4 - 1, b, s, last)
                            if ahead:
                                for half in range(2):
                                    if i == 0:
                                        for k in (2, 3):
                                            consumed(pe, use("P", s, k, half, b, last))
                                    row_scores(use("M", s, i, half, b, last), s % 4, i, half)
                        weigh_values(grp, NCH - 1, b, s, last).then_inc(o_full, 1)
                        if ahead and not (last and s == 3):
                            if s == 3:
                                pe.wait_ge(x_high, b + 2)
                                pe.wait_ge(x_low, b + 2)
                            for i in range(2):
                                for half in range(2):
                                    project(use("P", s, i, half, b, last), 2 * ((s + 1) % 4), i, half)
                        pe.wait_ge(o_copied, b * 4 + s + 1)
                        for half, (c0, c1) in enumerate(((0, 4), (4, NCH))):
                            u = use("S", s, 0, half, b, last)
                            fill_wait(pe, u)
                            for c in range(c0, c1):
                                at = (c - c0) * 128
                                m = nc.tensor.transpose(u.tile[0:CH, at:at + 128], osb[:, c * CH:c * CH + CH], ident[:])
                            m.then_inc(filled[u.slot], 1)
                    pe.wait_ge(ctx_ready, b * 4 + 5)
                    for i, (c0, c1) in enumerate(TURNS):
                        u = use("C", 4, i, 0, b, last)
                        fill_wait(pe, u)
                        for c in range(c0, c1):
                            for k in range(KC):
                                at = ((c - c0) * KC + k) * 128
                                m = nc.tensor.transpose(u.tile[:, at:at + CH], ctok[:, c, k * 128:k * 128 + 128],
                                                        ident[0:CH, 0:CH])
                        m.then_inc(filled[u.slot], 1)
                    for i, (c0, c1) in enumerate(TURNS):
                        consumed(pe, use("C", 4, i, 0, b, last))
                        for c in range(c0, c1):
                            u = use("O", 4, c, 0, b, last)
                            fill_wait(pe, u)
                            for k in range(KC):
                                m = nc.tensor.matmul(u.tile[0:CH, 0:C], ctxt[:, c, k, :], w_proj[:, k, :],
                                                     start=k == 0, stop=k == KC - 1)
                            m.then_inc(filled[u.slot], 1)

                with pe.Fori(0, B - 1) as b:
                    batch(b, False)
                batch(B - 1, True)

            @block.scalar
            def _(act):
                act.sem_inc(o_copied, 1)
                act.wait_ge(loaded, LOADED)
                nc.scalar.activation(whi[:], w_qk[:], ACT.Copy).then_inc(w_high, 1)
                nc.scalar.activation(vhi[:], w_v[:], ACT.Copy).then_inc(w_high, 1)
                act.wait_ge(gt_dve, 4)
                nc.scalar.activation(g[:, 8:9], g[:, 7:8], ACT.Sqrt).then_inc(gt_act, 1)

                def split_x(b):
                    nc.scalar.activation(xhi[:], x[:, :, bass.ds(b, 1), :].rearrange("p k b n -> p k (b n)"),
                                         ACT.Copy).then_inc(x_high, 1)

                def high_part(u, pair, qk):
                    act.wait_ge(filled[u.slot], u.n + 1)
                    cb = CB_QK + qk * PAIRS + pair
                    nc.scalar.activation(part[:, u.slot, :], u.tile[:, 0:HALF],
                                         ACT.Identity, bias=cols[:, cb:cb + 1],
                                         scale=cols[:, MASK + qk:MASK + qk + 1]).then_inc(part_ready, 1)

                act.wait_ge(gt_dve, 10)
                split_x(0)
                for i in range(4):
                    for half in range(2):
                        high_part(pro("P", i, half), i // 2, i % 2)
                for i in range(2):
                    for half in range(2):
                        high_part(pro("N", i, half), 2, i)

                def batch(b, last):
                    for s in range(1, 5):
                        if not (last and s == 4):
                            for i in (2, 3):
                                for half in range(2):
                                    high_part(use("P", s, i, half, b, last), 2 * (s % 4) + 1, i % 2)
                        if s == 3 and not last:
                            split_x(b + 1)
                        for i in range(20):
                            sz = KSIZE[i // 4]
                            for half in range(2):
                                u = use("T", s, i, half, b, last)
                                act.wait_ge(filled[u.slot], u.n + 1)
                                nc.scalar.activation(probs[0:sz, i % 8, span(half)], u.tile[0:sz, 0:HALF], ACT.Exp,
                                                     scale=SCALE).then_inc(freed[u.slot], 1)
                        act.wait_ge(o_full, b * 4 + s)
                        act.wait_ge(ctx_ready, b * 4 + s)
                        nc.scalar.activation(osb[:].rearrange("p (h n) -> p h n", h=2), ps_o[:, :, 0:HALF],
                                             ACT.Copy).then_inc(o_copied, 1)
                        if not last or s < 3:
                            for i in range(2):
                                for half in range(2):
                                    high_part(use("P", s, i, half, b, last), 2 * ((s + 1) % 4), i)
                    for i, (c0, c1) in enumerate(TURNS):
                        u = use("C", 4, i, 0, b, last)
                        act.wait_ge(filled[u.slot], u.n + 1)
                        nc.scalar.activation(ctxt[:, c0:c1].rearrange("p c k n -> p (c k) n"),
                                             u.tile[:].rearrange("p (c n) -> p c n", n=128)[:, 0:(c1 - c0) * KC, 0:CH],
                                             ACT.Copy).then_inc(freed[u.slot], 1)

                with act.Fori(0, B - 1) as b:
                    batch(b, False)
                batch(B - 1, True)

            @block.vector
            def _(dve):
                gp = ps_o[:, 0, :]

                def c_(i, n=1):
                    return cols[:, i:i + n]

                dve.sem_inc(ctx_ready, 1)
                dve.wait_ge(gt_pe, 1)
                nc.vector.tensor_tensor(g[:, 0:2], gp[:, 0:2], c_(B_P, 2), ALU.add).then_inc(gt_dve, 1)
                dve.wait_ge(gt_pe, 2)
                dve.wait_ge(gt_dve, 1)
                nc.vector.tensor_scalar(g[:, 2:4], g[:, 0:2], gp[:, 2:3], None, ALU.subtract).then_inc(gt_dve, 1)
                dve.wait_ge(gt_dve, 2)
                nc.vector.tensor_tensor(g[:, 4:6], g[:, 2:4], g[:, 2:4], ALU.mult).then_inc(gt_dve, 1)
                dve.wait_ge(gt_pe, 3)
                nc.vector.tensor_scalar(g[:, 7:8], gp[:, 3:4], EPS, None, ALU.add).then_inc(gt_dve, 1)
                dve.wait_ge(gt_act, 1)
                nc.vector.reciprocal(g[:, 9:10], g[:, 8:9]).then_inc(gt_dve, 1)
                dve.wait_ge(gt_dve, 5)
                nc.vector.scalar_tensor_tensor(g[:, 10:11], g[:, 9:10], g[:, 9:10], g[:, 7:8], ALU.mult,
                                               ALU.mult).then_inc(gt_dve, 1)
                dve.wait_ge(gt_dve, 6)
                nc.vector.tensor_scalar(g[:, 11:12], g[:, 10:11], -0.5, 1.5, ALU.mult, ALU.add).then_inc(gt_dve, 1)
                dve.wait_ge(gt_dve, 7)
                nc.vector.tensor_scalar(g[:, 12:14], g[:, 2:4], g[:, 9:10], g[:, 11:12], ALU.mult,
                                        ALU.mult).then_inc(gt_dve, 1)
                dve.wait_ge(gt_dve, 8)
                nc.vector.tensor_tensor(g[:, 14:16], g[:, 12:14], c_(LN_G, 2), ALU.mult).then_inc(gt_dve, 1)
                dve.wait_ge(gt_dve, 9)
                nc.vector.tensor_tensor(g[:, 16:18], g[:, 14:16], c_(LN_B, 2), ALU.add).then_inc(gt_x, 1)
                dve.wait_ge(gt_x, 1)
                for k in range(KC):
                    m = nc.vector.tensor_scalar(x[:, k, :, N], ident[:, 0:B], 0.0, g[:, 16 + k:17 + k],
                                                ALU.mult, ALU.add)
                m.then_inc(gt_dve, 1)
                dve.wait_ge(w_high, 2)
                nc.vector.tensor_tensor(wlo[:], w_qk[:], f32(whi[:]), ALU.subtract).then_inc(w_low, 1)
                nc.vector.tensor_tensor(vlo[:], w_v[:], f32(vhi[:]), ALU.subtract).then_inc(w_low, 1)

                def split_x(b):
                    dve.wait_ge(x_high, b + 1)
                    nc.vector.tensor_tensor(xlo[:], x[:, :, bass.ds(b, 1), :].rearrange("p k b n -> p k (b n)"),
                                            f32(xhi[:]), ALU.subtract).then_inc(x_low, 1)

                def operand(u, pair, qk, half, n):
                    dve.wait_ge(part_ready, n + 1)
                    cb = B_QK + qk * PAIRS + pair
                    parts = [(q_op[:, pair, span(half)], 0, 128)] if qk == 0 else \
                        [(k_op[64 * e:64 * e + 64, e, pair, span(half)], 64 * e, 64 * e + 64) for e in range(2)]
                    for dst, lo, hi in parts:
                        m = nc.vector.scalar_tensor_tensor(dst, u.tile[lo:hi, 0:HALF], cols[lo:hi, cb:cb + 1],
                                                           f32(part[lo:hi, u.slot, :]), ALU.add, ALU.subtract)
                    m.then_inc(freed[u.slot], 1)

                def maxima(u, i, half):
                    sz = QSIZE[i // 4]
                    dve.wait_ge(filled[u.slot], u.n + 1)
                    nc.vector.tensor_reduce(mx[0:sz, i % 4, i // 4, half:half + 1], u.tile[0:sz, 0:HALF],
                                            AX_X, ALU.max).then_inc(freed[u.slot], 1)
                    if i == 19 and half:
                        consumed(dve, u)

                def negate(n):
                    nc.vector.tensor_tensor(mx1[:], mx[:, :, :, 0], mx[:, :, :, 1], ALU.max).then_inc(max_done, 1)
                    dve.wait_ge(max_done, n + 1)
                    nc.vector.tensor_scalar(negm[:], mx1[:], -1.0, None, ALU.mult).then_inc(neg_done, 1)
                    dve.wait_ge(neg_done, n + 1)
                    cols_of = mcols[:].rearrange("p l c (e r) -> p l e c r", e=2)
                    neg4 = negm[:].rearrange("p (l e) c -> p l e c", l=2)
                    nc.vector.tensor_copy(cols_of[:, :, :, :, 48].bitcast(F32R), neg4).then_inc(high_done, 1)
                    dve.wait_ge(high_done, n + 1)
                    nc.vector.tensor_tensor(cols_of[:, :, :, :, 49], neg4, cols_of[:, :, :, :, 48],
                                            ALU.subtract).then_inc(mcols_ready, 1)

                nc.vector.memset(mx[:], 0.0).then_inc(zero_mx, 1)
                split_x(0)
                for i in range(4):
                    for half in range(2):
                        operand(pro("P", i, half), i // 2, i % 2, half, 2 * i + half)
                dve.wait_ge(zero_mx, 1)
                for i in range(20):
                    for half in range(2):
                        maxima(pro("M", i, half), i, half)
                dve.wait_ge(zeroed, 2)
                negate(0)
                for i in range(2):
                    for half in range(2):
                        operand(pro("N", i, half), 2, i, half, 8 + 2 * i + half)

                def batch(b, last):
                    for s in range(1, 5):
                        ahead = not (last and s == 4)
                        if s == 1:
                            for c in range(NCH):
                                u = use("V", s, c, 0, b, last)
                                dve.wait_ge(filled[u.slot], u.n + 1)
                                nc.vector.tensor_tensor(
                                    vaug[0:KSIZE[c], c, :, 0:HD],
                                    u.tile[0:KSIZE[c], 0:C].rearrange("p (h d) -> p h d", h=H),
                                    rows[0:KSIZE[c], 0, :].rearrange("p (h d) -> p h d", h=H),
                                    ALU.add).then_inc(freed[u.slot], 1)
                        if ahead:
                            for i in (2, 3):
                                for half in range(2):
                                    operand(use("P", s, i, half, b, last), 2 * (s % 4) + 1, i % 2, half,
                                            b * 32 + 8 * s + 2 * i + half)
                        for i in range(2):
                            for half in range(2):
                                u = use("X", s, i, half, b, last)
                                dve.wait_ge(filled[u.slot], u.n + 1)
                                q = q_op[:, 2 * (s - 1) + i, span(half)]
                                nc.vector.tensor_tensor(q, f32(q), u.tile[:, 0:HALF], ALU.add).then_inc(freed[u.slot], 1)
                        if s == 3 and not last:
                            split_x(b + 1)
                        if ahead:
                            for i in range(20):
                                for half in range(2):
                                    maxima(use("M", s, i, half, b, last), i, half)
                            negate(b * 4 + s)
                        if ahead and not (last and s == 3):
                            for i in range(2):
                                for half in range(2):
                                    operand(use("P", s, i, half, b, last), 2 * ((s + 1) % 4), i, half,
                                            b * 32 + 8 * s + 8 + 2 * i + half)
                        for half, (c0, c1) in enumerate(((0, 4), (4, NCH))):
                            u = use("S", s, 0, half, b, last)
                            dve.wait_ge(filled[u.slot], u.n + 1)
                            heads = u.tile[:].rearrange("p (c j x) -> p c j x", c=4, j=4)[0:CH, 0:c1 - c0]
                            nc.vector.reciprocal(rsum[:, c0:c1], heads[:, :, :, HD]).then_inc(recip_done, 1)
                            dve.wait_ge(recip_done, b * 8 + 2 * s + half - 1)
                            nc.vector.tensor_tensor(
                                ctok[:, c0:c1, 64 * (s - 1):64 * s].rearrange("p c (j x) -> p c j x", j=4),
                                heads[:, :, :, 0:HD], rsum[:, c0:c1].unsqueeze(3).to_broadcast([CH, c1 - c0, 4, HD]),
                                ALU.mult).then_inc(freed[u.slot], 1)
                            consumed(dve, u)
                        dve.sem_inc(ctx_ready, 1)
                    for c in range(NCH):
                        u = use("O", 4, c, 0, b, last)
                        dve.wait_ge(filled[u.slot], u.n + 1)
                        nc.vector.tensor_tensor(h0[:, bass.ds(b * NCH + c, 1), :].rearrange("p t f -> p (t f)"),
                                                u.tile[0:CH, 0:C], rows[0:CH, 1, :],
                                                ALU.add).then_inc(freed[u.slot], 1)

                with dve.Fori(0, B - 1) as b:
                    batch(b, False)
                batch(B - 1, True)


def relative_attention(nc, d, h0, route, y, xh, xl):
    with ExitStack() as ctx:
        def sb(name, shape, dt=F32):
            return ctx.enter_context(nc.sbuf_tensor("b_" + name, shape, dt))

        def sem(name):
            return ctx.enter_context(nc.semaphore("b_" + name))

        W2 = REL * H
        w_in = sb("w_in", [128, KC, QKVB])
        w_q = sb("w_q", [128, KC, C])
        w_pos = sb("w_pos", [128, KC, C])
        w_out = sb("w_out", [128, KC, C])
        w_gate = sb("w_gate", [128, KC, E])
        pos = sb("pos", [128, KC, REL])
        own = sb("own", [128, KC, W2])
        small = sb("small", [128, 16])
        B_POS, B_Q, R_R = 0, 2, 4
        in_rows = sb("in_rows", [128, QKVB])
        rw_row = sb("rw_row", [128, C])
        out_row = sb("out_row", [128, C])
        gate_row = sb("gate_row", [128, E])
        ident = sb("ident", [128, 128])

        posT = sb("posT", [128, KC, REL])
        pblk = sb("pblk", [128, KC, W2])
        qrr = sb("qrr", [128, KC])
        qrr_all = sb("qrr_all", [128, KC, 128])
        inhi = sb("inhi", [128, KC, QKVB], F32R)
        inlo = sb("inlo", [128, KC, QKVB], F32R)
        ghi = sb("ghi", [128, KC, E], F32R)
        glo = sb("glo", [128, KC, E], F32R)

        stats = sb("stats", [CH, TILES, 6])
        stat = sb("stat", [CH, 6, TILES])
        MEAN, VAR, RSTD, TMP, TMP2 = range(5)
        xn = sb("xn", [CH, 2, C])
        hT = sb("hT", [128, 2, KC, CH], F32R)
        hTl = sb("hTl", [128, 2, KC, CH], F32R)
        qkvb = sb("qkvb", [CH, 4272])
        prod = sb("prod", [CH, B, B, C])
        sc = sb("sc", [CH, B, B * H])
        m2 = sb("m2", [CH, B, 2 * H])
        m1 = sb("m1", [CH, B, H])
        ctx_t = sb("ctx_t", [CH, B, C])
        cT = sb("cT", [128, 2, KC, CH])
        hs = sb("hs", [CH, 2, C])
        lg = sb("lg", [CH, TILES, E])
        choice = sb("choice", [CH, TILES, E])
        masked = sb("masked", [CH, TILES, E])
        left = sb("left", [CH, TILES, E])
        top = sb("top", [CH, TILES, EGROUPS, 8])
        gs = sb("gs", [CH, TILES, EGROUPS])
        beat = sb("beat", [CH, TILES, EGROUPS])
        rank = sb("rank", [CH, TILES, EGROUPS])
        gsum = sb("gsum", [CH, TILES, 2])
        w64 = sb("w64", [CH, TILES, 2 * E])
        whi_r = sb("whi_r", [CH, TILES, E], F32R)

        tp = [ctx.enter_context(nc.psum_tensor(f"b_tp{i}", [128, 512], F32)) for i in range(2)]
        pq = [ctx.enter_context(nc.psum_tensor(f"b_pq{i}", [128, 2, 512], F32)) for i in range(2)]
        po = [ctx.enter_context(nc.psum_tensor(f"b_po{i}", [128, 512], F32)) for i in range(2)]

        loaded = sem("loaded")
        setup_pe = sem("setup_pe")
        setup = sem("setup")
        setup_act = sem("setup_act")
        rel_ready = sem("rel_ready")
        stats_done = sem("stats_done")
        chain = sem("chain")
        xn_ready = sem("xn_ready")
        turned = sem("turned")
        hi_ready = sem("hi_ready")
        lo_ready = sem("lo_ready")
        qkv_full = sem("qkv_full")
        qkv_read = sem("qkv_read")
        qk_done = sem("qk_done")
        shifted = sem("shifted")
        expd = sem("expd")
        p_ready = sem("p_ready")
        pv_done = sem("pv_done")
        ctx_ready = sem("ctx_ready")
        c_turned = sem("c_turned")
        c_copied = sem("c_copied")
        out_full = sem("out_full")
        h_half = sem("h_half")
        h_done = sem("h_done")
        prod_used = sem("prod_used")
        sq = sem("sq")
        sq2 = sem("sq2")
        h_copied = sem("h_copied")
        x2_ready = sem("x2_ready")
        t2 = sem("t2")
        x2hi = sem("x2hi")
        y_copied = sem("y_copied")
        x2lo = sem("x2lo")
        x2_stored = sem("x2_stored")
        lg_full = sem("lg_full")
        lg_read = sem("lg_read")
        routed = sem("routed")
        w_turned = sem("w_turned")
        w_stored = sem("w_stored")

        COLS = [(0, 512), (512, QKVB)]

        with nc.Block() as block:
            @block.sync
            def _(sp):
                for dst, name in ((w_pos, "w_pos"), (pos, "pos"), (own, "own"), (small, "small"), (w_q, "w_q"),
                                  (ident, "ident"), (out_row, "out_row"), (gate_row, "gate_row"), (rw_row, "rw_row"),
                                  (w_out, "w_out"), (w_gate, "w_gate")):
                    sp.dma_start(dst[:], d[name]).then_inc(loaded, 16)
                sp.dma_start(w_in[:, :, 0:3 * C], d["w_in"]).then_inc(loaded, 16)
                sp.dma_start(in_rows[:, 0:3 * C], d["in_rows"]).then_inc(loaded, 16)

            LOADED = 13 * 16

            @block.tensor
            def _(pe):
                pe.wait_ge(loaded, LOADED)
                for j in range(KC):
                    for k in range(KC):
                        m = nc.tensor.matmul(po[0][:, 8 * j:8 * j + REL], w_pos[:, k, 128 * j:128 * j + 128],
                                             pos[:, k, :], start=k == 0, stop=k == KC - 1)
                m.then_inc(setup_pe, 1)
                pe.wait_ge(rel_ready, 1)
                for j in range(KC):
                    for k in range(KC):
                        nc.tensor.matmul(po[1][:, W2 * j:W2 * j + W2], w_q[:, k, 128 * j:128 * j + 128],
                                         pblk[:, k, :], start=k == 0, stop=k == KC - 1)
                for k in range(KC):
                    m = nc.tensor.matmul(po[1][:, W2 * 2:W2 * 3], qrr_all[:, k, :], pblk[:, k, :],
                                         start=k == 0, stop=k == KC - 1)
                m.then_inc(setup_pe, 1)
                pe.wait_ge(setup_act, 1)
                pe.wait_ge(rel_ready, 3)

                def turn(b, n):
                    pe.wait_ge(xn_ready, n + 1)
                    pe.wait_ge(lo_ready, n - 1 + 2)
                    for k in range(KC):
                        m = nc.tensor.transpose(tp[b % 2][:, k * 128:k * 128 + CH], xn[:, b % 2, 128 * k:128 * k + 128],
                                                ident[0:CH, 0:CH])
                    m.then_inc(turned, 1)

                def project(b, n):
                    pe.wait_ge(hi_ready, n + 1)
                    pe.wait_ge(lo_ready, n + 1 + 2)
                    pe.wait_ge(qkv_read, n - 1 + 2)
                    for i, (a, z) in enumerate(COLS):
                        m = split_matmul(nc, pq[b % 2][0:CH, i, 0:z - a],
                                         [(hT[:, b % 2, k, 0:CH], hTl[:, b % 2, k, 0:CH]) for k in range(KC)],
                                         [(inhi[:, k, a:z], inlo[:, k, a:z]) for k in range(KC)])
                    m.then_inc(qkv_full, 1)

                with pe.Fori(0, NCH) as c:
                    turn(0, c * B)
                    for b in range(B):
                        if b + 1 < B:
                            turn(b + 1, c * B + b + 1)
                        project(b, c * B + b)
                    pe.wait_ge(ctx_ready, c + 1)
                    for b in range(B):
                        n = c * B + b
                        pe.wait_ge(c_copied, n - 1 + 2)
                        for k in range(KC):
                            m = nc.tensor.transpose(tp[b % 2][:, 256 + k * 128:256 + k * 128 + CH],
                                                    ctx_t[:, b, 128 * k:128 * k + 128], ident[0:CH, 0:CH])
                        m.then_inc(c_turned, 1)
                        pe.wait_ge(c_copied, n + 1 + 2)
                        pe.wait_ge(h_half, n - 1 + 2)
                        for k in range(KC):
                            m = nc.tensor.matmul(po[b % 2][0:CH, 0:C], cT[:, b % 2, k, :], w_out[:, k, :],
                                                 start=k == 0, stop=k == KC - 1)
                        m.then_inc(out_full, 1)

                with pe.Fori(0, NCH) as c:
                    for b in range(B):
                        n = c * B + b
                        pe.wait_ge(h_copied, n + 1)
                        pe.wait_ge(x2_ready, n + 1)
                        pe.wait_ge(x2lo, n - 1 + 2)
                        pe.wait_ge(y_copied, n - 1 + 2)
                        for k in range(KC):
                            nc.tensor.transpose(tp[b % 2][:, k * 128:k * 128 + CH], xn[:, b % 2, 128 * k:128 * k + 128],
                                                ident[0:CH, 0:CH])
                            m = nc.tensor.transpose(pq[b % 2][:, 0, k * 128:k * 128 + CH],
                                                    hs[:, b % 2, 128 * k:128 * k + 128], ident[0:CH, 0:CH])
                        m.then_inc(t2, 1)
                        pe.wait_ge(x2lo, n + 1 + 2)
                        pe.wait_ge(lg_read, n - 1 + 2)
                        split_matmul(nc, po[b % 2][0:CH, 0:E],
                                     [(hT[:, b % 2, k, 0:CH], hTl[:, b % 2, k, 0:CH]) for k in range(KC)],
                                     [(ghi[:, k, :], glo[:, k, :]) for k in range(KC)]).then_inc(lg_full, 1)
                pe.wait_ge(routed, 1)
                for t in range(TILES):
                    if t % 4 == 0 and t >= 8:
                        pe.wait_ge(w_stored, t // 4 - 1)
                    m = nc.tensor.transpose(pq[t // 4 % 2][0:2 * E, 0, t % 4 * CH:t % 4 * CH + CH], w64[:, t, :],
                                            ident[0:CH, 0:CH])
                    if t % 4 == 3:
                        m.then_inc(w_turned, 1)

            @block.gpsimd
            def _(pool):
                with pool.Fori(0, NCH) as c:
                    pool.wait_ge(qkv_read, c * B + B + 2)
                    for t in (2, 3):
                        for s in range(B):
                            m = nc.gpsimd.tensor_tensor(prod[:, t, s, :], qkvb[:, t * QKVB:t * QKVB + C],
                                                        qkvb[:, s * QKVB + C:s * QKVB + 2 * C], ALU.mult)
                    m.then_inc(qk_done, 1)
                pool.wait_ge(h_done, TILES)
                with pool.Fori(0, NCH) as c:
                    for b in range(B):
                        n = c * B + b
                        pool.wait_ge(t2, n - 1 + 2)
                        nc.gpsimd.tensor_copy(hs[:, b % 2, :], h0[:, bass.ds(b * NCH + c, 1), :].rearrange(
                            "p t f -> p (t f)")).then_inc(h_copied, 1)
                        pool.wait_ge(x2lo, n + 1 + 2)
                        pos_ = b * NCH + c
                        nc.gpsimd.tensor_copy(xh[:, :, bass.ds(pos_, 1), :].rearrange("p k t n -> p k (t n)"),
                                              f32(hT[:, b % 2]))
                        nc.gpsimd.tensor_copy(xl[:, :, bass.ds(pos_, 1), :].rearrange("p k t n -> p k (t n)"),
                                              f32(hTl[:, b % 2])).then_inc(x2_stored, 1)

            @block.scalar
            def _(act):
                act.wait_ge(rel_ready, 2)
                nc.scalar.activation(inhi[:], w_in[:], ACT.Copy)
                nc.scalar.activation(ghi[:], w_gate[:], ACT.Copy).then_inc(setup_act, 1)
                act.wait_ge(stats_done, 1)
                nc.scalar.activation(stat[:, TMP, :], stat[:, VAR, :], ACT.Sqrt).then_inc(sq, 1)
                with act.Fori(0, NCH) as c:
                    for b in range(B):
                        n = c * B + b
                        act.wait_ge(turned, n + 1)
                        act.wait_ge(qkv_full, n - 1 + 2)
                        nc.scalar.activation(hT[:, b % 2, :, :],
                                             tp[b % 2][:, 0:256].rearrange("p (k n) -> p k n", k=KC)[:, :, 0:CH],
                                             ACT.Copy).then_inc(hi_ready, 1)
                    act.wait_ge(shifted, c + 1)
                    nc.scalar.activation(sc[:], sc[:], ACT.Exp, scale=SCALE).then_inc(expd, 1)
                    for b in range(B):
                        n = c * B + b
                        act.wait_ge(c_turned, n + 1)
                        act.wait_ge(out_full, n - 1 + 2)
                        nc.scalar.activation(cT[:, b % 2, :, :],
                                             tp[b % 2][:, 256:512].rearrange("p (k n) -> p k n", k=KC)[:, :, 0:CH],
                                             ACT.Copy).then_inc(c_copied, 1)
                act.wait_ge(stats_done, 2)
                nc.scalar.activation(stat[:, TMP, :], stat[:, VAR, :], ACT.Sqrt).then_inc(sq, 1)
                with act.Fori(0, NCH) as c:
                    for b in range(B):
                        n = c * B + b
                        act.wait_ge(t2, n + 1 + 2)
                        act.wait_ge(lg_full, n - 1 + 2)
                        act.wait_ge(x2_stored, n - 1 + 2)
                        turned_x, turned_h = (t_.rearrange("p (k n) -> p k n", k=KC)[:, :, 0:CH]
                                              for t_ in (tp[b % 2][:, 0:256], pq[b % 2][:, 0, 0:256]))
                        nc.scalar.activation(hT[:, b % 2, :, :], turned_x, ACT.Copy).then_inc(x2hi, 1)
                        nc.scalar.activation(y[:, :, bass.ds(b * NCH + c, 1), :].rearrange("p k t n -> p k (t n)"),
                                             turned_h, ACT.Copy).then_inc(y_copied, 1)
                        act.wait_ge(lg_full, n + 1 + 2)
                        nc.scalar.activation(lg[:, bass.ds(b * NCH + c, 1), :].rearrange("p t f -> p (t f)"),
                                             po[b % 2][0:CH, 0:E], ACT.Sigmoid).then_inc(lg_read, 1)
                for k in range(TILES // 4):
                    act.wait_ge(w_turned, k + 1)
                    nc.scalar.activation(route[:, k * BLKP:(k + 1) * BLKP], pq[k % 2][0:2 * E, 0, 0:BLKP],
                                         ACT.Copy).then_inc(w_stored, 1)
                act.wait_ge(w_stored, TILES // 4)

            @block.vector
            def _(dve):
                V = nc.vector
                done = [0]

                def link(ins):
                    done[0] += 1
                    ins.then_inc(setup, 1)
                    dve.wait_ge(setup, done[0])

                for s_ in (lo_ready, qkv_read, h_half, x2lo, c_copied, y_copied, lg_read, qkv_full, out_full,
                           lg_full, x2_stored, t2):
                    dve.sem_inc(s_, 2)

                dve.wait_ge(loaded, LOADED)
                dve.wait_ge(setup_pe, 1)
                for k in range(KC):
                    link(V.tensor_scalar(posT[:, k, :], po[0][:, 8 * k:8 * k + REL], small[:, B_POS + k:B_POS + k + 1],
                                         None, ALU.add))
                    link(V.tensor_tensor(pblk[:, k, :].rearrange("p (r h) -> p r h", h=H),
                                         own[:, k, :].rearrange("p (r h) -> p r h", h=H),
                                         posT[:, k, :].unsqueeze(2).to_broadcast([128, REL, H]), ALU.mult))
                link(V.tensor_tensor(qrr[:], small[:, B_Q:B_Q + 2], small[:, R_R:R_R + 2], ALU.add))
                for k in range(KC):
                    m = V.tensor_scalar(qrr_all[:, k, :], ident[:], 0.0, qrr[:, k:k + 1], ALU.mult, ALU.add)
                m.then_inc(rel_ready, 1)
                link(V.tensor_tensor(in_rows[:, 0:C], in_rows[:, 0:C], rw_row[:], ALU.add))
                dve.wait_ge(setup_pe, 2)
                for k in range(KC):
                    link(V.tensor_copy(w_in[:, k, 3 * C:QKVB], po[1][:, W2 * k:W2 * k + W2]))
                V.tensor_copy(in_rows[:, 3 * C:QKVB], po[1][:, 2 * W2:3 * W2]).then_inc(rel_ready, 1)
                dve.wait_ge(rel_ready, 2)
                dve.wait_ge(setup_act, 1)
                V.tensor_tensor(inlo[:], w_in[:], f32(inhi[:]), ALU.subtract)
                V.tensor_tensor(glo[:], w_gate[:], f32(ghi[:]), ALU.subtract).then_inc(rel_ready, 1)

                def statistics(k):
                    for t in range(TILES):
                        m = V.bn_stats(stats[:, t, :], h0[:, t, :])
                    link(m)
                    me, ve, mo, vo = (stats[:, :, i] for i in (1, 2, 4, 5))
                    link(V.tensor_tensor(stat[:, MEAN, :], me, mo, ALU.add))
                    link(V.tensor_scalar(stat[:, MEAN, :], stat[:, MEAN, :], 0.5, None, ALU.mult))
                    link(V.tensor_tensor(stat[:, TMP, :], me, mo, ALU.subtract))
                    link(V.tensor_tensor(stat[:, TMP, :], stat[:, TMP, :], stat[:, TMP, :], ALU.mult))
                    link(V.tensor_scalar(stat[:, TMP, :], stat[:, TMP, :], 0.25, EPS, ALU.mult, ALU.add))
                    link(V.tensor_tensor(stat[:, TMP2, :], ve, vo, ALU.add))
                    V.scalar_tensor_tensor(stat[:, VAR, :], stat[:, TMP2, :], 1.0 / C, stat[:, TMP, :], ALU.mult,
                                           ALU.add).then_inc(stats_done, 1)
                    dve.wait_ge(sq, k)
                    link(V.reciprocal(stat[:, RSTD, :], stat[:, TMP, :]))
                    link(V.tensor_tensor(stat[:, TMP2, :], stat[:, RSTD, :], stat[:, RSTD, :], ALU.mult))
                    link(V.tensor_tensor(stat[:, TMP2, :], stat[:, TMP2, :], stat[:, VAR, :], ALU.mult))
                    link(V.tensor_scalar(stat[:, TMP2, :], stat[:, TMP2, :], -0.5, 1.5, ALU.mult, ALU.add))
                    link(V.tensor_tensor(stat[:, RSTD, :], stat[:, RSTD, :], stat[:, TMP2, :], ALU.mult))

                def normalise(b, c):
                    t = b * NCH + c
                    V.tensor_scalar(xn[:, b % 2, :], h0[:, bass.ds(t, 1), :].rearrange("p t f -> p (t f)"),
                                    stat[:, MEAN, bass.ds(t, 1)], stat[:, RSTD, bass.ds(t, 1)],
                                    ALU.subtract, ALU.mult).then_inc(xn_ready, 1)

                statistics(1)
                qk = qkvb[:, 0:B * QKVB].rearrange("p (t f) -> p t f", t=B)
                STEP = QKVB - H
                rel = qkvb[:, 3 * C + 3 * H:3 * C + 3 * H + B * STEP].rearrange("p (t f) -> p t f", f=STEP)[:, :, 0:B * H]
                STEPS = 14
                with dve.Fori(0, NCH) as c:
                    steps = [0]

                    def step(ins):
                        steps[0] += 1
                        ins.then_inc(chain, 1)
                        dve.wait_ge(chain, c * STEPS + steps[0])

                    def low(b):
                        n = c * B + b
                        dve.wait_ge(hi_ready, n + 1)
                        V.tensor_tensor(hTl[:, b % 2, :, :],
                                        tp[b % 2][:, 0:256].rearrange("p (k n) -> p k n", k=KC)[:, :, 0:CH],
                                        f32(hT[:, b % 2, :, :]), ALU.subtract).then_inc(lo_ready, 1)

                    def bias(b):
                        n = c * B + b
                        dve.wait_ge(qkv_full, n + 1 + 2)
                        V.tensor_tensor(qk[:, b, 0:512], pq[b % 2][0:CH, 0, :], in_rows[0:CH, 0:512], ALU.add)
                        V.tensor_tensor(qk[:, b, 512:QKVB], pq[b % 2][0:CH, 1, 0:QKVB - 512],
                                        in_rows[0:CH, 512:QKVB], ALU.add).then_inc(qkv_read, 1)

                    normalise(0, c)
                    normalise(1, c)
                    low(0)
                    low(1)
                    for b in range(B):
                        bias(b)
                        if b + 2 < B:
                            normalise(b + 2, c)
                            low(b + 2)
                    dve.wait_ge(qkv_read, c * B + B + 2)
                    for t in (0, 1):
                        m = V.tensor_tensor(prod[:, t, :, :], qk[:, t, 0:C].unsqueeze(1).to_broadcast([CH, B, C]),
                                            qk[:, :, C:2 * C], ALU.mult)
                    step(m)
                    dve.wait_ge(qk_done, c + 1)
                    step(V.tensor_reduce(sc[:].rearrange("p t x -> p (t x)"),
                                         prod[:].rearrange("p t s (h e) -> p (t s h) e", e=HD), AX_X, ALU.add))
                    step(V.tensor_tensor(sc[:], sc[:], rel, ALU.add))
                    step(V.tensor_tensor(m2[:], sc[:, :, 0:2 * H], sc[:, :, 2 * H:4 * H], ALU.max))
                    step(V.tensor_tensor(m1[:], m2[:, :, 0:H], m2[:, :, H:2 * H], ALU.max))
                    V.tensor_tensor(sc[:].rearrange("p t (s h) -> p t s h", h=H),
                                    sc[:].rearrange("p t (s h) -> p t s h", h=H),
                                    m1[:].unsqueeze(2).to_broadcast([CH, B, B, H]), ALU.subtract).then_inc(shifted, 1)
                    dve.wait_ge(expd, c + 1)
                    step(V.tensor_tensor(m2[:], sc[:, :, 0:2 * H], sc[:, :, 2 * H:4 * H], ALU.add))
                    step(V.tensor_tensor(m1[:], m2[:, :, 0:H], m2[:, :, H:2 * H], ALU.add))
                    step(V.reciprocal(m1[:], m1[:]))
                    step(V.tensor_tensor(sc[:].rearrange("p t (s h) -> p t s h", h=H),
                                         sc[:].rearrange("p t (s h) -> p t s h", h=H),
                                         m1[:].unsqueeze(2).to_broadcast([CH, B, B, H]), ALU.mult))
                    for t in range(B):
                        for s in range(B):
                            m = V.tensor_tensor(prod[:, t, s, :].rearrange("p (h e) -> p h e", e=HD),
                                                sc[:, t, s * H:(s + 1) * H].unsqueeze(2).to_broadcast([CH, H, HD]),
                                                qk[:, s, 2 * C:3 * C].rearrange("p (h e) -> p h e", e=HD), ALU.mult)
                    step(m)
                    step(V.tensor_tensor(prod[:, :, 0:2, :], prod[:, :, 0:2, :], prod[:, :, 2:4, :], ALU.add))
                    V.tensor_tensor(ctx_t[:], prod[:, :, 0, :], prod[:, :, 1, :], ALU.add).then_inc(ctx_ready, 1)
                    for b in range(B):
                        n = c * B + b
                        t = b * NCH + c
                        hb = h0[:, bass.ds(t, 1), :].rearrange("p t f -> p (t f)")
                        dve.wait_ge(out_full, n + 1 + 2)
                        V.tensor_tensor(hs[:, b % 2, :], po[b % 2][0:CH, 0:C], out_row[0:CH, :],
                                        ALU.add).then_inc(h_half, 1)
                        dve.wait_ge(h_half, n + 1 + 2)
                        V.tensor_tensor(hb, hb, hs[:, b % 2, :], ALU.add).then_inc(h_done, 1)
                    while steps[0] < STEPS:
                        step(V.tensor_copy(m2[:, 0, 0:1], m1[:, 0, 0:1]))
                    assert steps[0] == STEPS

                dve.wait_ge(h_done, TILES)
                statistics(2)
                with dve.Fori(0, NCH) as c:
                    for b in range(B):
                        n = c * B + b
                        t = b * NCH + c
                        dve.wait_ge(t2, n - 1 + 2)
                        V.tensor_scalar(xn[:, b % 2, :], h0[:, bass.ds(t, 1), :].rearrange("p t f -> p (t f)"),
                                        stat[:, MEAN, bass.ds(t, 1)], stat[:, RSTD, bass.ds(t, 1)],
                                        ALU.subtract, ALU.mult).then_inc(x2_ready, 1)
                        dve.wait_ge(x2hi, n + 1)
                        V.tensor_tensor(hTl[:, b % 2, :, :],
                                        tp[b % 2][:, 0:256].rearrange("p (k n) -> p k n", k=KC)[:, :, 0:CH],
                                        f32(hT[:, b % 2, :, :]), ALU.subtract).then_inc(x2lo, 1)

                dve.wait_ge(lg_read, TILES + 2)
                link(V.tensor_tensor(choice[:], lg[:], gate_row[0:CH, :].unsqueeze(1).to_broadcast([CH, TILES, E]),
                                     ALU.add))
                for t in range(TILES):
                    for g_ in range(EGROUPS):
                        m = V.max(top[:, t, g_, :], choice[:, t, g_ * GE:(g_ + 1) * GE])
                link(m)
                link(V.tensor_tensor(gs[:], top[:, :, :, 0], top[:, :, :, 1], ALU.add))
                link(V.memset(rank[:], 0.0))
                for i in range(1, EGROUPS):
                    link(V.tensor_tensor(beat[:, :, 0:EGROUPS - i], gs[:, :, 0:EGROUPS - i], gs[:, :, i:EGROUPS],
                                         ALU.is_ge))
                    link(V.tensor_tensor(rank[:, :, i:EGROUPS], rank[:, :, i:EGROUPS], beat[:, :, 0:EGROUPS - i],
                                         ALU.add))
                    link(V.tensor_scalar(beat[:, :, 0:EGROUPS - i], beat[:, :, 0:EGROUPS - i], -1.0, 1.0,
                                         ALU.mult, ALU.add))
                    link(V.tensor_tensor(rank[:, :, 0:EGROUPS - i], rank[:, :, 0:EGROUPS - i],
                                         beat[:, :, 0:EGROUPS - i], ALU.add))
                link(V.tensor_scalar(beat[:], rank[:], KGROUPS - 0.5, None, ALU.is_lt))
                link(V.tensor_tensor(masked[:].rearrange("p t (g e) -> p (t g) e", e=GE),
                                     choice[:].rearrange("p t (g e) -> p (t g) e", e=GE),
                                     beat[:].rearrange("p t g -> p (t g)").unsqueeze(2).to_broadcast(
                                         [CH, TILES * EGROUPS, GE]), ALU.mult))
                for t in range(TILES):
                    m = V.max(top[:, t, 0, :], masked[:, t, :])
                link(m)
                for t in range(TILES):
                    m = V.match_replace(left[:, t, :], top[:, t, 0, :], masked[:, t, :], LOWEST)
                link(m)
                link(V.tensor_tensor(left[:], left[:], masked[:], ALU.not_equal))
                link(V.tensor_tensor(left[:], left[:], lg[:], ALU.mult))
                link(V.tensor_reduce(gsum[:, :, 0:1], left[:], AX_X, ALU.add))
                link(V.tensor_scalar(gsum[:, :, 0:1], gsum[:, :, 0:1], 1e-20, None, ALU.add))
                link(V.reciprocal(gsum[:, :, 1:2], gsum[:, :, 0:1]))
                link(V.tensor_tensor(left[:], left[:], gsum[:, :, 1:2].to_broadcast([CH, TILES, E]), ALU.mult))
                link(V.tensor_scalar(left[:], left[:], ROUTED_SCALING, None, ALU.mult))
                link(V.tensor_copy(whi_r[:], left[:]))
                link(V.tensor_copy(w64[:, :, 0:E], f32(whi_r[:])))
                V.tensor_tensor(w64[:, :, E:2 * E], left[:], f32(whi_r[:]), ALU.subtract).then_inc(routed, 1)


BLKP = 4 * CH
TP = B * NCH * CH
NB = TP // BLKP
WU = 3 * KC * INNER


def experts(nc, d, route, y, xh, xl, out):
    with ExitStack() as ctx:
        def sb(name, shape, dt=F32):
            return ctx.enter_context(nc.sbuf_tensor("e_" + name, shape, dt))

        def sem(name):
            return ctx.enter_context(nc.semaphore("e_" + name))

        stage = sb("stage", [128, 2, UNITS * WU])
        wh = sb("wh", [128, 2, UNITS * WU], F32R)
        wl = sb("wl", [128, 2, UNITS * WU], F32R)
        sel_in = sb("sel_in", [2 * E, E, 128])
        sel = sb("sel", [2 * E, E, 128], F32R)
        sg = sb("sg", [128, 2, BLKP])
        su = sb("su", [128, 2, BLKP])
        hv = sb("hv", [128, 2, BLKP])
        hh = sb("hh", [128, 2, BLKP], F32R)
        hl = sb("hl", [128, 2, BLKP], F32R)
        ps = [[ctx.enter_context(nc.psum_tensor(f"e_{n}{i}", [128, 512], F32)) for n in ("g", "u", "w")]
              for i in range(2)]
        ps_y = [ctx.enter_context(nc.psum_tensor(f"e_y{i}", [128, 512], F32)) for i in range(KC)]

        sel_loaded = sem("sel_loaded")
        sel_ready = sem("sel_ready")
        w_loaded = [sem("w_loaded0"), sem("w_loaded1")]
        w_high = sem("w_high")
        w_low = sem("w_low")
        up_full = sem("up_full")
        silu_done = sem("silu_done")
        mul_done = sem("mul_done")
        h_ready = sem("h_ready")
        high_done = sem("high_done")
        low_done = sem("low_done")
        down_done = sem("down_done")
        y_added = sem("y_added")
        stored = sem("stored")

        groups = [(2, None)] + [(UNITS, e) for e in range(0, E, UNITS)]
        base = [NB * sum(n for n, _ in groups[:i]) for i in range(len(groups) + 1)]
        G = len(groups)

        with nc.Block() as block:
            def yv(nb):
                return y[:].rearrange("p k t n -> p k (t n)")[:, :, bass.ds(nb * BLKP, BLKP)]

            @block.sync
            def _(sp):
                sp.dma_start(sel_in[:], d["sel"]).then_inc(sel_loaded, 16)
                for i, (n, _) in enumerate(groups):
                    if i >= 2:
                        sp.wait_ge(w_high, i - 1)
                        sp.wait_ge(w_low, i - 1)
                    sp.dma_start(stage[:, i % 2, 0:n * WU], d["w_exp"][i, :, 0:n * WU]).then_inc(w_loaded[i % 2], 16)
                with sp.Fori(0, NB) as nb:
                    sp.wait_ge(y_added, (G - 1) * NB + nb + 2)
                    sp.dma_start(out.rearrange("(k p) n -> p k n", k=KC)[:, :, bass.ds(nb * BLKP, BLKP)],
                                 yv(nb)).then_inc(stored, 16)
                sp.wait_ge(stored, NB * 16)

            def xv(x, k, nb):
                return x[:, k].rearrange("p t n -> p (t n)")[:, bass.ds(nb * BLKP, BLKP)]

            def weights(slot, u, kind, k):
                a = u * WU + kind * KC * INNER + k * INNER
                return wh[:, slot, a:a + INNER], wl[:, slot, a:a + INNER]

            @block.gpsimd
            def _(pool):
                for i, (n, _) in enumerate(groups):
                    pool.wait_ge(w_high, i + 1)
                    s = i % 2
                    nc.gpsimd.tensor_tensor(wl[:, s, 0:n * WU], stage[:, s, 0:n * WU], f32(wh[:, s, 0:n * WU]),
                                            ALU.subtract).then_inc(w_low, 1)

            @block.tensor
            def _(pe):
                def up(i, u, nb, n):
                    _, e0 = groups[i]
                    slot = u % 2
                    pe.wait_ge(h_ready, n - 1 + 2)
                    xs = [(xv(xh, k, nb), xv(xl, k, nb)) for k in range(KC)]
                    for kind in range(2):
                        m = split_matmul(nc, ps[slot][kind][:, 0:BLKP],
                                         [weights(i % 2, u, kind, k) for k in range(KC)], xs)
                    if e0 is not None:
                        m = nc.tensor.matmul(ps[slot][2][:, 0:BLKP], sel[:, e0 + u, :],
                                             route[:, bass.ds(nb * BLKP, BLKP)], start=True, stop=True)
                    m.then_inc(up_full, 1)

                def down(i, u, nb, n):
                    slot = u % 2
                    if u == 0:
                        pe.wait_ge(y_added, i * NB + nb + 1)
                    pe.wait_ge(low_done, n + 2)
                    last = u == groups[i][0] - 1
                    for k in range(KC):
                        m = split_matmul(nc, ps_y[k][:, 0:BLKP], [weights(i % 2, u, 2, k)],
                                         [(hh[:, slot, :], hl[:, slot, :])], first=u == 0, last=last)
                    m.then_inc(down_done, 1)

                pe.sem_inc(down_done, 2)
                pe.wait_ge(sel_ready, 1)
                pe.wait_ge(w_low, 1)
                for u in range(2):
                    up(0, u, 0, u)
                for i, (U, _) in enumerate(groups):
                    def block_of(nb, nxt):
                        for u in range(U):
                            n = nb * U + base[i] + u
                            if u + 2 < U:
                                up(i, u + 2, nb, n + 2)
                            elif nxt is None:
                                up(i, u + 2 - U, nb + 1, n + 2)
                            elif nxt < G:
                                if u == U - 2:
                                    pe.wait_ge(w_low, nxt + 1)
                                up(nxt, u + 2 - U, 0, n + 2)
                            down(i, u, nb, n)
                    with pe.Fori(0, NB - 1) as nb:
                        block_of(nb, None)
                    block_of(NB - 1, i + 1)

            @block.scalar
            def _(act):
                act.wait_ge(sel_loaded, 16)
                nc.scalar.activation(sel[:], sel_in[:], ACT.Copy).then_inc(sel_ready, 1)

                def split_weights(i):
                    n = groups[i][0]
                    act.wait_ge(w_loaded[i % 2], 16 * (i // 2 + 1))
                    if i >= 2:
                        act.wait_ge(down_done, base[i - 1] + 2)
                    nc.scalar.activation(wh[:, i % 2, 0:n * WU], stage[:, i % 2, 0:n * WU], ACT.Copy).then_inc(w_high, 1)

                def silu(slot, n):
                    act.wait_ge(up_full, n + 1)
                    nc.scalar.activation(sg[:, slot, :], ps[slot][0][:, 0:BLKP], ACT.Silu).then_inc(silu_done, 1)

                split_weights(0)
                split_weights(1)
                silu(0, 0)
                for i, (U, _) in enumerate(groups):
                    def block_of(nb, final):
                        for u in range(U):
                            n = nb * U + base[i] + u
                            if not (final and u == U - 1):
                                silu((u + 1) % 2, n + 1)
                            act.wait_ge(h_ready, n + 1 + 2)
                            act.wait_ge(down_done, n - 1 + 2)
                            nc.scalar.activation(hh[:, u % 2, :], hv[:, u % 2, :], ACT.Copy).then_inc(high_done, 1)
                    block_of(0, False)
                    if i >= 1 and i + 1 < G:
                        split_weights(i + 1)
                    with act.Fori(1, NB - 1) as nb:
                        block_of(nb, False)
                    block_of(NB - 1, i == G - 1)

            @block.vector
            def _(dve):
                V = nc.vector
                dve.sem_inc(h_ready, 2)
                dve.sem_inc(low_done, 1)
                dve.sem_inc(y_added, 1)

                def multiply(shared, slot, n, first=False):
                    dve.wait_ge(silu_done, n + 1)
                    if not first:
                        dve.wait_ge(low_done, n)
                    if shared:
                        V.tensor_tensor(hv[:, slot, :], sg[:, slot, :], ps[slot][1][:, 0:BLKP],
                                        ALU.mult).then_inc(h_ready, 1)
                        return
                    V.tensor_tensor(su[:, slot, :], sg[:, slot, :], ps[slot][1][:, 0:BLKP],
                                    ALU.mult).then_inc(mul_done, 1)
                    dve.wait_ge(mul_done, n + 1 - base[1])
                    V.tensor_tensor(hv[:, slot, :], su[:, slot, :], ps[slot][2][:, 0:BLKP],
                                    ALU.mult).then_inc(h_ready, 1)

                def add_y(i, nb, count):
                    dve.wait_ge(down_done, count + 2)
                    for k in range(KC):
                        part = y[:, k].rearrange("p t n -> p (t n)")[:, bass.ds(nb * BLKP, BLKP)]
                        m = V.tensor_tensor(part, part, ps_y[k][:, 0:BLKP], ALU.add)
                    m.then_inc(y_added, 1)

                multiply(True, 0, 0, first=True)
                for i, (U, e0) in enumerate(groups):
                    def block_of(nb, end):
                        for u in range(U):
                            n = nb * U + base[i] + u
                            if u < U - 1 or not end:
                                multiply(e0 is None, (u + 1) % 2, n + 1)
                            elif i + 1 < G:
                                multiply(False, (u + 1) % 2, n + 1)
                            dve.wait_ge(high_done, n + 1)
                            V.tensor_tensor(hl[:, u % 2, :], hv[:, u % 2, :], f32(hh[:, u % 2, :]),
                                            ALU.subtract).then_inc(low_done, 1)
                        add_y(i, nb, nb * U + base[i] + U)
                    with dve.Fori(0, NB - 1) as nb:
                        block_of(nb, False)
                    block_of(NB - 1, True)


def build(nc, d, out):
    with ExitStack() as ctx:
        def sb(name, shape, dt=F32):
            return ctx.enter_context(nc.sbuf_tensor(name, shape, dt))
        h0 = sb("h0", [CH, TILES, C])
        token_attention(nc, d, h0)
        route = sb("route", [2 * E, TP], F32R)
        y = sb("y", [128, KC, TILES, CH])
        xh = sb("xh", [128, KC, TILES, CH], F32R)
        xl = sb("xl", [128, KC, TILES, CH], F32R)
        relative_attention(nc, d, h0, route, y, xh, xl)
        experts(nc, d, route, y, xh, xl, out)


def kernel(**inputs):
    import numpy as _np
    import concourse.bacc as _bacc
    from concourse import mybir as _mybir
    from concourse.bass_utils import run_bass_kernel_spmd as _run

    v = {k: _np.asarray(a) for k, a in inputs.items()}
    f = _np.float32
    dt = v["x"].dtype

    def fold(a):
        return a.reshape(KC, 128, -1).transpose(1, 0, 2)

    def col(a):
        return a.reshape(KC, 128).T

    def row(a):
        return _np.broadcast_to(a, (128, a.shape[0]))

    a = {}
    xt = v["x"].transpose(2, 0, 1)
    xt = _np.concatenate([xt, xt[:, :, 0:LP - N]], axis=2)
    a["xt"] = xt.reshape(KC, 128, B, LP).transpose(1, 0, 2, 3)
    wqkv, bqkv = v["L0_tok_W_qkv"], v["L0_tok_b_qkv"]
    wqk = _np.zeros((C, 2, PAIRS, 2, 4, HD), dt)
    bqk = _np.zeros((2, PAIRS, 2, 4, HD), dt)
    for s in range(3):
        wqk[:, :, :, :, s] = wqkv[:, 0:2 * C].reshape(C, 2, PAIRS, 2, HD)
        bqk[:, :, :, s] = bqkv[0:2 * C].reshape(2, PAIRS, 2, HD)
    low = (2, 1)
    mbqk = _np.zeros_like(bqk)
    mask = _np.zeros((2, 4, HD, 2), dt)
    for i in range(2):
        mbqk[i, :, :, low[i]] = bqk[i, :, :, low[i]]
        mask[:, low[i], :, i] = 1
    bqk[1, :, :, 3] = 1
    a["w_qk"] = fold(wqk.reshape(C, -1)).reshape(128, KC, 2, PAIRS * 128)
    a["w_v"] = fold(wqkv[:, 2 * C:])
    a["w_proj"] = fold(v["L0_tok_W_proj"])
    cols = _np.zeros((128, 64), dt)
    cols[:, 0:16] = bqk.reshape(16, 128).T
    cols[:, 16:32] = mbqk.reshape(16, 128).T
    cols[:, 32:34] = mask.reshape(128, 2)
    cols[:, 34:36] = col(v["L0_tok_b_proj"])
    cols[:, 36:38] = col(v["L0_tok_ln_g"])
    cols[:, 38:40] = col(v["L0_tok_ln_b"])
    cols[:, 40:42] = col(v["L0_tok_general_token"].reshape(C))
    a["cols"] = cols
    a["rows"] = _np.stack([row(bqkv[2 * C:]), row(v["L0_tok_b_proj"])], axis=1)
    a["ident"] = _np.eye(128, dtype=f)
    a["mean_all"] = _np.full((128, 128), 1.0 / C, f)

    w_in = v["L0_attn_in_proj_weight"]
    b_in = v["L0_attn_in_proj_bias"]
    a["w_in"] = fold(w_in.T)
    a["w_q"] = fold(w_in[0:C])
    a["w_pos"] = fold(v["L0_attn_pos_proj_weight"].T)
    a["w_out"] = fold(v["L0_attn_out_proj_weight"].T)
    a["w_gate"] = fold(v["L0_ffn_gate_w"].T)
    a["pos"] = fold(v["L0_attn_pos"][0:REL, 0].T)
    own = _np.zeros((H, HD, REL, H), f)
    for h in range(H):
        own[h, :, :, h] = 1
    a["own"] = fold(own.reshape(C, REL * H))
    small = _np.zeros((128, 16), dt)
    small[:, 0:2] = col(v["L0_attn_pos_proj_bias"])
    small[:, 2:4] = col(b_in[0:C])
    small[:, 4:6] = col(v["L0_attn_r_r_bias"].reshape(C))
    a["small"] = small
    a["in_rows"] = row(b_in)
    a["rw_row"] = row(v["L0_attn_r_w_bias"].reshape(C))
    a["out_row"] = row(v["L0_attn_out_proj_bias"])
    a["gate_row"] = row(v["L0_ffn_gate_bias"])

    def unit(wg, wu, wd):
        return _np.concatenate([fold(wg.T).reshape(128, -1), fold(wu.T).reshape(128, -1), wd.T], axis=1)

    units = [unit(v["L0_ffn_shared_gate"][i:i + INNER], v["L0_ffn_shared_up"][i:i + INNER],
                  v["L0_ffn_shared_down"][:, i:i + INNER]) for i in (0, INNER)]
    units += [_np.zeros_like(units[0])] * (UNITS - 2)
    units += [unit(v["L0_ffn_expert_gate"][e], v["L0_ffn_expert_up"][e], v["L0_ffn_expert_down"][e])
              for e in range(E)]
    a["w_exp"] = _np.stack(units).reshape(-1, UNITS, 128, WU).transpose(0, 2, 1, 3).reshape(-1, 128, UNITS * WU)
    sel = _np.zeros((2, E, E, 128), f)
    for e in range(E):
        sel[:, e, e] = 1
    a["sel"] = sel.reshape(2 * E, E, 128)

    nc = _bacc.Bacc("TRN2", target_bir_lowering=False, num_devices=1)
    arrays, d = {}, {}
    for name, arr in a.items():
        arr = _np.ascontiguousarray(arr)
        arrays[f"in_{name}"] = arr
        d[name] = nc.dram_tensor(f"in_{name}", arr.shape, _mybir.dt.from_np(arr.dtype), kind="ExternalInput").ap()
    out = nc.dram_tensor("out", (C, TP), F32, kind="ExternalOutput").ap()
    build(nc, d, out)
    r = _run(nc, [arrays], core_ids=[0])
    res = r.results[0]["out"].reshape(C, B, NCH * CH)[:, :, 0:L]
    return _np.ascontiguousarray(res.transpose(1, 2, 0))
```

```python
from contextlib import ExitStack

import numpy as np

import concourse.bass as bass
from concourse import mybir

F32 = mybir.dt.float32
F32R = mybir.dt.float32r
ALU = mybir.AluOpType
ACT = mybir.ActivationFunctionType
AX_X = mybir.AxisListType.X

B, N, C, H = 4, 512, 256, 16
HD = C // H
L = N + 1
LP = 516
HALF = LP // 2
KC = C // 128
SCALE = float(HD) ** -0.5
EPS = 1e-5
NCH = 5
CH = 103
QSIZE = [CH] * 4 + [LP - 4 * CH]
KSIZE = [CH] * 4 + [L - 4 * CH]
PAIRS = H // 2
TILES = B * NCH
REL = 2 * B - 1
QKVB = 3 * C + REL * H
E, GE, TOPK, EGROUPS, KGROUPS = 32, 8, 8, 4, 2
ROUTED_SCALING = 2.5
INNER = 128
UNITS = 4
TURNS = [(0, 2), (2, 3), (3, 4), (4, 5)]
LOWEST = -3.0e38
BLKP = 4 * CH
TP = B * NCH * CH
NB = TP // BLKP
WU = 3 * KC * INNER
RING = 6


def f32(ap):
    return ap.bitcast(F32)


def split_matmul(nc, out, left, right, first=True, last=True):
    terms = [(l, r) for l, r in zip(left, right)]
    n = 3 * len(terms)
    i = 0
    for (lh, ll), (rh, rl) in terms:
        for a, b in ((lh, rh), (lh, rl), (ll, rh)):
            m = nc.tensor.matmul(out, a, b, start=first and i == 0, stop=last and i == n - 1)
            i += 1
    return m


def token_attention(nc, d, h0, early, early_loaded):
    with ExitStack() as ctx:
        def sb(name, shape, dt=F32):
            return ctx.enter_context(nc.sbuf_tensor("a_" + name, shape, dt))

        def sem(name):
            return ctx.enter_context(nc.semaphore("a_" + name))

        x = sb("x", [128, KC, B, LP])
        w_qk = early[:, 0:KC * 2 * PAIRS * 128].rearrange("p (k i n) -> p k i n", k=KC, i=2)
        w_v = sb("w_v", [128, KC, C])
        w_proj = sb("w_proj", [128, KC, C])
        cols = sb("cols", [128, 64])
        rows = sb("rows", [128, 2, C])
        ident = sb("ident", [128, 128])
        mean_all = sb("mean_all", [128, 128])
        B_QK, CB_QK, MASK, B_P, LN_G, LN_B, GT = 0, 16, 32, 34, 36, 38, 40

        whi = sb("whi", [128, KC, 2, PAIRS * 128], F32R)
        wlo = sb("wlo", [128, KC, 2, PAIRS * 128], F32R)
        vhi = sb("vhi", [128, KC, C], F32R)
        vlo = sb("vlo", [128, KC, C], F32R)
        xhi = sb("xhi", [128, KC, LP], F32R)
        xlo = sb("xlo", [128, KC, LP], F32R)
        q_op = sb("q_op", [128, PAIRS, LP], F32R)
        k_op = sb("k_op", [128, 2, PAIRS, LP], F32R)
        part = sb("part", [128, 6, HALF], F32R)
        vaug = sb("vaug", [CH, NCH, H, 2 * HD])
        mx = sb("mx", [128, 4, NCH, 2])
        mx1 = sb("mx1", [128, 4, NCH])
        negm = sb("negm", [128, 4, NCH])
        mcols = sb("mcols", [128, 2, NCH, 128], F32R)
        ident_r = sb("ident_r", [128, CH // 2 + 1 + HALF], F32R)
        shifted = sb("shifted", [128, 128], F32R)
        probs = sb("probs", [CH, 8, LP])
        osb = sb("osb", [128, LP])
        rsum = sb("rsum", [CH, NCH, 4])
        ctok = sb("ctok", [CH, NCH, C])
        ctxt = sb("ctxt", [128, NCH, KC, CH])
        g = sb("g", [128, 32])

        ring = [ctx.enter_context(nc.psum_tensor(f"a_ring{i}", [128, 512], F32)) for i in range(RING)]
        ps_o = ctx.enter_context(nc.psum_tensor("a_ps_o", [128, 2, 512], F32))

        loaded = sem("loaded")
        w_loaded = [sem("wq_loaded"), sem("wk_loaded")]
        v_loaded = sem("v_loaded")
        x_loaded = sem("x_loaded")
        others_loaded = sem("others_loaded")
        gt_pe = sem("gt_pe")
        gt_dve = sem("gt_dve")
        gt_act = sem("gt_act")
        w_high = sem("w_high")
        w_low = sem("w_low")
        x_high = sem("x_high")
        x_low = sem("x_low")
        filled = [sem(f"filled{i}") for i in range(RING)]
        freed = [sem(f"freed{i}") for i in range(RING)]
        part_ready = sem("part_ready")
        gt_x = sem("gt_x")
        zero_mx = sem("zero_mx")
        max_done = sem("max_done")
        k_zeroed = sem("k_zeroed")
        neg_done = sem("neg_done")
        high_done = sem("high_done")
        mcols_ready = sem("mcols_ready")
        o_full = sem("o_full")
        o_copied = sem("o_copied")
        ctx_ready = sem("ctx_ready")
        recip_done = sem("recip_done")
        zeroed = sem("zeroed")

        def halves(kind, s, n):
            return [(kind, s, i, h) for i in n for h in range(2)]

        PRO = halves("P", 0, range(4)) + halves("M", 0, range(20)) + halves("N", 0, range(2))
        order = []
        for s in range(1, 5):
            if s == 1:
                order += [("V", s, i, 0) for i in range(NCH)]
            order += halves("X", s, range(2)) + halves("P", s, (2, 3))
            for i in range(20):
                order += halves("T", s, (i,)) + halves("M", s, (i,))
            order += halves("P", s, (0, 1)) + halves("S", s, (0,))
            if s == 4:
                order += [("C", s, i, 0) for i in range(len(TURNS))] + [("O", s, i, 0) for i in range(NCH)]
        tail = [t for t in order if not (
            (t[0] == "P" and (t[1] == 4 or (t[1] == 3 and t[2] < 2))) or (t[0] == "M" and t[1] == 4))]
        assert len(order) % RING == 0
        START = len(PRO)
        BODY = len(order) // RING
        at_pro = {t: i for i, t in enumerate(PRO)}
        at_body = {t: START + i for i, t in enumerate(order)}
        at_tail = {t: START + i for i, t in enumerate(tail)}

        class Use:

            def __init__(self, u, b=0):
                self.slot = u % RING
                self.tile = ring[self.slot]
                self.n = u // RING + b * BODY

        def use(kind, s, i, half, b, last):
            return Use((at_tail if last else at_body)[kind, s, i, half], b)

        def pro(kind, i, half):
            return Use(at_pro[kind, 0, i, half])

        def consumed(eng, u):
            eng.wait_ge(freed[u.slot], u.n + 1)

        def fill_wait(pe, u):
            if not (isinstance(u.n, int) and u.n == 0):
                pe.wait_ge(freed[u.slot], u.n)

        def span(half):
            return slice(half * HALF, half * HALF + HALF)

        with nc.Block() as block:
            @block.sync
            def _(sp):
                for dst, src in ((w_proj, d["w_proj"]), (cols, d["cols"]), (ident, d["ident"]),
                                 (mean_all, d["mean_all"]), (rows, d["rows"])):
                    sp.dma_start(dst[:], src).then_inc(loaded, 16)
                for i in range(2):
                    sp.dma_start(w_qk[:, :, i], d["w_qk"][:, :, i]).then_inc(w_loaded[i], 16)
                sp.dma_start(w_v[:], d["w_v"]).then_inc(v_loaded, 16)
                sp.dma_start(x[:, :, 0], d["xt"][:, :, 0]).then_inc(x_loaded, 16)
                sp.dma_start(x[:, :, 1:B], d["xt"][:, :, 1:B]).then_inc(others_loaded, 16)
                sp.wait_ge(w_high, 2)
                sp.wait_ge(w_low, 2)
                sp.dma_start(early[:, 0:EARLY], d["early"]).then_inc(early_loaded, 16)

            LOADED = 5 * 16

            @block.gpsimd
            def _(pool):
                nc.gpsimd.memset(f32(k_op[64:128, 0]), 0.0).then_inc(k_zeroed, 1)
                pool.wait_ge(k_zeroed, 1)
                nc.gpsimd.memset(f32(k_op[0:64, 1]), 0.0).then_inc(k_zeroed, 1)
                pool.wait_ge(k_zeroed, 2)
                nc.gpsimd.memset(f32(mcols[:]), 0.0).then_inc(zeroed, 1)
                nc.gpsimd.memset(vaug[:], 1.0).then_inc(zeroed, 1)

            @block.tensor
            def _(pe):
                gp = ps_o[:, 0, :]
                pe.wait_ge(loaded, LOADED)
                for j in range(KC):
                    for k in range(KC):
                        m = nc.tensor.matmul(gp[:, j:j + 1], w_proj[:, k, 128 * j:128 * j + 128],
                                             cols[:, GT + k:GT + k + 1], start=k == 0, stop=k == KC - 1)
                m.then_inc(gt_pe, 1)
                pe.wait_ge(gt_dve, 1)
                for k in range(KC):
                    m = nc.tensor.matmul(gp[:, 2:3], mean_all[:], g[:, k:k + 1], start=k == 0, stop=k == KC - 1)
                m.then_inc(gt_pe, 1)
                pe.wait_ge(gt_dve, 3)
                for k in range(KC):
                    m = nc.tensor.matmul(gp[:, 3:4], mean_all[:], g[:, 4 + k:5 + k], start=k == 0, stop=k == KC - 1)
                m.then_inc(gt_pe, 1)

                def project(u, pair, qk, half):
                    fill_wait(pe, u)
                    c0 = pair * 128
                    split_matmul(nc, u.tile[:, 0:HALF],
                                 [(whi[:, k, qk, c0:c0 + 128], wlo[:, k, qk, c0:c0 + 128]) for k in range(KC)],
                                 [(xhi[:, k, span(half)], xlo[:, k, span(half)])
                                  for k in range(KC)]).then_inc(filled[u.slot], 1)

                def values(u, c):
                    fill_wait(pe, u)
                    ks = slice(c * CH, c * CH + KSIZE[c])
                    split_matmul(nc, u.tile[0:KSIZE[c], 0:C],
                                 [(xhi[:, k, ks], xlo[:, k, ks]) for k in range(KC)],
                                 [(vhi[:, k, :], vlo[:, k, :]) for k in range(KC)]).then_inc(filled[u.slot], 1)

                def head(grp, j):
                    return j % 2, 2 * grp + j // 2

                def row_scores(u, grp, i, half):
                    fill_wait(pe, u)
                    e, pair = head(grp, i % 4)
                    c = i // 4
                    nc.tensor.matmul(u.tile[0:QSIZE[c], 0:HALF], q_op[:, pair, c * CH:c * CH + QSIZE[c]],
                                     k_op[:, e, pair, span(half)], start=True, stop=True).then_inc(filled[u.slot], 1)

                def turn_max(u, pl, half):
                    fill_wait(pe, u)
                    pieces = []
                    for c in range(NCH):
                        lo, hi = c * CH, c * CH + QSIZE[c]
                        a, z = max(lo, half * HALF), min(hi, half * HALF + HALF)
                        if a < z:
                            odd = (a - half * HALF) % 2
                            pieces.append((c, a - half * HALF - odd, z - half * HALF + (z % 2), a - lo, odd))
                    for i, (c, a, z, first, odd) in enumerate(pieces):
                        z = HALF if i == 0 else z
                        m = nc.tensor.matmul(u.tile[:, a:z], mcols[0:QSIZE[c], pl, c, :],
                                             (shifted if odd else ident_r)[0:QSIZE[c], first:first + z - a],
                                             start=i == 0, stop=i == len(pieces) - 1)
                    m.then_inc(filled[u.slot], 1)

                def key_scores(u, grp, i, half):
                    fill_wait(pe, u)
                    e, pair = head(grp, i % 4)
                    c = i // 4
                    nc.tensor.matmul(u.tile[0:KSIZE[c], 0:HALF], k_op[:, e, pair, c * CH:c * CH + KSIZE[c]],
                                     q_op[:, pair, span(half)], start=True, stop=True).then_inc(filled[u.slot], 1)

                def weigh_values(grp, c, piece, b, s, last):
                    half, quarter = piece // 2, piece % 2
                    a, z = quarter * (HALF // 2 + 1), HALF // 2 + 1 if quarter == 0 else HALF
                    for j in range(4):
                        consumed(pe, use("T", s, 4 * c + j, half, b, last))
                        m = nc.tensor.matmul(ps_o[32 * j:32 * j + 32, half, a:z],
                                             vaug[0:KSIZE[c], c, 4 * grp + j, :],
                                             probs[0:KSIZE[c], (4 * c + j) % 8, half * HALF + a:half * HALF + z],
                                             start=c == 0 and quarter == 0, stop=c == NCH - 1 and quarter == 1)
                    return m

                pe.wait_ge(w_high, 3)
                pe.wait_ge(w_low, 3)
                pe.wait_ge(x_high, 1)
                pe.wait_ge(x_low, 1)
                for i in range(4):
                    for half in range(2):
                        project(pro("P", i, half), i // 2, i % 2, half)
                for i in range(4):
                    for half in range(2):
                        consumed(pe, pro("P", i, half))
                pe.wait_ge(k_zeroed, 2)
                for i in range(20):
                    for half in range(2):
                        row_scores(pro("M", i, half), 0, i, half)
                for i in range(2):
                    for half in range(2):
                        project(pro("N", i, half), 2, i, half)

                def batch(b, last):
                    for s in range(1, 5):
                        grp = s - 1
                        ahead = not (last and s == 4)
                        if s == 1:
                            for i in range(NCH):
                                values(use("V", s, i, 0, b, last), i)
                        pe.wait_ge(mcols_ready, b * 4 + s)
                        for i in range(2):
                            for half in range(2):
                                turn_max(use("X", s, i, half, b, last), i, half)
                        if ahead:
                            for i in (2, 3):
                                for half in range(2):
                                    project(use("P", s, i, half, b, last), 2 * (s % 4) + 1, i % 2, half)
                        for i in range(2):
                            for half in range(2):
                                consumed(pe, use("X", s, i, half, b, last))
                        if s == 1:
                            for i in range(NCH):
                                consumed(pe, use("V", s, i, 0, b, last))
                        for i in range(20):
                            for half in range(2):
                                key_scores(use("T", s, i, half, b, last), grp, i, half)
                            if ahead:
                                for half in range(2):
                                    if i == 0:
                                        for k in (2, 3):
                                            consumed(pe, use("P", s, k, half, b, last))
                                    row_scores(use("M", s, i, half, b, last), s % 4, i, half)
                            if i >= 4:
                                if i == 4:
                                    pe.wait_ge(o_copied, b * 4 + s)
                                weigh_values(grp, i // 4 - 1, i % 4, b, s, last)
                        for piece in range(4):
                            m = weigh_values(grp, NCH - 1, piece, b, s, last)
                        m.then_inc(o_full, 1)
                        if ahead and not (last and s == 3):
                            if s == 3:
                                pe.wait_ge(x_high, b + 2)
                                pe.wait_ge(x_low, b + 2)
                            for i in range(2):
                                for half in range(2):
                                    project(use("P", s, i, half, b, last), 2 * ((s + 1) % 4), i, half)
                        pe.wait_ge(o_copied, b * 4 + s + 1)
                        for half, (c0, c1) in enumerate(((0, 4), (4, NCH))):
                            u = use("S", s, 0, half, b, last)
                            fill_wait(pe, u)
                            for c in range(c0, c1):
                                at = (c - c0) * 128
                                m = nc.tensor.transpose(u.tile[0:CH, at:at + 128], osb[:, c * CH:c * CH + CH], ident[:])
                            m.then_inc(filled[u.slot], 1)
                    pe.wait_ge(ctx_ready, b * 4 + 5)
                    for i, (c0, c1) in enumerate(TURNS):
                        u = use("C", 4, i, 0, b, last)
                        fill_wait(pe, u)
                        for c in range(c0, c1):
                            for k in range(KC):
                                at = ((c - c0) * KC + k) * 128
                                m = nc.tensor.transpose(u.tile[:, at:at + CH], ctok[:, c, k * 128:k * 128 + 128],
                                                        ident[0:CH, 0:CH])
                        m.then_inc(filled[u.slot], 1)
                    for i, (c0, c1) in enumerate(TURNS):
                        consumed(pe, use("C", 4, i, 0, b, last))
                        for c in range(c0, c1):
                            u = use("O", 4, c, 0, b, last)
                            fill_wait(pe, u)
                            for k in range(KC):
                                m = nc.tensor.matmul(u.tile[0:CH, 0:C], ctxt[:, c, k, :], w_proj[:, k, :],
                                                     start=k == 0, stop=k == KC - 1)
                            m.then_inc(filled[u.slot], 1)

                with pe.Fori(0, B - 1) as b:
                    batch(b, False)
                batch(B - 1, True)

            @block.scalar
            def _(act):
                act.sem_inc(o_copied, 1)
                act.wait_ge(gt_dve, 4)
                nc.scalar.activation(g[:, 8:9], g[:, 7:8], ACT.Sqrt).then_inc(gt_act, 1)
                for i in range(2):
                    act.wait_ge(w_loaded[i], 16)
                    nc.scalar.activation(whi[:, :, i], w_qk[:, :, i], ACT.Copy).then_inc(w_high, 1)
                act.wait_ge(v_loaded, 16)
                nc.scalar.activation(vhi[:], w_v[:], ACT.Copy).then_inc(w_high, 1)

                def split_x(b):
                    nc.scalar.activation(xhi[:], x[:, :, bass.ds(b, 1), :].rearrange("p k b n -> p k (b n)"),
                                         ACT.Copy).then_inc(x_high, 1)

                def high_part(u, pair, qk):
                    act.wait_ge(filled[u.slot], u.n + 1)
                    cb = CB_QK + qk * PAIRS + pair
                    nc.scalar.activation(part[:, u.slot, :], u.tile[:, 0:HALF],
                                         ACT.Identity, bias=cols[:, cb:cb + 1],
                                         scale=cols[:, MASK + qk:MASK + qk + 1]).then_inc(part_ready, 1)

                act.wait_ge(gt_dve, 10)
                split_x(0)
                for i in range(4):
                    for half in range(2):
                        high_part(pro("P", i, half), i // 2, i % 2)
                for i in range(2):
                    for half in range(2):
                        high_part(pro("N", i, half), 2, i)

                def batch(b, last):
                    for s in range(1, 5):
                        if not (last and s == 4):
                            for i in (2, 3):
                                for half in range(2):
                                    high_part(use("P", s, i, half, b, last), 2 * (s % 4) + 1, i % 2)
                        if s == 3 and not last:
                            split_x(b + 1)
                        for i in range(20):
                            sz = KSIZE[i // 4]
                            for half in range(2):
                                u = use("T", s, i, half, b, last)
                                act.wait_ge(filled[u.slot], u.n + 1)
                                nc.scalar.activation(probs[0:sz, i % 8, span(half)], u.tile[0:sz, 0:HALF], ACT.Exp,
                                                     scale=SCALE).then_inc(freed[u.slot], 1)
                        act.wait_ge(o_full, b * 4 + s)
                        act.wait_ge(ctx_ready, b * 4 + s)
                        nc.scalar.activation(osb[:].rearrange("p (h n) -> p h n", h=2), ps_o[:, :, 0:HALF],
                                             ACT.Copy).then_inc(o_copied, 1)
                        if not last or s < 3:
                            for i in range(2):
                                for half in range(2):
                                    high_part(use("P", s, i, half, b, last), 2 * ((s + 1) % 4), i)
                    for i, (c0, c1) in enumerate(TURNS):
                        u = use("C", 4, i, 0, b, last)
                        act.wait_ge(filled[u.slot], u.n + 1)
                        nc.scalar.activation(ctxt[:, c0:c1].rearrange("p c k n -> p (c k) n"),
                                             u.tile[:].rearrange("p (c n) -> p c n", n=128)[:, 0:(c1 - c0) * KC, 0:CH],
                                             ACT.Copy).then_inc(freed[u.slot], 1)

                act.wait_ge(gt_dve, 11)
                with act.Fori(0, B - 1) as b:
                    batch(b, False)
                batch(B - 1, True)

            @block.vector
            def _(dve):
                gp = ps_o[:, 0, :]

                def c_(i, n=1):
                    return cols[:, i:i + n]

                dve.sem_inc(ctx_ready, 1)
                dve.wait_ge(gt_pe, 1)
                nc.vector.tensor_tensor(g[:, 0:2], gp[:, 0:2], c_(B_P, 2), ALU.add).then_inc(gt_dve, 1)
                dve.wait_ge(gt_pe, 2)
                dve.wait_ge(gt_dve, 1)
                nc.vector.tensor_scalar(g[:, 2:4], g[:, 0:2], gp[:, 2:3], None, ALU.subtract).then_inc(gt_dve, 1)
                dve.wait_ge(gt_dve, 2)
                nc.vector.tensor_tensor(g[:, 4:6], g[:, 2:4], g[:, 2:4], ALU.mult).then_inc(gt_dve, 1)
                dve.wait_ge(gt_pe, 3)
                nc.vector.tensor_scalar(g[:, 7:8], gp[:, 3:4], EPS, None, ALU.add).then_inc(gt_dve, 1)
                dve.wait_ge(gt_act, 1)
                nc.vector.reciprocal(g[:, 9:10], g[:, 8:9]).then_inc(gt_dve, 1)
                dve.wait_ge(gt_dve, 5)
                nc.vector.scalar_tensor_tensor(g[:, 10:11], g[:, 9:10], g[:, 9:10], g[:, 7:8], ALU.mult,
                                               ALU.mult).then_inc(gt_dve, 1)
                dve.wait_ge(gt_dve, 6)
                nc.vector.tensor_scalar(g[:, 11:12], g[:, 10:11], -0.5, 1.5, ALU.mult, ALU.add).then_inc(gt_dve, 1)
                dve.wait_ge(gt_dve, 7)
                nc.vector.tensor_scalar(g[:, 12:14], g[:, 2:4], g[:, 9:10], g[:, 11:12], ALU.mult,
                                        ALU.mult).then_inc(gt_dve, 1)
                dve.wait_ge(gt_dve, 8)
                nc.vector.tensor_tensor(g[:, 14:16], g[:, 12:14], c_(LN_G, 2), ALU.mult).then_inc(gt_dve, 1)
                dve.wait_ge(gt_dve, 9)
                nc.vector.tensor_tensor(g[:, 16:18], g[:, 14:16], c_(LN_B, 2), ALU.add).then_inc(gt_x, 1)
                dve.wait_ge(gt_x, 1)
                for i in range(2):
                    dve.wait_ge(w_high, i + 1)
                    nc.vector.tensor_tensor(wlo[:, :, i], w_qk[:, :, i], f32(whi[:, :, i]), ALU.subtract).then_inc(w_low, 1)
                dve.wait_ge(w_high, 3)
                nc.vector.tensor_tensor(vlo[:], w_v[:], f32(vhi[:]), ALU.subtract).then_inc(w_low, 1)

                def general_column(b0, b1):
                    for k in range(KC):
                        m = nc.vector.tensor_scalar(x[:, k, b0:b1, N], ident[:, b0:b1], 0.0, g[:, 16 + k:17 + k],
                                                    ALU.mult, ALU.add)
                    m.then_inc(gt_dve, 1)

                dve.wait_ge(x_loaded, 16)
                general_column(0, 1)

                def split_x(b):
                    dve.wait_ge(x_high, b + 1)
                    nc.vector.tensor_tensor(xlo[:], x[:, :, bass.ds(b, 1), :].rearrange("p k b n -> p k (b n)"),
                                            f32(xhi[:]), ALU.subtract).then_inc(x_low, 1)

                def operand(u, pair, qk, half, n):
                    dve.wait_ge(part_ready, n + 1)
                    cb = B_QK + qk * PAIRS + pair
                    parts = [(q_op[:, pair, span(half)], 0, 128)] if qk == 0 else \
                        [(k_op[64 * e:64 * e + 64, e, pair, span(half)], 64 * e, 64 * e + 64) for e in range(2)]
                    for dst, lo, hi in parts:
                        m = nc.vector.scalar_tensor_tensor(dst, u.tile[lo:hi, 0:HALF], cols[lo:hi, cb:cb + 1],
                                                           f32(part[lo:hi, u.slot, :]), ALU.add, ALU.subtract)
                    m.then_inc(freed[u.slot], 1)

                def maxima(u, i, half):
                    sz = QSIZE[i // 4]
                    dve.wait_ge(filled[u.slot], u.n + 1)
                    nc.vector.tensor_reduce(mx[0:sz, i % 4, i // 4, half:half + 1], u.tile[0:sz, 0:HALF],
                                            AX_X, ALU.max).then_inc(freed[u.slot], 1)
                    if i == 19 and half:
                        consumed(dve, u)

                def negate(n):
                    nc.vector.tensor_tensor(mx1[:], mx[:, :, :, 0], mx[:, :, :, 1], ALU.max).then_inc(max_done, 1)
                    dve.wait_ge(max_done, n + 1)
                    nc.vector.tensor_scalar(negm[:], mx1[:], -1.0, None, ALU.mult).then_inc(neg_done, 1)
                    dve.wait_ge(neg_done, n + 1)
                    cols_of = mcols[:].rearrange("p l c (e r) -> p l e c r", e=2)
                    neg4 = negm[:].rearrange("p (l e) c -> p l e c", l=2)
                    nc.vector.tensor_copy(cols_of[:, :, :, :, 48], neg4).then_inc(high_done, 1)
                    dve.wait_ge(high_done, n + 1)
                    nc.vector.tensor_tensor(cols_of[:, :, :, :, 49], neg4, f32(cols_of[:, :, :, :, 48]),
                                            ALU.subtract).then_inc(mcols_ready, 1)

                nc.vector.memset(mx[:], 0.0).then_inc(zero_mx, 1)
                nc.vector.tensor_copy(ident_r[:, 0:128], ident[:])
                nc.vector.memset(f32(ident_r[:, 128:]), 0.0)
                nc.vector.tensor_copy(shifted[:, 1:128], ident[:, 0:127])
                nc.vector.tensor_scalar(shifted[:, 0:1], ident[:, 0:1], 0.0, None, ALU.mult)
                split_x(0)
                for i in range(4):
                    for half in range(2):
                        operand(pro("P", i, half), i // 2, i % 2, half, 2 * i + half)
                dve.wait_ge(zero_mx, 1)
                for i in range(20):
                    for half in range(2):
                        maxima(pro("M", i, half), i, half)
                dve.wait_ge(zeroed, 2)
                negate(0)
                dve.wait_ge(others_loaded, 16)
                general_column(1, B)
                for i in range(2):
                    for half in range(2):
                        operand(pro("N", i, half), 2, i, half, 8 + 2 * i + half)

                def batch(b, last):
                    for s in range(1, 5):
                        ahead = not (last and s == 4)
                        if s == 1:
                            for c in range(NCH):
                                u = use("V", s, c, 0, b, last)
                                dve.wait_ge(filled[u.slot], u.n + 1)
                                nc.vector.tensor_tensor(
                                    vaug[0:KSIZE[c], c, :, 0:HD],
                                    u.tile[0:KSIZE[c], 0:C].rearrange("p (h d) -> p h d", h=H),
                                    rows[0:KSIZE[c], 0, :].rearrange("p (h d) -> p h d", h=H),
                                    ALU.add).then_inc(freed[u.slot], 1)
                        for i in range(2):
                            for half in range(2):
                                u = use("X", s, i, half, b, last)
                                dve.wait_ge(filled[u.slot], u.n + 1)
                                q = q_op[:, 2 * (s - 1) + i, span(half)]
                                nc.vector.tensor_tensor(q, f32(q), u.tile[:, 0:HALF], ALU.add).then_inc(freed[u.slot], 1)
                        if ahead:
                            for i in (2, 3):
                                for half in range(2):
                                    operand(use("P", s, i, half, b, last), 2 * (s % 4) + 1, i % 2, half,
                                            b * 32 + 8 * s + 2 * i + half)
                        if s == 3 and not last:
                            split_x(b + 1)
                        if ahead:
                            for i in range(20):
                                for half in range(2):
                                    maxima(use("M", s, i, half, b, last), i, half)
                            negate(b * 4 + s)
                        if ahead and not (last and s == 3):
                            for i in range(2):
                                for half in range(2):
                                    operand(use("P", s, i, half, b, last), 2 * ((s + 1) % 4), i, half,
                                            b * 32 + 8 * s + 8 + 2 * i + half)
                        for half, (c0, c1) in enumerate(((0, 4), (4, NCH))):
                            u = use("S", s, 0, half, b, last)
                            dve.wait_ge(filled[u.slot], u.n + 1)
                            heads = u.tile[:].rearrange("p (c j x) -> p c j x", c=4, j=4)[0:CH, 0:c1 - c0]
                            nc.vector.reciprocal(rsum[:, c0:c1], heads[:, :, :, HD]).then_inc(recip_done, 1)
                            dve.wait_ge(recip_done, b * 8 + 2 * s + half - 1)
                            nc.vector.tensor_tensor(
                                ctok[:, c0:c1, 64 * (s - 1):64 * s].rearrange("p c (j x) -> p c j x", j=4),
                                heads[:, :, :, 0:HD], rsum[:, c0:c1].unsqueeze(3).to_broadcast([CH, c1 - c0, 4, HD]),
                                ALU.mult).then_inc(freed[u.slot], 1)
                            consumed(dve, u)
                        dve.sem_inc(ctx_ready, 1)
                    for c in range(NCH):
                        u = use("O", 4, c, 0, b, last)
                        dve.wait_ge(filled[u.slot], u.n + 1)
                        nc.vector.tensor_tensor(h0[:, bass.ds(b * NCH + c, 1), :].rearrange("p t f -> p (t f)"),
                                                u.tile[0:CH, 0:C], rows[0:CH, 1, :],
                                                ALU.add).then_inc(freed[u.slot], 1)

                with dve.Fori(0, B - 1) as b:
                    batch(b, False)
                batch(B - 1, True)


EARLY_PARTS = [("w_in", KC * QKVB), ("w_q", KC * C), ("w_pos", KC * C), ("w_out", KC * C), ("w_gate", KC * E),
               ("own", KC * REL * H), ("pos", KC * REL), ("small", 16), ("ident", 128)]
EARLY = sum(n for _, n in EARLY_PARTS)


def early_views(early):
    views, a = [], 0
    for name, n in EARLY_PARTS:
        v = early[:, a:a + n]
        a += n
        views.append(v if name in ("small", "ident") else v.rearrange("p (k n) -> p k n", k=KC))
    return views


def relative_attention(nc, d, h0, early, early_loaded, y, xh, xl, lg, shared_w, shared_loaded):
    with ExitStack() as ctx:
        def sb(name, shape, dt=F32):
            return ctx.enter_context(nc.sbuf_tensor("b_" + name, shape, dt))

        def sem(name):
            return ctx.enter_context(nc.semaphore("b_" + name))

        W2 = REL * H
        w_in, w_q, w_pos, w_out, w_gate, own, pos, small, ident = early_views(early)
        B_POS, B_Q, R_R = 0, 2, 4

        in_rows = sb("in_rows", [2, 2, QKVB])
        out_row = sb("out_row", [128, C])
        pick = sb("pick", [2, 2])
        bias_hl = sb("bias_hl", [2, QKVB], F32R)
        ones2 = sb("ones2", [2, 128], F32R)

        posT = sb("posT", [128, KC, REL])
        pblk = sb("pblk", [128, KC, W2])
        qrr = sb("qrr", [128, KC])
        qrr_all = sb("qrr_all", [128, KC, 128])
        inhi = sb("inhi", [128, KC, QKVB], F32R)
        inlo = sb("inlo", [128, KC, QKVB], F32R)
        ghi = sb("ghi", [128, KC, E], F32R)
        glo = sb("glo", [128, KC, E], F32R)

        stats = sb("stats", [CH, TILES, 6])
        stat = sb("stat", [CH, 6, TILES])
        stats2 = sb("stats2", [CH, B, 6])
        stat2 = sb("stat2", [CH, 6, B])
        MEAN, VAR, RSTD, TMP, TMP2, SHIFT = range(6)
        warm = sb("warm", [CH, 2])
        xn = sb("xn", [CH, B, C])
        hT = sb("hT", [128, KC, BLKP], F32R)
        hTl = sb("hTl", [128, KC, BLKP], F32R)
        xT = sb("xT", [128, KC, BLKP], F32R)
        xTl = sb("xTl", [128, KC, BLKP], F32R)
        qkvb = sb("qkvb", [CH, 2, 3 * C + 3 * H + B * (QKVB - H)])
        prod = sb("prod", [CH, B, B, C])
        sc = sb("sc", [CH, B, B * H])
        m2 = sb("m2", [CH, B, 2 * H])
        m1 = sb("m1", [CH, B, H])
        ctx_t = sb("ctx_t", [CH, B, C])
        cT = sb("cT", [128, 2, KC, CH])
        hs = sb("hs", [CH, B, C])
        xn2 = sb("xn2", [CH, B, C])
        lgT = sb("lgT", [128, BLKP])

        tb = ctx.enter_context(nc.psum_tensor("b_tb", [128, 2, 512], F32))
        pq = [ctx.enter_context(nc.psum_tensor(f"b_pq{i}", [128, 2, 512], F32)) for i in range(2)]
        xb = ctx.enter_context(nc.psum_tensor("b_xb", [128, 2, 512], F32))

        rows_loaded = sem("rows_loaded")
        setup_pe = sem("setup_pe")
        setup = sem("setup")
        setup_act = sem("setup_act")
        rel_ready = sem("rel_ready")
        rel_row = sem("rel_row")
        bias_ready = sem("bias_ready")
        stats_done = sem("stats_done")
        sq = sem("sq")
        chain = sem("chain")
        xn_ready = sem("xn_ready")
        turned = sem("turned")
        hi_ready = sem("hi_ready")
        lo_ready = sem("lo_ready")
        qkv_full = sem("qkv_full")
        qkv_read = sem("qkv_read")
        qk_done = sem("qk_done")
        shifted = sem("shifted")
        expd = sem("expd")
        p_ready = sem("p_ready")
        pv_done = sem("pv_done")
        ctx_ready = sem("ctx_ready")
        h_bias = sem("h_bias")
        c_turned = sem("c_turned")
        c_copied = sem("c_copied")
        out_full = sem("out_full")
        h_done = sem("h_done")
        var2 = sem("var2")
        sq2 = sem("sq2")
        inverted = sem("inverted")
        inverted2 = sem("inverted2")
        x2_ready = sem("x2_ready")
        x2_turned = sem("x2_turned")
        x2hi = sem("x2hi")
        x2lo = sem("x2lo")
        x2_stored = sem("x2_stored")
        h_turned = sem("h_turned")
        y_copied = sem("y_copied")
        lg_zeroed = sem("lg_zeroed")
        lg_full = sem("lg_full")
        lgT_read = sem("lgT_read")
        lg_turned = sem("lg_turned")
        lg_read = sem("lg_read")

        COLS = [(0, 512), (512, QKVB)]
        ROWS = 3 * 16

        def of_chunk(a, c):
            return a.rearrange("p (b c) n -> p b c n", c=NCH)[:, :, bass.ds(c, 1), :].rearrange("p b c n -> p b (c n)")

        def chunks(eng, body):
            with eng.Fori(0, 2) as j:
                with eng.Fori(0, j * -1 + 2) as p:
                    body((j * 2 + p).with_bounds(min_val=0, max_val=NCH - 3), p, True)
            body(3, 1, False)
            body(4, 0, False)

        def buffer(p):
            return qkvb[:, bass.ds(p, 1), :].rearrange("p i n -> p (i n)")

        def weighted_values(engine, p, t):
            return engine.tensor_tensor(
                prod[:, t, :, :].rearrange("p s (h e) -> p s h e", e=HD),
                sc[:, t, :].rearrange("p (s h) -> p s h", h=H).unsqueeze(3).to_broadcast([CH, B, H, HD]),
                tiles_of(p)[:, :, 2 * C:3 * C].rearrange("p s (h e) -> p s h e", e=HD), ALU.mult)

        def tiles_of(p):
            return buffer(p)[:, 0:B * QKVB].rearrange("p (t f) -> p t f", t=B)

        with nc.Block() as block:
            @block.sync
            def _(sp):
                for dst, name in ((in_rows, "in_rows"), (out_row, "out_row"), (pick, "pick")):
                    sp.dma_start(dst[:], d[name]).then_inc(rows_loaded, 16)
                sp.dma_start(shared_w[:], d["w_exp"][0, :, 0:2 * WU]).then_inc(shared_loaded, 16)

            @block.tensor
            def _(pe):
                def turn(k, c):
                    for b in range(B):
                        m = nc.tensor.transpose(tb[:, k, b * CH:(b + 1) * CH], xn[:, b, 128 * k:128 * k + 128],
                                                ident[0:CH, 0:CH])
                    m.then_inc(turned, 1)

                def project(k, b):
                    n = k * B + b
                    pe.wait_ge(qkv_read, n - 1 + 2)
                    for i, (a, z) in enumerate(COLS):
                        out = pq[b % 2][0:CH, i, 0:z - a]
                        cut = slice(b * CH, (b + 1) * CH)
                        split_matmul(nc, out, [(hT[:, k_, cut], hTl[:, k_, cut]) for k_ in range(KC)],
                                     [(inhi[:, k_, a:z], inlo[:, k_, a:z]) for k_ in range(KC)], last=False)
                        m = nc.tensor.matmul(out, ones2[:, 0:CH], bias_hl[:, a:z], start=False, stop=True)
                    m.then_inc(qkv_full, 1)

                def turn_chunk(k):
                    pe.wait_ge(xn_ready, k * B + B)
                    pe.wait_ge(lo_ready, k * KC + 1)
                    for i in range(KC):
                        turn(i, k)

                pe.wait_ge(early_loaded, 16)
                for j in range(KC):
                    for k in range(KC):
                        m = nc.tensor.matmul(xb[:, 0, 8 * j:8 * j + REL], w_pos[:, k, 128 * j:128 * j + 128],
                                             pos[:, k, :], start=k == 0, stop=k == KC - 1)
                m.then_inc(setup_pe, 1)
                pe.wait_ge(rel_ready, 1)
                for j in range(KC):
                    for k in range(KC):
                        nc.tensor.matmul(xb[:, 1, W2 * j:W2 * j + W2], w_q[:, k, 128 * j:128 * j + 128],
                                         pblk[:, k, :], start=k == 0, stop=k == KC - 1)
                for k in range(KC):
                    m = nc.tensor.matmul(xb[:, 1, W2 * 2:W2 * 3], qrr_all[:, k, :], pblk[:, k, :],
                                         start=k == 0, stop=k == KC - 1)
                m.then_inc(setup_pe, 1)
                pe.wait_ge(setup_act, 1)
                pe.wait_ge(rel_ready, 3)
                for k in range(2):
                    turn_chunk(k)
                    pe.wait_ge(lo_ready, k * KC + KC + 1)
                    if k == 0:
                        pe.wait_ge(bias_ready, 9)
                    for b in range(B):
                        project(k, b)

                def chunk(c, p, ahead):
                    def turn_output(b):
                        n = c * B + b
                        pe.wait_ge(ctx_ready, n + 1 + 1)
                        pe.wait_ge(c_copied, n - 1 + 2)
                        pe.wait_ge(lg_read, c + 1)
                        for k in range(KC):
                            m = nc.tensor.transpose(xb[:, b % 2, k * 128:k * 128 + CH],
                                                    ctx_t[:, b, 128 * k:128 * k + 128], ident[0:CH, 0:CH])
                        m.then_inc(c_turned, 1)

                    def project_output(b):
                        n = c * B + b
                        pe.wait_ge(c_copied, n + 1 + 2)
                        pe.wait_ge(qkv_read, min(c + 2, NCH) * B + 2 if isinstance(c, int) else (c + 2) * B + 2)
                        pe.wait_ge(h_done, c * B + 1)
                        for k in range(KC):
                            m = nc.tensor.matmul(pq[b // 2][0:CH, b % 2, 0:C], cT[:, b % 2, k, :], w_out[:, k, :],
                                                 start=k == 0, stop=k == KC - 1)
                        m.then_inc(out_full, 1)

                    turn_output(0)
                    project_output(0)
                    turn_output(1)
                    turn_output(2)
                    if ahead:
                        pe.wait_ge(y_copied, c + 1)
                        turn_chunk(c + 2)
                    project_output(1)
                    project_output(2)
                    turn_output(3)
                    project_output(3)
                    if ahead:
                        pe.wait_ge(lo_ready, (c + 2) * KC + KC + 1)
                        for b in range(2):
                            pe.wait_ge(h_done, c * B + 2 * b + 2 + 1)
                            project(c + 2, b)
                    pe.wait_ge(x2_ready, c * B + B)
                    for k in range(KC):
                        for b in range(B):
                            m = nc.tensor.transpose(xb[:, k, b * CH:(b + 1) * CH], xn2[:, b, 128 * k:128 * k + 128],
                                                    ident[0:CH, 0:CH])
                        m.then_inc(x2_turned, 1)
                    pe.wait_ge(y_copied, c + 1)
                    for k in range(KC):
                        for b in range(B):
                            m = nc.tensor.transpose(tb[:, k, b * CH:(b + 1) * CH], hs[:, b, 128 * k:128 * k + 128],
                                                    ident[0:CH, 0:CH])
                        m.then_inc(h_turned, 1)
                    if ahead:
                        project(c + 2, 2)
                    pe.wait_ge(x2lo, c * KC + KC)
                    split_matmul(nc, xb[0:E, 0, 0:BLKP], [(ghi[:, k, :], glo[:, k, :]) for k in range(KC)],
                                 [(xT[:, k, :], xTl[:, k, :]) for k in range(KC)]).then_inc(lg_full, 1)
                    if ahead:
                        project(c + 2, 3)
                    pe.wait_ge(lgT_read, c + 1)
                    for b in range(B):
                        m = nc.tensor.transpose(xb[0:CH, 1, b * 128:(b + 1) * 128], lgT[:, b * CH:(b + 1) * CH], ident)
                    m.then_inc(lg_turned, 1)

                chunks(pe, chunk)

            @block.gpsimd
            def _(pool):
                P = nc.gpsimd
                pool.wait_ge(rows_loaded, ROWS)
                pool.wait_ge(early_loaded, 16)
                P.tensor_scalar(ones2[:], ident[0:2, :], 0.0, 1.0, ALU.mult, ALU.add)
                P.tensor_tensor(in_rows[:, 0, 0:C], in_rows[:, 0, 0:C], in_rows[:, 1, 0:C], ALU.add).then_inc(bias_ready, 1)
                for i, (a, z) in enumerate(((0, 3 * C), (3 * C, QKVB))):
                    row, parts = in_rows[:, 0, a:z], bias_hl[:, a:z]
                    if i == 1:
                        pool.wait_ge(rel_row, 1)
                    else:
                        pool.wait_ge(bias_ready, 1)
                    P.tensor_copy(parts, row).then_inc(bias_ready, 1)
                    pool.wait_ge(bias_ready, 4 * i + 2)
                    P.tensor_tensor(row, row, f32(parts), ALU.subtract).then_inc(bias_ready, 1)
                    pool.wait_ge(bias_ready, 4 * i + 3)
                    P.tensor_scalar(row, row, pick[:, 1:2], None, ALU.mult)
                    P.tensor_scalar(parts, f32(parts), pick[:, 0:1], None, ALU.mult).then_inc(bias_ready, 1)
                    pool.wait_ge(bias_ready, 4 * i + 4)
                    P.tensor_tensor(parts, f32(parts), row, ALU.add).then_inc(bias_ready, 1)

                def chunk(c, p, ahead):
                    qk = tiles_of(p)
                    pool.wait_ge(qkv_read, c * B + B + 2)
                    pool.wait_ge(ctx_ready, c * B + 1)
                    for t in (1, 2, 3):
                        nc.gpsimd.tensor_tensor(prod[:, t, :, :], qk[:, t, 0:C].unsqueeze(1).to_broadcast([CH, B, C]),
                                                qk[:, :, C:2 * C], ALU.mult).then_inc(qk_done, 1)
                    hb = of_chunk(h0[:], c)
                    nc.gpsimd.tensor_tensor(hb, hb, out_row[0:CH, :].unsqueeze(1).to_broadcast([CH, B, C]),
                                            ALU.add).then_inc(h_bias, 1)
                    pool.wait_ge(p_ready, c + 1)
                    for t in (2, 3):
                        weighted_values(nc.gpsimd, p, t).then_inc(pv_done, 1)
                chunks(pool, chunk)

            @block.scalar
            def _(act):
                act.wait_ge(early_loaded, 16)
                nc.scalar.activation(warm[:, 1:2], ident[0:CH, 0:1], ACT.Sqrt)
                act.wait_ge(stats_done, 1)
                nc.scalar.activation(stat[:, TMP, :], stat[:, VAR, :], ACT.Sqrt).then_inc(sq, 1)
                act.wait_ge(rel_ready, 2)
                nc.scalar.activation(inhi[:], w_in, ACT.Copy)
                nc.scalar.activation(ghi[:], w_gate, ACT.Copy).then_inc(setup_act, 1)

                def high(c):
                    for k in range(KC):
                        act.wait_ge(turned, c * KC + k + 1)
                        nc.scalar.activation(hT[:, k, :], tb[:, k, 0:BLKP], ACT.Copy).then_inc(hi_ready, 1)

                def normalise(k):
                    if not (isinstance(k, int) and k == 0):
                        act.wait_ge(turned, k * KC)
                    for b in range(B):
                        t = b * NCH + k
                        nc.scalar.activation(xn[:, b, :], h0[:, bass.ds(t, 1), :].rearrange("p t f -> p (t f)"),
                                             ACT.Identity, bias=stat[:, SHIFT, bass.ds(t, 1)],
                                             scale=stat[:, RSTD, bass.ds(t, 1)]).then_inc(xn_ready, 1)

                def store_projection(k, p, b):
                    act.wait_ge(qkv_full, k * B + b + 1)
                    nc.scalar.activation(tiles_of(p)[:, b, :], pq[b % 2][0:CH].rearrange("p i n -> p (i n)")[:, 0:QKVB],
                                         ACT.Copy).then_inc(qkv_read, 1)

                act.wait_ge(inverted, 1)
                normalise(0)
                high(0)
                normalise(1)
                nc.scalar.activation(warm[:, 0:1], ident[0:CH, 0:1], ACT.Exp)
                for b in range(B):
                    store_projection(0, 0, b)
                high(1)
                store_projection(1, 1, 0)

                def exponentials(c):
                    act.wait_ge(shifted, c + 1)
                    nc.scalar.activation(sc[:], sc[:], ACT.Exp, scale=SCALE).then_inc(expd, 1)

                exponentials(0)
                for b in range(1, B):
                    store_projection(1, 1, b)

                def chunk(c, p, ahead):
                    for b in range(B):
                        n = c * B + b
                        act.wait_ge(c_turned, n + 1)
                        act.wait_ge(out_full, n - 1 + 2)
                        nc.scalar.activation(cT[:, b % 2, :, :],
                                             xb[:, b % 2, 0:256].rearrange("p (k n) -> p k n", k=KC)[:, :, 0:CH],
                                             ACT.Copy).then_inc(c_copied, 1)
                        if b == 0 and ahead:
                            normalise(c + 2)
                        if b == 2 and ahead:
                            high(c + 2)
                    nc.scalar.activation(warm[:, 1:2], ident[0:CH, 0:1], ACT.Sqrt)
                    act.wait_ge(var2, c + 1)
                    nc.scalar.activation(stat2[:, TMP, :], stat2[:, VAR, :], ACT.Sqrt).then_inc(sq2, 1)
                    nc.scalar.activation(warm[:, 0:1], ident[0:CH, 0:1], ACT.Exp)
                    act.wait_ge(inverted2, c + 1)
                    for b in range(B):
                        nc.scalar.activation(xn2[:, b, :], hs[:, b, :], ACT.Identity, bias=stat2[:, SHIFT, b:b + 1],
                                             scale=stat2[:, RSTD, b:b + 1]).then_inc(x2_ready, 1)
                    if ahead:
                        store_projection(c + 2, p, 0)
                    for k in range(KC):
                        act.wait_ge(x2_turned, c * KC + k + 1)
                        nc.scalar.activation(xT[:, k, :], xb[:, k, 0:BLKP], ACT.Copy).then_inc(x2hi, 1)
                    for k in range(KC):
                        act.wait_ge(x2hi, c * KC + k + 1)
                        nc.scalar.activation(of_chunk(xh[:, k], c), f32(xT[:, k, :]).rearrange("p (b n) -> p b n", b=B),
                                             ACT.Copy)
                    for k in range(KC):
                        act.wait_ge(h_turned, c * KC + k + 1)
                        m = nc.scalar.activation(of_chunk(y[:, k], c),
                                                 tb[:, k, 0:BLKP].rearrange("p (b n) -> p b n", b=B), ACT.Copy)
                    m.then_inc(y_copied, 1)
                    if ahead:
                        store_projection(c + 2, p, 1)
                    if ahead or c < NCH - 1:
                        exponentials(c + 1)
                    act.wait_ge(x2lo, c * KC + KC)
                    for k in range(KC):
                        m = nc.scalar.activation(of_chunk(xl[:, k], c),
                                                 f32(xTl[:, k, :]).rearrange("p (b n) -> p b n", b=B), ACT.Copy)
                    m.then_inc(x2_stored, 1)
                    if ahead:
                        store_projection(c + 2, p, 2)
                    act.wait_ge(lg_zeroed, 1)
                    act.wait_ge(lg_full, c + 1)
                    nc.scalar.activation(lgT[0:E, :], xb[0:E, 0, 0:BLKP], ACT.Copy).then_inc(lgT_read, 1)
                    if ahead:
                        store_projection(c + 2, p, 3)
                    act.wait_ge(lg_turned, c + 1)
                    nc.scalar.activation(of_chunk(lg[:], c), xb[0:CH, 1, :].rearrange("p (b e) -> p b e", b=B)[:, :, 0:E],
                                         ACT.Copy).then_inc(lg_read, 1)

                chunks(act, chunk)
                act.wait_ge(lg_read, NCH + 1)

            @block.vector
            def _(dve):
                V = nc.vector
                done = [0]

                def link(ins):
                    done[0] += 1
                    ins.then_inc(setup, 1)
                    dve.wait_ge(setup, done[0])

                for s_ in (qkv_read, c_copied, out_full):
                    dve.sem_inc(s_, 2)
                for s_ in (lo_ready, ctx_ready, lg_read, h_done, y_copied):
                    dve.sem_inc(s_, 1)

                def variance(do, st, sm):
                    me, ve, mo, vo = (st[:, :, i] for i in (1, 2, 4, 5))
                    V.tensor_tensor(sm[:, TMP2, :], ve, vo, ALU.add)
                    V.tensor_tensor(sm[:, TMP, :], me, mo, ALU.subtract)
                    do(V.tensor_tensor(sm[:, MEAN, :], me, mo, ALU.add))
                    V.tensor_scalar(sm[:, MEAN, :], sm[:, MEAN, :], 0.5, None, ALU.mult)
                    do(V.tensor_tensor(sm[:, TMP, :], sm[:, TMP, :], sm[:, TMP, :], ALU.mult))
                    do(V.tensor_scalar(sm[:, TMP, :], sm[:, TMP, :], 0.25, EPS, ALU.mult, ALU.add))
                    return V.scalar_tensor_tensor(sm[:, VAR, :], sm[:, TMP2, :], 1.0 / C, sm[:, TMP, :], ALU.mult,
                                                  ALU.add)

                def inverse(do, sm):
                    do(V.reciprocal(sm[:, RSTD, :], sm[:, TMP, :]))
                    do(V.tensor_tensor(sm[:, TMP2, :], sm[:, RSTD, :], sm[:, RSTD, :], ALU.mult))
                    do(V.tensor_tensor(sm[:, TMP2, :], sm[:, TMP2, :], sm[:, VAR, :], ALU.mult))
                    do(V.tensor_scalar(sm[:, TMP2, :], sm[:, TMP2, :], -0.5, 1.5, ALU.mult, ALU.add))
                    do(V.tensor_tensor(sm[:, RSTD, :], sm[:, RSTD, :], sm[:, TMP2, :], ALU.mult))
                    return V.scalar_tensor_tensor(sm[:, SHIFT, :], sm[:, MEAN, :], -1.0, sm[:, RSTD, :], ALU.mult, ALU.mult)

                V.memset(lgT[:], 0.0).then_inc(lg_zeroed, 1)
                dve.wait_ge(early_loaded, 16)
                dve.wait_ge(setup_pe, 1)
                for k in range(KC):
                    V.tensor_scalar(posT[:, k, :], xb[:, 0, 8 * k:8 * k + REL], small[:, B_POS + k:B_POS + k + 1],
                                        None, ALU.add)
                link(V.tensor_tensor(qrr[:], small[:, B_Q:B_Q + 2], small[:, R_R:R_R + 2], ALU.add))
                for k in range(KC):
                    V.tensor_tensor(pblk[:, k, :].rearrange("p (r h) -> p r h", h=H),
                                    own[:, k, :].rearrange("p (r h) -> p r h", h=H),
                                    posT[:, k, :].unsqueeze(2).to_broadcast([128, REL, H]), ALU.mult)
                for k in range(KC):
                    m = V.tensor_scalar(qrr_all[:, k, :], ident, 0.0, qrr[:, k:k + 1], ALU.mult, ALU.add)
                m.then_inc(rel_ready, 1)
                for t in range(TILES):
                    m = V.bn_stats(stats[:, t, :], h0[:, t, :])
                link(m)
                variance(link, stats, stat).then_inc(stats_done, 1)
                dve.wait_ge(setup_pe, 2)
                dve.wait_ge(rows_loaded, ROWS)
                for k in range(KC):
                    m = V.tensor_copy(w_in[:, k, 3 * C:QKVB], xb[:, 1, W2 * k:W2 * k + W2])
                m.then_inc(rel_ready, 1)
                V.tensor_copy(in_rows[:, 0, 3 * C:QKVB], xb[0:2, 1, 2 * W2:3 * W2]).then_inc(rel_row, 1)
                dve.wait_ge(sq, 1)
                inverse(link, stat).then_inc(inverted, 1)

                def low(c):
                    for k in range(KC):
                        dve.wait_ge(hi_ready, c * KC + k + 1)
                        V.tensor_tensor(hTl[:, k, :], tb[:, k, 0:BLKP], f32(hT[:, k, :]),
                                        ALU.subtract).then_inc(lo_ready, 1)

                def products(c, p):
                    qk = tiles_of(p)
                    dve.wait_ge(qkv_read, c * B + B + 2)
                    return V.tensor_tensor(prod[:, 0, :, :], qk[:, 0, 0:C].unsqueeze(1).to_broadcast([CH, B, C]),
                                           qk[:, :, C:2 * C], ALU.mult)

                dve.wait_ge(setup_act, 1)
                V.tensor_tensor(inlo[:], w_in, f32(inhi[:]), ALU.subtract)
                V.tensor_tensor(glo[:], w_gate, f32(ghi[:]), ALU.subtract).then_inc(rel_ready, 1)
                low(0)

                def sums(t):
                    return V.tensor_reduce(sc[:, t:t + 2, :].rearrange("p t x -> p (t x)"),
                                           prod[:, t:t + 2].rearrange("p t s (h e) -> p (t s h) e", e=HD), AX_X, ALU.add)

                by_head = sc[:].rearrange("p t (s h) -> p t s h", h=H)
                over_s = m1[:].unsqueeze(2).to_broadcast([CH, B, B, H])

                def scores(c, p, do):
                    skip = QKVB - H
                    first = 3 * C + 3 * H
                    rel = buffer(p)[:, first:first + B * skip].rearrange("p (t f) -> p t f", f=skip)[:, :, 0:B * H]
                    dve.wait_ge(qk_done, c * 3 + 1)
                    sums(0)
                    dve.wait_ge(qk_done, c * 3 + 3)
                    do(sums(2))
                    do(V.tensor_tensor(sc[:], sc[:], rel, ALU.add))
                    do(V.tensor_tensor(m2[:], sc[:, :, 0:2 * H], sc[:, :, 2 * H:4 * H], ALU.max))
                    do(V.tensor_tensor(m1[:], m2[:, :, 0:H], m2[:, :, H:2 * H], ALU.max))
                    V.tensor_tensor(by_head, by_head, over_s, ALU.subtract).then_inc(shifted, 1)

                link(products(0, 0))
                low(1)
                scores(0, 0, link)

                STEPS = 23

                def chunk(c, p, ahead):
                    more = ahead or c < NCH - 1
                    steps = [0]

                    def step(ins):
                        steps[0] += 1
                        ins.then_inc(chain, 1)
                        dve.wait_ge(chain, c * STEPS + steps[0])

                    dve.wait_ge(expd, c + 1)
                    step(V.tensor_tensor(m2[:], sc[:, :, 0:2 * H], sc[:, :, 2 * H:4 * H], ALU.add))
                    step(V.tensor_tensor(m1[:], m2[:, :, 0:H], m2[:, :, H:2 * H], ALU.add))
                    step(V.reciprocal(m1[:], m1[:]))
                    V.tensor_tensor(by_head, by_head, over_s, ALU.mult).then_inc(p_ready, 1)
                    dve.wait_ge(p_ready, c + 1)
                    for t in range(B):
                        if t < 2:
                            step(weighted_values(V, p, t))
                        else:
                            dve.wait_ge(pv_done, c * 2 + t - 1)
                        step(V.tensor_tensor(prod[:, t, 0:2, :], prod[:, t, 0:2, :], prod[:, t, 2:4, :], ALU.add))
                        V.tensor_tensor(ctx_t[:, t, :], prod[:, t, 0, :], prod[:, t, 1, :], ALU.add).then_inc(ctx_ready, 1)
                    if ahead:
                        low(c + 2)
                    dve.wait_ge(h_bias, c + 1)
                    for b in range(B):
                        t = b * NCH + c
                        dve.wait_ge(out_full, c * B + b + 1 + 2)
                        V.tensor_tensor(hs[:, b, :], pq[b // 2][0:CH, b % 2, 0:C],
                                        h0[:, bass.ds(t, 1), :].rearrange("p t f -> p (t f)"), ALU.add).then_inc(h_done, 1)
                        if b > 0:
                            dve.wait_ge(h_done, c * B + b + 1)
                            V.bn_stats(stats2[:, b - 1, :], hs[:, b - 1, :])
                    dve.wait_ge(h_done, c * B + B + 1)
                    step(V.bn_stats(stats2[:, B - 1, :], hs[:, B - 1, :]))
                    variance(step, stats2, stat2).then_inc(var2, 1)
                    if more:
                        step(products(c + 1, p * -1 + 1))
                    dve.wait_ge(sq2, c + 1)
                    inverse(step, stat2).then_inc(inverted2, 1)
                    if more:
                        scores(c + 1, p * -1 + 1, step)
                    for k in range(KC):
                        dve.wait_ge(x2hi, c * KC + k + 1)
                        V.tensor_tensor(xTl[:, k, :], xb[:, k, 0:BLKP], f32(xT[:, k, :]),
                                        ALU.subtract).then_inc(x2lo, 1)
                    assert steps[0] == STEPS or not more

                chunks(dve, chunk)


def experts(nc, d, h0, early, lg, shared_w, shared_loaded, y, xh, xl, out):
    with ExitStack() as ctx:
        def sb(name, shape, dt=F32):
            return ctx.enter_context(nc.sbuf_tensor("e_" + name, shape, dt))

        def sem(name):
            return ctx.enter_context(nc.semaphore("e_" + name))

        stage = sb("stage", [128, 2, UNITS * WU])
        wh = sb("wh", [128, 2, UNITS * WU], F32R)
        wl = sb("wl", [128, 2, UNITS * WU], F32R)
        sel_in = early[0:2 * E, :].rearrange("p (e n) -> p e n", e=E)
        sel = sb("sel", [2 * E, E, 128], F32R)
        route = sb("route", [2 * E, TP], F32R)
        gate_row = sb("gate_row", [128, E])
        used = [0]

        def area(*shape):
            n = int(np.prod(shape))
            a = h0[:].rearrange("p t n -> p (t n)")[:, used[0]:used[0] + n]
            used[0] += n
            if len(shape) == 3:
                return a.rearrange("p (t g e) -> p t g e", t=shape[0], g=shape[1])
            return a.rearrange("p (t e) -> p t e", t=shape[0])

        choice, masked, left = (area(TILES, E) for _ in range(3))
        top = area(TILES, TOPK)
        big, small = (area(TILES * EGROUPS, GE // 2) for _ in range(2))
        gs, beat, rank = (area(TILES, EGROUPS) for _ in range(3))
        gsum = area(TILES, 2)
        w64 = area(TILES, 2 * E)
        ident = area(1, CH).rearrange("p t e -> p (t e)")
        whi_r = sb("whi_r", [CH, TILES, E], F32R)
        sg = sb("sg", [128, 2, BLKP])
        su = sb("su", [128, 2, BLKP])
        hv = sb("hv", [128, 2, BLKP])
        hh = sb("hh", [128, 2, BLKP], F32R)
        hl = sb("hl", [128, 2, BLKP], F32R)
        ps = [[ctx.enter_context(nc.psum_tensor(f"e_{n}{i}", [128, 512], F32)) for n in ("g", "u", "w")]
              for i in range(2)]
        ps_y = [ctx.enter_context(nc.psum_tensor(f"e_y{i}", [128, 512], F32)) for i in range(KC)]

        sel_loaded = sem("sel_loaded")
        sel_ready = sem("sel_ready")
        rows_loaded = sem("rows_loaded")
        scored = sem("scored")
        routing = sem("routing")
        routed = sem("routed")
        w_turned = sem("w_turned")
        w_stored = sem("w_stored")
        w_loaded = [sem("w_loaded0"), sem("w_loaded1")]
        w_high = sem("w_high")
        w_low = sem("w_low")
        up_full = sem("up_full")
        silu_done = sem("silu_done")
        mul_done = sem("mul_done")
        h_ready = sem("h_ready")
        high_done = sem("high_done")
        low_done = sem("low_done")
        down_done = sem("down_done")
        y_added = sem("y_added")
        stored = sem("stored")

        groups = [(2, None)] + [(UNITS, e) for e in range(0, E, UNITS)]
        base = [NB * sum(n for n, _ in groups[:i]) for i in range(len(groups) + 1)]
        G = len(groups)

        with nc.Block() as block:
            def yv(nb):
                return y[:].rearrange("p k t n -> p k (t n)")[:, :, bass.ds(nb * BLKP, BLKP)]

            @block.sync
            def _(sp):
                for i, (n, _) in enumerate(groups):
                    if i == 0:
                        continue
                    if i == 1:
                        sp.dma_start(gate_row[:], d["gate_row"]).then_inc(rows_loaded, 16)
                        sp.dma_start(ident, d["ident"][0:CH, 0:CH]).then_inc(rows_loaded, 16)
                        sp.dma_start(sel_in, d["sel"]).then_inc(sel_loaded, 16)
                    if i >= 3:
                        sp.wait_ge(w_high, i - 1)
                        sp.wait_ge(w_low, i - 1)
                    sp.dma_start(stage[:, i % 2, 0:n * WU], d["w_exp"][i, :, 0:n * WU]).then_inc(w_loaded[i % 2], 16)
                with sp.Fori(0, NB) as nb:
                    sp.wait_ge(y_added, (G - 1) * NB + nb + 2)
                    sp.dma_start(out.rearrange("(k p) n -> p k n", k=KC)[:, :, bass.ds(nb * BLKP, BLKP)],
                                 yv(nb)).then_inc(stored, 16)
                sp.wait_ge(stored, NB * 16)

            def xv(x, k, nb):
                return x[:, k].rearrange("p t n -> p (t n)")[:, bass.ds(nb * BLKP, BLKP)]

            def weights(slot, u, kind, k):
                a = u * WU + kind * KC * INNER + k * INNER
                return wh[:, slot, a:a + INNER], wl[:, slot, a:a + INNER]

            @block.gpsimd
            def _(pool):
                def split_weights(i, a, z):
                    pool.wait_ge(w_high, i + 1)
                    s = i % 2
                    return nc.gpsimd.tensor_tensor(wl[:, s, a:z], stage[:, s, a:z], f32(wh[:, s, a:z]), ALU.subtract)

                PART = UNITS * WU // 8
                for n in range(NB * groups[0][0]):
                    if 1 <= n <= 8:
                        m = split_weights(1, (n - 1) * PART, n * PART)
                        if n == 8:
                            m.then_inc(w_low, 1)
                    pool.wait_ge(high_done, n + 1)
                    nc.gpsimd.tensor_tensor(hl[:, n % 2, :], hv[:, n % 2, :], f32(hh[:, n % 2, :]),
                                            ALU.subtract).then_inc(low_done, 1)
                for i in range(2, G):
                    split_weights(i, 0, UNITS * WU).then_inc(w_low, 1)

            @block.tensor
            def _(pe):
                def up(i, u, nb, n):
                    _, e0 = groups[i]
                    slot = u % 2
                    pe.wait_ge(h_ready, n - 1 + 2)
                    xs = [(xv(xh, k, nb), xv(xl, k, nb)) for k in range(KC)]
                    for kind in range(2):
                        m = split_matmul(nc, ps[slot][kind][:, 0:BLKP],
                                         [weights(i % 2, u, kind, k) for k in range(KC)], xs)
                    if e0 is not None:
                        m = nc.tensor.matmul(ps[slot][2][:, 0:BLKP], sel[:, e0 + u, :],
                                             route[:, bass.ds(nb * BLKP, BLKP)], start=True, stop=True)
                    m.then_inc(up_full, 1)

                def down(i, u, nb, n):
                    slot = u % 2
                    if u == 0:
                        pe.wait_ge(y_added, i * NB + nb + 1)
                    pe.wait_ge(low_done, n + 2)
                    last = u == groups[i][0] - 1
                    for k in range(KC):
                        m = split_matmul(nc, ps_y[k][:, 0:BLKP], [weights(i % 2, u, 2, k)],
                                         [(hh[:, slot, :], hl[:, slot, :])], first=u == 0, last=last)
                    m.then_inc(down_done, 1)

                def turn_route():
                    pe.wait_ge(sel_ready, 1)
                    pe.wait_ge(rows_loaded, 32)
                    pe.wait_ge(routed, 1)
                    for t in range(TILES):
                        if t % 4 == 0 and t >= 8:
                            pe.wait_ge(w_stored, t // 4 - 1)
                        m = nc.tensor.transpose(ps[t // 4 % 2][2][0:2 * E, t % 4 * CH:t % 4 * CH + CH], w64[:, t, :],
                                                ident)
                        if t % 4 == 3:
                            m.then_inc(w_turned, 1)
                    pe.wait_ge(w_stored, TILES // 4)

                pe.sem_inc(down_done, 2)
                pe.wait_ge(w_low, 1)
                for u in range(2):
                    up(0, u, 0, u)
                for i, (U, _) in enumerate(groups):
                    def block_of(nb, nxt):
                        for u in range(U):
                            n = nb * U + base[i] + u
                            if u + 2 < U:
                                up(i, u + 2, nb, n + 2)
                            elif nxt is None:
                                up(i, u + 2 - U, nb + 1, n + 2)
                            elif nxt < G:
                                if u == U - 2:
                                    pe.wait_ge(w_low, nxt + 1)
                                    if nxt == 1:
                                        turn_route()
                                up(nxt, u + 2 - U, 0, n + 2)
                            down(i, u, nb, n)
                    with pe.Fori(0, NB - 1) as nb:
                        block_of(nb, None)
                    block_of(NB - 1, i + 1)

            @block.scalar
            def _(act):
                def store_route():
                    for k in range(TILES // 4):
                        act.wait_ge(w_turned, k + 1)
                        nc.scalar.activation(route[:, k * BLKP:(k + 1) * BLKP], ps[k % 2][2][0:2 * E, 0:BLKP],
                                             ACT.Copy).then_inc(w_stored, 1)


                def split_weights(i):
                    n = groups[i][0]
                    if i == 0:
                        act.wait_ge(shared_loaded, 16)
                        nc.scalar.activation(wh[:, 0, 0:n * WU], shared_w[:], ACT.Copy).then_inc(w_high, 1)
                        return
                    act.wait_ge(w_loaded[i % 2], 16 * ((i + 1) // 2))
                    if i >= 2:
                        act.wait_ge(down_done, base[i - 1] + 2)
                    nc.scalar.activation(wh[:, i % 2, 0:n * WU], stage[:, i % 2, 0:n * WU], ACT.Copy).then_inc(w_high, 1)

                def silu(slot, n):
                    act.wait_ge(up_full, n + 1)
                    nc.scalar.activation(sg[:, slot, :], ps[slot][0][:, 0:BLKP], ACT.Silu).then_inc(silu_done, 1)

                split_weights(0)
                nc.scalar.activation(lg[:], lg[:], ACT.Sigmoid).then_inc(scored, 1)
                silu(0, 0)
                for i, (U, _) in enumerate(groups):
                    def block_of(nb, final, before_last=None):
                        for u in range(U):
                            n = nb * U + base[i] + u
                            if before_last and u == U - 1:
                                before_last()
                            if not (final and u == U - 1):
                                silu((u + 1) % 2, n + 1)
                            act.wait_ge(h_ready, n + 1 + 2)
                            act.wait_ge(down_done, n - 1 + 2)
                            nc.scalar.activation(hh[:, u % 2, :], hv[:, u % 2, :], ACT.Copy).then_inc(high_done, 1)
                    block_of(0, False)
                    if i == 0:
                        split_weights(1)
                        block_of(1, False)
                        act.wait_ge(sel_loaded, 16)
                        nc.scalar.activation(sel[:], sel_in, ACT.Copy).then_inc(sel_ready, 1)
                        with act.Fori(2, NB - 1) as nb:
                            block_of(nb, False)
                        block_of(NB - 1, False, store_route)
                        continue
                    if i >= 1 and i + 1 < G:
                        split_weights(i + 1)
                    with act.Fori(1, NB - 1) as nb:
                        block_of(nb, False)
                    block_of(NB - 1, i == G - 1)

            @block.vector
            def _(dve):
                V = nc.vector
                dve.sem_inc(h_ready, 2)
                dve.sem_inc(low_done, 1)
                dve.sem_inc(y_added, 1)

                def multiply(shared, slot, n, first=False):
                    dve.wait_ge(silu_done, n + 1)
                    if not first:
                        dve.wait_ge(low_done, n)
                    if shared:
                        V.tensor_tensor(hv[:, slot, :], sg[:, slot, :], ps[slot][1][:, 0:BLKP],
                                        ALU.mult).then_inc(h_ready, 1)
                        return
                    V.tensor_tensor(su[:, slot, :], sg[:, slot, :], ps[slot][1][:, 0:BLKP],
                                    ALU.mult).then_inc(mul_done, 1)
                    dve.wait_ge(mul_done, n + 1 - base[1])
                    V.tensor_tensor(hv[:, slot, :], su[:, slot, :], ps[slot][2][:, 0:BLKP],
                                    ALU.mult).then_inc(h_ready, 1)

                def add_y(i, nb, count):
                    dve.wait_ge(down_done, count + 2)
                    for k in range(KC):
                        part = y[:, k].rearrange("p t n -> p (t n)")[:, bass.ds(nb * BLKP, BLKP)]
                        m = V.tensor_tensor(part, part, ps_y[k][:, 0:BLKP], ALU.add)
                    m.then_inc(y_added, 1)

                counted = [0]

                def link(ins):
                    counted[0] += 1
                    ins.then_inc(routing, 1)
                    dve.wait_ge(routing, counted[0])

                def group_sums():
                    dve.wait_ge(scored, 1)
                    dve.wait_ge(rows_loaded, 32)
                    link(V.tensor_tensor(choice, lg[:], gate_row[0:CH, :].unsqueeze(1).to_broadcast([CH, TILES, E]),
                                         ALU.add))
                    pairs = choice.rearrange("p t (g e) -> p (t g) e", e=GE)
                    V.tensor_tensor(big, pairs[:, :, 0:4], pairs[:, :, 4:8], ALU.max)
                    link(V.tensor_tensor(small, pairs[:, :, 0:4], pairs[:, :, 4:8], ALU.min))
                    for half in (2, 1):
                        b0, b1 = big[:, :, 0:half], big[:, :, half:2 * half]
                        s0, s1 = small[:, :, 0:half], small[:, :, half:2 * half]
                        link(V.tensor_tensor(s0, s0, s1, ALU.max))
                        link(V.tensor_tensor(s1, b0, b1, ALU.min))
                        V.tensor_tensor(b0, b0, b1, ALU.max)
                        link(V.tensor_tensor(s0, s0, s1, ALU.max))
                    link(V.tensor_tensor(gs.rearrange("p t g -> p (t g)").unsqueeze(2), big[:, :, 0:1], small[:, :, 0:1],
                                         ALU.add))

                def group_ranks():
                    link(V.memset(rank, 0.0))
                    for i in range(1, EGROUPS):
                        link(V.tensor_tensor(beat[:, :, 0:EGROUPS - i], gs[:, :, 0:EGROUPS - i], gs[:, :, i:EGROUPS],
                                             ALU.is_ge))
                        link(V.tensor_tensor(rank[:, :, i:EGROUPS], rank[:, :, i:EGROUPS], beat[:, :, 0:EGROUPS - i],
                                             ALU.add))
                        link(V.tensor_scalar(beat[:, :, 0:EGROUPS - i], beat[:, :, 0:EGROUPS - i], -1.0, 1.0,
                                             ALU.mult, ALU.add))
                        link(V.tensor_tensor(rank[:, :, 0:EGROUPS - i], rank[:, :, 0:EGROUPS - i],
                                             beat[:, :, 0:EGROUPS - i], ALU.add))

                def mask_groups():
                    link(V.tensor_scalar(beat, rank, KGROUPS - 0.5, None, ALU.is_lt))
                    link(V.tensor_tensor(masked.rearrange("p t (g e) -> p (t g) e", e=GE),
                                         choice.rearrange("p t (g e) -> p (t g) e", e=GE),
                                         beat.rearrange("p t g -> p (t g)").unsqueeze(2).to_broadcast(
                                             [CH, TILES * EGROUPS, GE]), ALU.mult))

                def largest():
                    for t in range(TILES):
                        m = V.max(top[:, t, :], masked[:, t, :])
                    link(m)

                def replace():
                    for t in range(TILES):
                        m = V.match_replace(left[:, t, :], top[:, t, :], masked[:, t, :], LOWEST)
                    link(m)

                def chosen_sums():
                    link(V.tensor_tensor(left, left, masked, ALU.not_equal))
                    link(V.tensor_tensor(left, left, lg[:], ALU.mult))
                    link(V.tensor_reduce(gsum[:, :, 0:1], left, AX_X, ALU.add))

                def weigh():
                    link(V.tensor_scalar(gsum[:, :, 0:1], gsum[:, :, 0:1], 1e-20, None, ALU.add))
                    link(V.reciprocal(gsum[:, :, 1:2], gsum[:, :, 0:1]))
                    link(V.tensor_tensor(left, left, gsum[:, :, 1:2].to_broadcast([CH, TILES, E]), ALU.mult))
                    link(V.tensor_scalar(left, left, ROUTED_SCALING, None, ALU.mult))

                def split_route():
                    link(V.tensor_copy(whi_r[:], left))
                    V.tensor_copy(w64[:, :, 0:E], f32(whi_r[:]))
                    V.tensor_tensor(w64[:, :, E:2 * E], left, f32(whi_r[:]), ALU.subtract).then_inc(routed, 1)

                router = {1: group_ranks, 2: mask_groups, 3: largest, 4: replace, 5: chosen_sums, 6: weigh, 7: split_route}

                dve.wait_ge(w_high, 1)
                n0 = groups[0][0] * WU
                V.tensor_tensor(wl[:, 0, 0:n0], shared_w[:], f32(wh[:, 0, 0:n0]), ALU.subtract).then_inc(w_low, 1)
                group_sums()
                multiply(True, 0, 0, first=True)
                for i, (U, e0) in enumerate(groups):
                    def block_of(nb, end):
                        for u in range(U):
                            n = nb * U + base[i] + u
                            if u < U - 1 or not end:
                                multiply(e0 is None, (u + 1) % 2, n + 1)
                            elif i + 1 < G:
                                multiply(False, (u + 1) % 2, n + 1)
                            if i == 0:
                                if n in router:
                                    router[n]()
                                continue
                            dve.wait_ge(high_done, n + 1)
                            V.tensor_tensor(hl[:, u % 2, :], hv[:, u % 2, :], f32(hh[:, u % 2, :]),
                                            ALU.subtract).then_inc(low_done, 1)
                        add_y(i, nb, nb * U + base[i] + U)
                    if i == 0:
                        for nb in range(NB - 1):
                            block_of(nb, False)
                    else:
                        with dve.Fori(0, NB - 1) as nb:
                            block_of(nb, False)
                    block_of(NB - 1, True)


def build(nc, d, out):
    with ExitStack() as ctx:
        def sb(name, shape, dt=F32):
            return ctx.enter_context(nc.sbuf_tensor(name, shape, dt))
        h0 = sb("h0", [CH, TILES, C])
        early = sb("early", [128, 4096])
        early_loaded = ctx.enter_context(nc.semaphore("early_loaded"))
        shared_loaded = ctx.enter_context(nc.semaphore("shared_loaded"))
        token_attention(nc, d, h0, early, early_loaded)
        lg = sb("lg", [CH, TILES, E])
        shared_w = sb("shared_w", [128, 2 * WU])
        y = sb("y", [128, KC, TILES, CH])
        xh = sb("xh", [128, KC, TILES, CH], F32R)
        xl = sb("xl", [128, KC, TILES, CH], F32R)
        relative_attention(nc, d, h0, early, early_loaded, y, xh, xl, lg, shared_w, shared_loaded)
        experts(nc, d, h0, early, lg, shared_w, shared_loaded, y, xh, xl, out)


def kernel(**inputs):
    import numpy as _np
    import concourse.bacc as _bacc
    from concourse import mybir as _mybir
    from concourse.bass_utils import run_bass_kernel_spmd as _run

    v = {k: _np.asarray(a) for k, a in inputs.items()}
    f = _np.float32
    dt = v["x"].dtype

    def fold(a):
        return a.reshape(KC, 128, -1).transpose(1, 0, 2)

    def col(a):
        return a.reshape(KC, 128).T

    def row(a):
        return _np.broadcast_to(a, (128, a.shape[0]))

    a = {}
    xt = v["x"].transpose(2, 0, 1)
    xt = _np.concatenate([xt, xt[:, :, 0:LP - N]], axis=2)
    a["xt"] = xt.reshape(KC, 128, B, LP).transpose(1, 0, 2, 3)
    wqkv, bqkv = v["L0_tok_W_qkv"], v["L0_tok_b_qkv"]
    wqk = _np.zeros((C, 2, PAIRS, 2, 4, HD), dt)
    bqk = _np.zeros((2, PAIRS, 2, 4, HD), dt)
    for s in range(3):
        wqk[:, :, :, :, s] = wqkv[:, 0:2 * C].reshape(C, 2, PAIRS, 2, HD)
        bqk[:, :, :, s] = bqkv[0:2 * C].reshape(2, PAIRS, 2, HD)
    low = (2, 1)
    mbqk = _np.zeros_like(bqk)
    mask = _np.zeros((2, 4, HD, 2), dt)
    for i in range(2):
        mbqk[i, :, :, low[i]] = bqk[i, :, :, low[i]]
        mask[:, low[i], :, i] = 1
    bqk[1, :, :, 3] = 1
    a["w_qk"] = fold(wqk.reshape(C, -1)).reshape(128, KC, 2, PAIRS * 128)
    a["w_v"] = fold(wqkv[:, 2 * C:])
    a["w_proj"] = fold(v["L0_tok_W_proj"])
    cols = _np.zeros((128, 64), dt)
    cols[:, 0:16] = bqk.reshape(16, 128).T
    cols[:, 16:32] = mbqk.reshape(16, 128).T
    cols[:, 32:34] = mask.reshape(128, 2)
    cols[:, 34:36] = col(v["L0_tok_b_proj"])
    cols[:, 36:38] = col(v["L0_tok_ln_g"])
    cols[:, 38:40] = col(v["L0_tok_ln_b"])
    cols[:, 40:42] = col(v["L0_tok_general_token"].reshape(C))
    a["cols"] = cols
    a["rows"] = _np.stack([row(bqkv[2 * C:]), row(v["L0_tok_b_proj"])], axis=1)
    a["ident"] = _np.eye(128, dtype=f)
    a["mean_all"] = _np.full((128, 128), 1.0 / C, f)

    w_in = v["L0_attn_in_proj_weight"]
    b_in = v["L0_attn_in_proj_bias"]
    own = _np.zeros((H, HD, REL, H), dt)
    for h in range(H):
        own[h, :, :, h] = 1
    small = _np.zeros((128, 16), dt)
    small[:, 0:2] = col(v["L0_attn_pos_proj_bias"])
    small[:, 2:4] = col(b_in[0:C])
    small[:, 4:6] = col(v["L0_attn_r_r_bias"].reshape(C))
    wide = _np.zeros((C, QKVB), dt)
    wide[:, 0:3 * C] = w_in.T
    parts = {"w_in": fold(wide), "w_q": fold(w_in[0:C]), "w_pos": fold(v["L0_attn_pos_proj_weight"].T),
             "w_out": fold(v["L0_attn_out_proj_weight"].T), "w_gate": fold(v["L0_ffn_gate_w"].T),
             "own": fold(own.reshape(C, REL * H)), "pos": fold(v["L0_attn_pos"][0:REL, 0].T), "small": small,
             "ident": _np.eye(128, dtype=dt)}
    a["early"] = _np.concatenate([parts[name].reshape(128, n) for name, n in EARLY_PARTS], axis=1)
    in_rows = _np.zeros((2, 2, QKVB), dt)
    in_rows[:, 0, 0:3 * C] = b_in
    in_rows[:, 1, 0:C] = v["L0_attn_r_w_bias"].reshape(C)
    a["in_rows"] = in_rows
    a["pick"] = _np.eye(2, dtype=dt)
    a["out_row"] = row(v["L0_attn_out_proj_bias"])
    a["gate_row"] = row(v["L0_ffn_gate_bias"])

    def unit(wg, wu, wd):
        return _np.concatenate([fold(wg.T).reshape(128, -1), fold(wu.T).reshape(128, -1), wd.T], axis=1)

    units = [unit(v["L0_ffn_shared_gate"][i:i + INNER], v["L0_ffn_shared_up"][i:i + INNER],
                  v["L0_ffn_shared_down"][:, i:i + INNER]) for i in (0, INNER)]
    units += [_np.zeros_like(units[0])] * (UNITS - 2)
    units += [unit(v["L0_ffn_expert_gate"][e], v["L0_ffn_expert_up"][e], v["L0_ffn_expert_down"][e])
              for e in range(E)]
    a["w_exp"] = _np.stack(units).reshape(-1, UNITS, 128, WU).transpose(0, 2, 1, 3).reshape(-1, 128, UNITS * WU)
    sel = _np.zeros((2, E, E, 128), f)
    for e in range(E):
        sel[:, e, e] = 1
    a["sel"] = sel.reshape(2 * E, E, 128)

    nc = _bacc.Bacc("TRN2", target_bir_lowering=False, num_devices=1)
    arrays, d = {}, {}
    for name, arr in a.items():
        arr = _np.ascontiguousarray(arr)
        arrays[f"in_{name}"] = arr
        d[name] = nc.dram_tensor(f"in_{name}", arr.shape, _mybir.dt.from_np(arr.dtype), kind="ExternalInput").ap()
    out = nc.dram_tensor("out", (C, TP), F32, kind="ExternalOutput").ap()
    build(nc, d, out)
    r = _run(nc, [arrays], core_ids=[0])
    res = r.results[0]["out"].reshape(C, B, NCH * CH)[:, :, 0:L]
    return _np.ascontiguousarray(res.transpose(1, 2, 0))
```
